# Optimizing a Trainium2 kernel written in Bass

```python
import numpy as np
import jax
import jax.numpy as jnp

def _softmax(x, axis=-1):
    return jax.nn.softmax(x, axis=axis)

def _gelu(x):
    return jax.nn.gelu(x, approximate=True)

def _silu(x):
    return jax.nn.silu(x)

def _sigmoid(x):
    return jax.nn.sigmoid(x)

def _layernorm(x, axis=-1, eps=1e-05):
    m = jnp.mean(x, axis=axis, keepdims=True)
    v = jnp.var(x, axis=axis, keepdims=True)
    return (x - m) / jnp.sqrt(v + eps)

def _scatter_add(tgt, idx, src, axis=0):
    return tgt.at[idx].add(src)

def _segment_sum(src, seg, n):
    return jax.ops.segment_sum(src, seg, n)
kernel_name = 'mk_flamingo_gated_d2_seqx_r4_04738e'

def setup_inputs(seed: int=0):
    np.random.seed(seed)
    _w = jnp.asarray

    def _rec_inputs():
        import jax
        import jax.numpy as jnp
        _rk = jax.random.key(seed)
        x = 7.22e-05 + 1 * jax.random.normal(jax.random.fold_in(_rk, 1), (4, 512, 256), jnp.float32)
        _lenS = 512 - jax.random.randint(jax.random.fold_in(_rk, 7), (4,), 0, max(1, 512 // 4) + 1, jnp.int32)
        _lenS2 = 512 - jax.random.randint(jax.random.fold_in(_rk, 8), (4,), 0, max(1, 512 // 4) + 1, jnp.int32)
        _ctx_1024P = jax.random.normal(jax.random.fold_in(_rk, 11), (4, 16, 256), jnp.float32)
        _ctx_1024c = jax.random.dirichlet(jax.random.fold_in(_rk, 511), 0.3 * jnp.ones((16,), jnp.float32), (4, 512))
        _ctx_1024t = jnp.einsum('bsk,bkd->bsd', _ctx_1024c, _ctx_1024P)
        _ctx_1024t = _ctx_1024t * jax.lax.rsqrt(jnp.mean(jnp.square(_ctx_1024t)) + 1e-12) * 0.953939
        ctx_1024 = 4.13588e-05 + 0.999923 * (_ctx_1024t + 0.3 * jax.random.normal(jax.random.fold_in(_rk, 611), (4, 512, 256), jnp.float32))
        _g = jax.random.normal(jax.random.fold_in(_rk, 9001), (2, 2), jnp.float32)
        _g = jnp.sign(_g) * jnp.maximum(jnp.abs(_g), 1.0) + (_g == 0) * 1.0
        g_xattn = _g[0]
        g_ffn = _g[1]
        return (x, ctx_1024, g_xattn, g_ffn)
    x, ctx_1024, g_xattn, g_ffn = _rec_inputs()

    def _L0_xattn_setup():
        import jax, jax.numpy as jnp
        import numpy as np
        W = 64
        NUM_HEADS = 16
        HIDDEN = 256

        def _sliding_window_attention(q, k, v, w):
            B, H, S, D = q.shape
            nc = S // w
            kp = jnp.pad(k, ((0, 0), (0, 0), (w, w), (0, 0)))
            vp = jnp.pad(v, ((0, 0), (0, 0), (w, w), (0, 0)))
            kc = kp.reshape(B, H, nc + 2, w, D)
            vc = vp.reshape(B, H, nc + 2, w, D)
            k_win = jnp.concatenate([kc[:, :, 0:nc], kc[:, :, 1:nc + 1], kc[:, :, 2:nc + 2]], axis=3)
            v_win = jnp.concatenate([vc[:, :, 0:nc], vc[:, :, 1:nc + 1], vc[:, :, 2:nc + 2]], axis=3)
            qc = q.reshape(B, H, nc, w, D)
            scores = jnp.einsum('bhcqd,bhckd->bhcqk', qc, k_win)
            qi = jnp.arange(w)[None, :, None]
            ki = jnp.arange(3 * w)[None, None, :]
            ci = jnp.arange(nc)[:, None, None]
            rel = ki - w - qi
            abs_k = ci * w + (ki - w)
            valid = (jnp.abs(rel) <= w) & (abs_k >= 0) & (abs_k < S)
            scores = jnp.where(valid[None, None], scores, jnp.float32(-1000000000.0))
            attn = jax.nn.softmax(scores, axis=-1)
            out = jnp.einsum('bhcqk,bhckd->bhcqd', attn, v_win)
            return out.reshape(B, H, S, D)
        key = jax.random.key(seed)
        kq, kk, kv = jax.random.split(key, 3)
        B, S = (2, 1024)
        return {'query': jax.random.normal(kq, (B, S, HIDDEN), dtype=jnp.float32), 'key': jax.random.normal(kk, (B, S, HIDDEN), dtype=jnp.float32), 'value': jax.random.normal(kv, (B, S, HIDDEN), dtype=jnp.float32)}
    _L0_xattn_all = _L0_xattn_setup()
    _L0_xattn_in = {k: v for k, v in _L0_xattn_all.items() if k in ()}
    del _L0_xattn_all

    def _L0_ffn_setup():
        import jax, jax.numpy as jnp
        import numpy as np
        B, S, D = (4, 256, 256)
        I = 128
        E = 32
        TOP_K = 8
        N_GROUP = 8
        TOPK_GROUP = 4

        def _group_topk(scores):
            T = scores.shape[0]
            epg = E // N_GROUP
            group_scores = scores.reshape(T, N_GROUP, epg).sum(axis=-1)
            _, top_groups = jax.lax.top_k(group_scores, TOPK_GROUP)
            group_mask = jnp.zeros((T, N_GROUP), scores.dtype).at[jnp.arange(T)[:, None], top_groups].set(1.0)
            expert_mask = jnp.repeat(group_mask, epg, axis=1)
            masked_scores = scores * expert_mask
            topk_w, topk_i = jax.lax.top_k(masked_scores, TOP_K)
            return (topk_w, topk_i)

        def _reference_tuple_inner(hidden_states, gate_w, expert_gate, expert_up, expert_down, shared_gate_w, shared_up_w, shared_down_w):
            b, s, d = hidden_states.shape
            flat = hidden_states.reshape(-1, d)
            T = flat.shape[0]
            logits = flat @ gate_w.T
            scores = jax.nn.sigmoid(logits)
            topk_w, topk_i = _group_topk(scores)
            topk_w = topk_w / jnp.clip(topk_w.sum(axis=-1, keepdims=True), 1e-12)
            combine = jnp.zeros((T, E), flat.dtype).at[jnp.arange(T)[:, None], topk_i].add(topk_w)

            def body(acc, expert):
                wg, wu, wd, w = expert
                h = jax.nn.silu(flat @ wg.T) * (flat @ wu.T)
                return (acc + w[:, None] * (h @ wd.T), None)
            out, _ = jax.lax.scan(body, jnp.zeros_like(flat), (expert_gate, expert_up, expert_down, combine.T))
            shared = jax.nn.silu(flat @ shared_gate_w.T) * (flat @ shared_up_w.T) @ shared_down_w.T
            out = out + shared
            return (out.reshape(b, s, d), logits)
        key = jax.random.key(seed)
        ks = jax.random.split(key, 8)
        scale = 0.02
        return {'hidden_states': jax.random.normal(ks[0], (B, S, D), jnp.float32), 'gate_w': jax.random.normal(ks[1], (E, D), jnp.float32) * scale, 'expert_gate': jax.random.normal(ks[2], (E, I, D), jnp.float32) * scale, 'expert_up': jax.random.normal(ks[3], (E, I, D), jnp.float32) * scale, 'expert_down': jax.random.normal(ks[4], (E, D, I), jnp.float32) * scale, 'shared_gate_w': jax.random.normal(ks[5], (I, D), jnp.float32) * scale, 'shared_up_w': jax.random.normal(ks[6], (I, D), jnp.float32) * scale, 'shared_down_w': jax.random.normal(ks[7], (D, I), jnp.float32) * scale}
    _L0_ffn_all = _L0_ffn_setup()
    _L0_ffn_in = {k: v for k, v in _L0_ffn_all.items() if k in ('gate_w', 'expert_gate', 'expert_up', 'expert_down', 'shared_gate_w', 'shared_up_w', 'shared_down_w')}
    del _L0_ffn_all

    def _L1_xattn_setup():
        import jax, jax.numpy as jnp
        import numpy as np
        B, L_ENC, L_DEC, D = (16, 128, 128, 256)
        key = jax.random.key(seed)
        k1, k2, k3, k4, k5, k6 = jax.random.split(key, 6)
        encoder_hc = jax.random.normal(k1, (B, L_ENC, D), dtype=jnp.float32)
        decoder_hq = jax.random.normal(k2, (B, L_DEC, D), dtype=jnp.float32)
        w_sim = jax.random.normal(k3, (3 * D,), dtype=jnp.float32) * 0.02
        b_sim = jax.random.normal(k4, (1,), dtype=jnp.float32) * 0.02
        W_qv = jax.random.normal(k5, (4 * D, D), dtype=jnp.float32) * 0.02
        b_qv = jax.random.normal(k6, (D,), dtype=jnp.float32) * 0.02
        return {'encoder_hc': encoder_hc, 'decoder_hq': decoder_hq, 'w_sim': w_sim, 'b_sim': b_sim, 'W_qv': W_qv, 'b_qv': b_qv}
    _L1_xattn_all = _L1_xattn_setup()
    _L1_xattn_in = {k: v for k, v in _L1_xattn_all.items() if k in ('w_sim', 'b_sim', 'W_qv', 'b_qv')}
    del _L1_xattn_all

    def _L1_ffn_setup():
        import jax, jax.numpy as jnp
        import numpy as np
        DIM = 256
        INTER = 256
        N_EXPERTS = 8
        TOPK = 2
        N_SHARED = 2
        key = jax.random.key(seed)
        ks = jax.random.split(key, 10)
        s = 0.02
        return {'x': jax.random.normal(ks[0], (4, 512, DIM), dtype=jnp.float32), 'gate_w': jax.random.normal(ks[1], (N_EXPERTS, DIM), dtype=jnp.float32) * s, 'gate_bias': jax.random.normal(ks[2], (N_EXPERTS,), dtype=jnp.float32) * s, 'w1': jax.random.normal(ks[3], (N_EXPERTS, INTER, DIM), dtype=jnp.float32) * s, 'w3': jax.random.normal(ks[4], (N_EXPERTS, INTER, DIM), dtype=jnp.float32) * s, 'w2': jax.random.normal(ks[5], (N_EXPERTS, DIM, INTER), dtype=jnp.float32) * s, 'sw1': jax.random.normal(ks[6], (N_SHARED * INTER, DIM), dtype=jnp.float32) * s, 'sw3': jax.random.normal(ks[7], (N_SHARED * INTER, DIM), dtype=jnp.float32) * s, 'sw2': jax.random.normal(ks[8], (DIM, N_SHARED * INTER), dtype=jnp.float32) * s}
    _L1_ffn_all = _L1_ffn_setup()
    _L1_ffn_in = {k: v for k, v in _L1_ffn_all.items() if k in ('gate_w', 'gate_bias', 'w1', 'w3', 'w2', 'sw1', 'sw3', 'sw2')}
    del _L1_ffn_all
    return {'x': x, 'ctx_1024': ctx_1024, 'g_xattn': g_xattn, 'g_ffn': g_ffn, 'L0_ffn_gate_w': _L0_ffn_in['gate_w'], 'L0_ffn_expert_gate': _L0_ffn_in['expert_gate'], 'L0_ffn_expert_up': _L0_ffn_in['expert_up'], 'L0_ffn_expert_down': _L0_ffn_in['expert_down'], 'L0_ffn_shared_gate_w': _L0_ffn_in['shared_gate_w'], 'L0_ffn_shared_up_w': _L0_ffn_in['shared_up_w'], 'L0_ffn_shared_down_w': _L0_ffn_in['shared_down_w'], 'L1_xattn_w_sim': _L1_xattn_in['w_sim'], 'L1_xattn_b_sim': _L1_xattn_in['b_sim'], 'L1_xattn_W_qv': _L1_xattn_in['W_qv'], 'L1_xattn_b_qv': _L1_xattn_in['b_qv'], 'L1_ffn_gate_w': _L1_ffn_in['gate_w'], 'L1_ffn_gate_bias': _L1_ffn_in['gate_bias'], 'L1_ffn_w1': _L1_ffn_in['w1'], 'L1_ffn_w3': _L1_ffn_in['w3'], 'L1_ffn_w2': _L1_ffn_in['w2'], 'L1_ffn_sw1': _L1_ffn_in['sw1'], 'L1_ffn_sw3': _L1_ffn_in['sw3'], 'L1_ffn_sw2': _L1_ffn_in['sw2']}

def reference(x, ctx_1024, g_xattn, g_ffn, L0_ffn_gate_w, L0_ffn_expert_gate, L0_ffn_expert_up, L0_ffn_expert_down, L0_ffn_shared_gate_w, L0_ffn_shared_up_w, L0_ffn_shared_down_w, L1_xattn_w_sim, L1_xattn_b_sim, L1_xattn_W_qv, L1_xattn_b_qv, L1_ffn_gate_w, L1_ffn_gate_bias, L1_ffn_w1, L1_ffn_w3, L1_ffn_w2, L1_ffn_sw1, L1_ffn_sw3, L1_ffn_sw2):
    import jax
    import jax.numpy as jnp

    def _L0_xattn_ref(query, key, value):
        import jax, jax.numpy as jnp
        import numpy as np
        W = 64
        NUM_HEADS = 16
        HIDDEN = 256

        def _sliding_window_attention(q, k, v, w):
            B, H, S, D = q.shape
            nc = S // w
            kp = jnp.pad(k, ((0, 0), (0, 0), (w, w), (0, 0)))
            vp = jnp.pad(v, ((0, 0), (0, 0), (w, w), (0, 0)))
            kc = kp.reshape(B, H, nc + 2, w, D)
            vc = vp.reshape(B, H, nc + 2, w, D)
            k_win = jnp.concatenate([kc[:, :, 0:nc], kc[:, :, 1:nc + 1], kc[:, :, 2:nc + 2]], axis=3)
            v_win = jnp.concatenate([vc[:, :, 0:nc], vc[:, :, 1:nc + 1], vc[:, :, 2:nc + 2]], axis=3)
            qc = q.reshape(B, H, nc, w, D)
            scores = jnp.einsum('bhcqd,bhckd->bhcqk', qc, k_win)
            qi = jnp.arange(w)[None, :, None]
            ki = jnp.arange(3 * w)[None, None, :]
            ci = jnp.arange(nc)[:, None, None]
            rel = ki - w - qi
            abs_k = ci * w + (ki - w)
            valid = (jnp.abs(rel) <= w) & (abs_k >= 0) & (abs_k < S)
            scores = jnp.where(valid[None, None], scores, jnp.float32(-1000000000.0))
            attn = jax.nn.softmax(scores, axis=-1)
            out = jnp.einsum('bhcqk,bhckd->bhcqd', attn, v_win)
            return out.reshape(B, H, S, D)
        B, S, _ = query.shape
        D = HIDDEN // NUM_HEADS

        def split_heads(x):
            return x.reshape(B, S, NUM_HEADS, D).transpose(0, 2, 1, 3)
        q, k, v = map(split_heads, (query, key, value))
        out = _sliding_window_attention(q, k, v, W)
        return out.transpose(0, 2, 1, 3).reshape(B, S, HIDDEN)

    def _L0_ffn_ref(hidden_states, gate_w, expert_gate, expert_up, expert_down, shared_gate_w, shared_up_w, shared_down_w):
        import jax, jax.numpy as jnp
        import numpy as np
        B, S, D = (4, 256, 256)
        I = 128
        E = 32
        TOP_K = 8
        N_GROUP = 8
        TOPK_GROUP = 4

        def _group_topk(scores):
            T = scores.shape[0]
            epg = E // N_GROUP
            group_scores = scores.reshape(T, N_GROUP, epg).sum(axis=-1)
            _, top_groups = jax.lax.top_k(group_scores, TOPK_GROUP)
            group_mask = jnp.zeros((T, N_GROUP), scores.dtype).at[jnp.arange(T)[:, None], top_groups].set(1.0)
            expert_mask = jnp.repeat(group_mask, epg, axis=1)
            masked_scores = scores * expert_mask
            topk_w, topk_i = jax.lax.top_k(masked_scores, TOP_K)
            return (topk_w, topk_i)

        def _reference_tuple_inner(hidden_states, gate_w, expert_gate, expert_up, expert_down, shared_gate_w, shared_up_w, shared_down_w):
            b, s, d = hidden_states.shape
            flat = hidden_states.reshape(-1, d)
            T = flat.shape[0]
            logits = flat @ gate_w.T
            scores = jax.nn.sigmoid(logits)
            topk_w, topk_i = _group_topk(scores)
            topk_w = topk_w / jnp.clip(topk_w.sum(axis=-1, keepdims=True), 1e-12)
            combine = jnp.zeros((T, E), flat.dtype).at[jnp.arange(T)[:, None], topk_i].add(topk_w)

            def body(acc, expert):
                wg, wu, wd, w = expert
                h = jax.nn.silu(flat @ wg.T) * (flat @ wu.T)
                return (acc + w[:, None] * (h @ wd.T), None)
            out, _ = jax.lax.scan(body, jnp.zeros_like(flat), (expert_gate, expert_up, expert_down, combine.T))
            shared = jax.nn.silu(flat @ shared_gate_w.T) * (flat @ shared_up_w.T) @ shared_down_w.T
            out = out + shared
            return (out.reshape(b, s, d), logits)
        return _reference_tuple_inner(hidden_states, gate_w, expert_gate, expert_up, expert_down, shared_gate_w, shared_up_w, shared_down_w)[0]

    def _L1_xattn_ref(encoder_hc, decoder_hq, w_sim, b_sim, W_qv, b_qv):
        import jax, jax.numpy as jnp
        import numpy as np
        B, L_ENC, L_DEC, D = (16, 128, 128, 256)
        d = encoder_hc.shape[-1]
        w1, w2, w3 = (w_sim[:d], w_sim[d:2 * d], w_sim[2 * d:])
        Sim = (encoder_hc @ w1)[:, :, None] + (decoder_hq @ w2)[:, None, :] + jnp.einsum('bid,bjd->bij', encoder_hc * w3, decoder_hq) + b_sim[0]
        A = jax.nn.softmax(Sim, axis=2)
        hq_hat = jnp.einsum('bij,bjd->bid', A, decoder_hq)
        Batt = jax.nn.softmax(jnp.max(Sim, axis=2), axis=1)
        hc_bar = jnp.einsum('bi,bid->bd', Batt, encoder_hc)[:, None, :]
        hc_hat = jnp.broadcast_to(hc_bar, encoder_hc.shape)
        feats = jnp.concatenate([encoder_hc, hq_hat, encoder_hc * hq_hat, encoder_hc * hc_hat], axis=-1)
        hcq = feats @ W_qv + b_qv
        return hcq

    def _L1_ffn_ref(x, gate_w, gate_bias, w1, w3, w2, sw1, sw3, sw2):
        import jax, jax.numpy as jnp
        import numpy as np
        DIM = 256
        INTER = 256
        N_EXPERTS = 8
        TOPK = 2
        N_SHARED = 2
        shape = x.shape
        xt = x.reshape(-1, shape[-1])
        scores = jax.nn.softmax((xt @ gate_w.T).astype(jnp.float32), axis=-1)
        _, idx = jax.lax.top_k(scores + gate_bias, TOPK)
        weights = jnp.take_along_axis(scores, idx, axis=1).astype(x.dtype)
        y = jnp.zeros_like(xt)
        for e in range(N_EXPERTS):
            gate_e = jnp.sum(jnp.where(idx == e, weights, 0.0), axis=1)
            h = jax.nn.silu(xt @ w1[e].T) * (xt @ w3[e].T)
            y = y + gate_e[:, None] * (h @ w2[e].T)
        z = jax.nn.silu(xt @ sw1.T) * (xt @ sw3.T) @ sw2.T
        return (y + z).reshape(shape)
    x = x + jnp.tanh(g_xattn[0]) * _L0_xattn_ref(_layernorm(x, axis=-1), ctx_1024, ctx_1024)
    x = x + jnp.tanh(g_ffn[0]) * _L0_ffn_ref(_layernorm(x, axis=-1), L0_ffn_gate_w, L0_ffn_expert_gate, L0_ffn_expert_up, L0_ffn_expert_down, L0_ffn_shared_gate_w, L0_ffn_shared_up_w, L0_ffn_shared_down_w)
    x = x + jnp.tanh(g_xattn[1]) * _L1_xattn_ref(_layernorm(x, axis=-1), ctx_1024, L1_xattn_w_sim, L1_xattn_b_sim, L1_xattn_W_qv, L1_xattn_b_qv)
    x = x + jnp.tanh(g_ffn[1]) * _L1_ffn_ref(_layernorm(x, axis=-1), L1_ffn_gate_w, L1_ffn_gate_bias, L1_ffn_w1, L1_ffn_w3, L1_ffn_w2, L1_ffn_sw1, L1_ffn_sw3, L1_ffn_sw2)
    return x

_drawn_inputs = setup_inputs


def setup_inputs(seed=0):
    import zlib

    import numpy as np

    out = dict(_drawn_inputs(seed))
    spreads = {'g_ffn': (-1.0, 0.6)}
    factors = {'L0_ffn_gate_w': 8.0,
     'L0_ffn_expert_gate': 8.0,
     'L0_ffn_expert_up': 8.0,
     'L0_ffn_expert_down': 8.0,
     'L0_ffn_shared_gate_w': 8.0,
     'L0_ffn_shared_up_w': 8.0,
     'L0_ffn_shared_down_w': 8.0,
     'L1_xattn_b_qv': 4.514,
     'L1_ffn_gate_w': 8.0,
     'L1_ffn_gate_bias': 8.0,
     'L1_ffn_w1': 8.0,
     'L1_ffn_w3': 8.0,
     'L1_ffn_w2': 8.0,
     'L1_ffn_sw1': 4.557,
     'L1_ffn_sw3': 4.517,
     'L1_ffn_sw2': 4.499}
    for name, (base, spread) in spreads.items():
        noise = np.random.default_rng([zlib.crc32(name.encode()), seed]).standard_normal(out[name].shape)
        drawn = base * np.exp(spread * noise) if base else spread * noise
        out[name] = jnp.asarray(drawn.astype(out[name].dtype))
    for name, factor in factors.items():
        out[name] = (out[name] * factor).astype(out[name].dtype)
    return out
```

```python
from contextlib import ExitStack

import concourse.bass as bass
from concourse import mybir

P = 128
BATCH, SEQ, DIM = 4, 512, 256
TOKENS = BATCH * SEQ
TILES = TOKENS // P
TPB = SEQ // P
CH = DIM // P
HEADS, HD = 16, 16
PAIRS = HEADS // 2
BAND = 64
WIN = P + 2 * BAND
KCOLS = TOKENS + 2 * BAND
KSLICES = 8
KSL = KCOLS // KSLICES
VTILES = TILES + 1
VW = 3 * HD + 1
MASKED = -1e9
EPS = 1e-5
FF = 128
WCOLS = 2 * CH * FF + DIM
E0, TOP0, GROUPS0, TOPG0 = 32, 8, 8, 4
E1, TOP1 = 8, 2
NB0 = E0 + 1
NB1 = 2 * E1 + 4

ALU = mybir.AluOpType
ACT = mybir.ActivationFunctionType
AX_X = mybir.AxisListType.X
F32 = mybir.dt.float32
F32R = mybir.dt.float32r
BF16 = mybir.dt.bfloat16
F16 = mybir.dt.float16
RMAX = bass.bass_isa.ReduceOp.max
RADD = bass.bass_isa.ReduceOp.add


def f32(ap):
    return ap.bitcast(F32)


def late(t, n):
    return not isinstance(t, int) or t >= n


def gated_xattn_moe_kernel(nc, x_in, kt_in, v_in, ctx_in, ctxt_in, consts_in, gates_in, rw0_in, w0_in,
                           wsim_in, w1row_in, bsim_in, wqv_in, bqv_in, rw1_in, rbias1_in, w1_in, out):
    ctx = ExitStack()
    with ctx:
        def sb(name, shape, dt, scope=ctx):
            return scope.enter_context(nc.sbuf_tensor(name, shape, dt))

        def sem(name):
            return ctx.enter_context(nc.semaphore(name))

        bank = [ctx.enter_context(nc.psum_tensor(f"bank{i}", [P, 512], F32)) for i in range(8)]

        x = sb("x", [P, TILES, DIM], F32)
        consts = sb("consts", [P, P + 2 + TPB * WIN], F32)
        ident = consts[:, 0:P]
        head_mask = consts[:, P:P + 2]
        band_f32 = consts[:, P + 2:P + 2 + TPB * WIN]
        gates = sb("gates", [P, 4], F32)
        tg = sb("tg", [P, 4], F32)
        stats = sb("stats", [P, TILES, 6], F32)
        meanvar = sb("meanvar", [P, TILES, 2], F32)
        lnv = sb("lnv", [P, TILES], F32)
        lns = sb("lns", [P, TILES], F32)
        lnr = sb("lnr", [P, TILES], F32)
        lnt = sb("lnt", [P, TILES], F32)
        lnu = sb("lnu", [P, TILES], F32)
        lnw = sb("lnw", [P, TILES], F32)
        rstd = sb("rstd", [P, TILES], F32)

        a0 = ExitStack()
        kst = sb("kst", [P, PAIRS, KCOLS], F32R, a0)
        kraw = sb("kraw", [P, 2, PAIRS, KSL], F32, a0)
        v3 = sb("v3", [P, VTILES, HEADS, VW], BF16, a0)
        vraw = sb("vraw", [P, VTILES, DIM], F32, a0)
        band = sb("band", [P, TILES, WIN], BF16, a0)
        identb = sb("identb", [P, P], BF16, a0)
        qn = sb("qn", [P, 2, PAIRS, 4, 32], F32, a0)
        qst = sb("qst", [P, PAIRS, P], F32R, a0)
        qm = sb("qm", [P, 2, 2, PAIRS, P], F32R, a0)
        nmax = sb("nmax", [P, 4, 2], F32, a0)
        prob = sb("prob", [P, 4, 2, WIN], F32, a0)
        pth = sb("pth", [P, 2, 2, WIN], F16, a0)
        ptl = sb("ptl", [P, 2, 2, WIN], F16, a0)
        rden = sb("rden", [P, 2, PAIRS], F32, a0)
        rdeng = sb("rdeng", [P, 2, PAIRS], F32, a0)
        osum = sb("osum", [P, 2, PAIRS, HD], F32, a0)
        oscaled = sb("oscaled", [P, 2, PAIRS, HD], F32, a0)
        a0.close()

        xn = sb("xn", [P, TILES, DIM], F32)

        rt = ExitStack()
        xh = sb("xh", [P, CH, TOKENS], F32R, rt)
        xl = sb("xl", [P, CH, TOKENS], F32R, rt)
        wraw = sb("wraw", [P, 2, WCOLS], F32, rt)
        wh = sb("wh", [P, 2, WCOLS], F32R, rt)
        wl = sb("wl", [P, 2, WCOLS], F32R, rt)
        sil = sb("sil", [P, 2, 512], F32, rt)
        hid = sb("hid", [P, 2, 512], F32, rt)
        hidh = sb("hidh", [P, 2, 512], F32R, rt)
        hidl = sb("hidl", [P, 2, 512], F32R, rt)
        cw = sb("cw", [P, TILES, NB0], F32, rt)
        rraw = sb("rraw", [P, CH, E0], F32, rt)
        rwhl = sb("rwhl", [P, CH, 2 * E0], F32R, rt)
        rbias = sb("rbias", [P, E1], F32, rt)
        lgl = sb("lgl", [P, TILES, E0], F32, rt)
        lg = sb("lg", [P, TILES, E0], F32, rt)
        sc = sb("sc", [P, TILES, E0], F32, rt)
        msc = sb("msc", [P, TILES, E0], F32, rt)
        rep = sb("rep", [P, TILES, E0], F32, rt)
        selw = sb("selw", [P, TILES, E0], F32, rt)
        gs = sb("gs", [P, TILES, 8], F32, rt)
        rank = sb("rank", [P, TILES, 8], F32, rt)
        cmp = sb("cmp", [P, TILES, 8], F32, rt)
        top8 = sb("top8", [P, TILES, 8], F32, rt)
        rsum = sb("rsum", [P, TILES], F32, rt)
        rrec = sb("rrec", [P, TILES], F32, rt)
        rmx = sb("rmx", [P, TILES], F32, rt)
        rt.close()

        a1 = ExitStack()
        craw = sb("craw", [P, CH, SEQ], F32, a1)
        ch_ = sb("ch_", [P, CH, SEQ], F32R, a1)
        cl_ = sb("cl_", [P, CH, SEQ], F32R, a1)
        traw = sb("traw", [P, TPB, DIM], F32, a1)
        th_ = sb("th_", [P, TPB, DIM], F32R, a1)
        tl_ = sb("tl_", [P, TPB, DIM], F32R, a1)
        enc = sb("enc", [P, CH, SEQ], F32, a1)
        ench = sb("ench", [P, CH, SEQ], F32R, a1)
        encl = sb("encl", [P, CH, SEQ], F32R, a1)
        aenc = sb("aenc", [P, CH, SEQ], F32, a1)
        aench = sb("aench", [P, CH, SEQ], F32R, a1)
        aencl = sb("aencl", [P, CH, SEQ], F32R, a1)
        prob1 = sb("prob1", [P, TPB, SEQ], F32, a1)
        p1th = sb("p1th", [P, TPB, SEQ], F32R, a1)
        p1tl = sb("p1tl", [P, TPB, SEQ], F32R, a1)
        hqh = sb("hqh", [P, CH, SEQ], F32R, a1)
        hql = sb("hql", [P, CH, SEQ], F32R, a1)
        prod = sb("prod", [P, CH, SEQ], F32, a1)
        prodh = sb("prodh", [P, CH, SEQ], F32R, a1)
        prodl = sb("prodl", [P, CH, SEQ], F32R, a1)
        wqv = sb("wqv", [P, 4 * CH, DIM], F32, a1)
        wqh = sb("wqh", [P, 3 * CH, DIM], F32R, a1)
        wql = sb("wql", [P, 3 * CH, DIM], F32R, a1)
        w14 = sb("w14", [P, CH, DIM], F32, a1)
        wsim = sb("wsim", [P, 2, CH], F32, a1)
        w1row = sb("w1row", [P, DIM], F32, a1)
        bqv = sb("bqv", [P, DIM], F32, a1)
        bqvg = sb("bqvg", [P, DIM], F32, a1)
        bsim = sb("bsim", [P, 1], F32, a1)
        junk = sb("junk", [P, DIM], F32, a1)
        rterm = sb("rterm", [P, TPB], F32, a1)
        nm1 = sb("nm1", [P, TPB], F32, a1)
        den1 = sb("den1", [P, TPB], F32, a1)
        rd1 = sb("rd1", [P, TPB], F32, a1)
        msim = sb("msim", [P, TPB], F32, a1)
        mx1 = sb("mx1", [P, 1], F32, a1)
        gmx1 = sb("gmx1", [P, 1], F32, a1)
        ngmx1 = sb("ngmx1", [P, 1], F32, a1)
        eb = sb("eb", [P, TPB], F32, a1)
        ebs = sb("ebs", [P, 1], F32, a1)
        ebt = sb("ebt", [P, 1], F32, a1)
        ebr = sb("ebr", [P, 1], F32, a1)
        batt = sb("batt", [P, TPB], F32, a1)
        hbar = sb("hbar", [P, CH], F32, a1)
        a1.close()

        s_const = sem("const_loaded")
        s_gates = sem("gates_loaded")
        s_x = [sem(f"x_loaded{b}") for b in range(BATCH)]
        s_kraw = [sem(f"kraw_loaded{i}") for i in range(2)]
        s_vraw = sem("vraw_loaded")
        s_tg = sem("tanh_ready")
        s_band = sem("band_ready")
        s_ln = [sem(f"ln_step{i}") for i in range(4)]
        s_lns = [sem(f"ln_sqrt{i}") for i in range(4)]
        s_khi = sem("k_hi")
        s_klo = sem("k_ready")
        s_v = sem("v_step")
        s_qn = sem("qn_ready")
        s_tq = sem("q_transposed")
        s_ahi = sem("q_hi")
        s_alo = sem("q_lo")
        s_qm = sem("q_masked")
        s_s = sem("scores_ready")
        s_nm = sem("max_ready")
        s_p = sem("probs_ready")
        s_pt = sem("probs_transposed")
        s_pth = sem("pt_hi")
        s_ptl = sem("pt_lo")
        s_pv = sem("pv_done")
        s_rr = sem("rden_ready")
        s_o = sem("o_summed")
        s_os = sem("o_scaled")
        s_xa = sem("x_attended")

        class Moe:

            def __init__(self, n):
                def s(name):
                    return sem(f"{name}{n}")
                self.rload = s("router_loaded")
                self.rhi = s("router_hi")
                self.rlo = s("router_lo")
                self.xn = s("xn_ready")
                self.tr = s("xn_transposed")
                self.xh = s("xh_ready")
                self.xl = s("xl_ready")
                self.lg = s("logits_ready")
                self.lgl = s("logits_low_copied")
                self.rs = s("route_step")
                self.ra = s("route_act")
                self.cw = s("cw_ready")
                self.wload = [s(f"w_loaded_{i}_") for i in range(2)]
                self.whi = s("w_hi")
                self.wlo = s("w_lo")
                self.gate = s("gate_ready")
                self.up = s("up_ready")
                self.sil = s("silu_ready")
                self.h = s("h_ready")
                self.hh = s("h_hi")
                self.hl = s("h_lo")
                self.y = s("y_ready")
                self.acc = s("y_added")

        moe = [Moe(0), Moe(1)]
        s_a1 = {n: sem("a1_" + n) for n in (
            "par", "bq", "wq", "wqs", "ctx_t", "ctx", "chi", "clo", "thi", "tlo", "xn", "tr", "enc", "ehi", "elo",
            "a", "ahi", "alo", "r", "sim", "nm", "p", "rd", "pn", "pt", "pth", "ptl", "msim", "mx", "gmx", "ngmx", "eb", "ebt",
            "ebr", "batt", "hb", "hbc", "w14", "whi", "wlo", "hq", "hqh", "hql", "prod", "prh", "prl", "xb", "o", "x")}
        s_out = sem("out_stored")

        block = ctx.enter_context(nc.Block())

        UNITS = TILES * PAIRS

        def q_transpose(pe, t, h, par):
            if h == 0:
                pe.wait_ge(s_qn, t + 1)
            if late(t, 1):
                pe.wait_ge(s_alo, 2 * (t - 1) + h + 1)
            for j in range(4):
                pr = 4 * h + j
                src = qn[:, par, pr].rearrange("p a b -> p (a b)")
                mm = pe.transpose(bank[4 + h][:, j * P:(j + 1) * P], src, ident)
            mm.then_inc(s_tq, 1)

        def attention_tensor(pe):
            pe.wait_ge(s_const, 16)
            pe.wait_ge(s_band, 2)
            q_transpose(pe, 0, 0, 0)
            q_transpose(pe, 0, 1, 0)

            def step(t, k, par, last):
                u = 8 * t + k
                if not last:
                    if k == 0:
                        pe.wait_ge(s_qm, 2 * t + 2)
                        pe.wait_ge(s_klo, 2 if isinstance(t, int) and t < 2 else KSLICES)
                    if late(u, 2):
                        pe.wait_ge(s_p, u - 1)
                    sp = bank[u % 2] if isinstance(u, int) else bank[k % 2]
                    if isinstance(t, int):
                        msk = band[:, t:t + 1, :].broadcast_to([P, 2, WIN])
                    else:
                        msk = band[:, bass.ds(t, 1), :].broadcast_to([P, 2, WIN])
                    pe.matmul(sp[:, :], identb[:, :], msk, start=True, stop=False, skip_group_check=True)
                    for hh in range(2):
                        ks = kst[:, k, 128 * t:128 * t + WIN] if isinstance(t, int) else kst[:, k, bass.ds(128 * t, WIN)]
                        mm = pe.matmul(sp[:, hh * WIN:(hh + 1) * WIN], qm[:, par, hh, k, :], ks,
                                       start=False, stop=True, skip_group_check=True)
                    mm.then_inc(s_s, 1)
                    if (k == 2 or k == 3) and not (isinstance(t, int) and t + 1 >= TILES):
                        q_transpose(pe, t + 1, k - 2, 1 - par)
                if late(u, 2) and not (isinstance(u, int) and u - 2 >= UNITS):
                    pe.wait_ge(s_p, u - 1)
                    if late(u, 4):
                        pe.wait_ge(s_ptl, u - 3)
                    for hh in range(2):
                        for kb in range(2):
                            mm = pe.transpose(bank[2 + k % 2][:, hh * WIN + kb * P:hh * WIN + kb * P + P],
                                              prob[:, (k + 2) % 4, hh, kb * P:(kb + 1) * P], ident)
                    mm.then_inc(s_pt, 1)
                if late(u, 3):
                    kk = (k - 3) % PAIRS
                    tt = t if k >= 3 else t - 1
                    pe.wait_ge(s_ptl, u - 2)
                    if k == 3 or k == 7:
                        if late(tt, 1):
                            pe.wait_ge(s_o, 2 * (2 * (tt - 1) + kk // 4 + 1))
                        pe.wait_ge(s_v, 5 if isinstance(t, int) and t < 2 else 17)
                    for hh in range(2):
                        head = 2 * kk + hh
                        o = bank[6 + kk // 4][:, (head % 8) * VW:(head % 8 + 1) * VW]
                        n = 0
                        for kb in range(2):
                            if isinstance(tt, int):
                                vv = v3[:, tt + kb, head, :]
                            else:
                                vv = v3[:, bass.ds(tt + kb, 1), head, :]
                            for part in (pth, ptl):
                                mm = pe.matmul(o, part[:, (k + 1) % 2, hh, kb * P:(kb + 1) * P], vv,
                                               start=(n == 0), stop=(n == 3))
                                n += 1
                    mm.then_inc(s_pv, 1)

            for t in (0, 1):
                for k in range(PAIRS):
                    step(t, k, t, False)
            with pe.Fori(1, TILES // 2 - 1) as i:
                for par in (0, 1):
                    for k in range(PAIRS):
                        step(2 * i + par, k, par, False)
            for t in (TILES - 2, TILES - 1):
                for k in range(PAIRS):
                    step(t, k, t % 2, False)
            for k in range(3):
                step(TILES, k, 0, True)

        def q_hi(t, h):
            nc.scalar.wait_ge(s_tq, 2 * t + h + 1)
            if late(t, 1):
                nc.scalar.wait_ge(s_qm, 2 * t)
            nc.scalar.activation(qst[:, 4 * h:4 * h + 4, :], bank[4 + h][:, :].rearrange("p (a b) -> p a b", a=4),
                                 ACT.Copy).then_inc(s_ahi, 1)

        def k_hi(s):
            nc.scalar.wait_ge(s_kraw[s % 2], 64 * (s // 2 + 1))
            nc.scalar.activation(kst[:, :, s * KSL:(s + 1) * KSL], kraw[:, s % 2], ACT.Copy).then_inc(s_khi, 1)

        def attention_scalar(act):
            act.wait_ge(s_gates, 16)
            nc.scalar.activation(tg[:, :], gates[:, :], ACT.Tanh).then_inc(s_tg, 1)
            layernorm_sqrt(act, 0, 0)
            k_hi(0)
            k_hi(1)
            q_hi(0, 0)
            q_hi(0, 1)

            def step(t, k, last):
                u = 8 * t + k
                if late(u, 2) and not (isinstance(u, int) and u - 2 >= UNITS):
                    act.wait_ge(s_pt, u - 1)
                    if late(u, 4):
                        act.wait_ge(s_pv, u - 3)
                    nc.scalar.activation(pth[:, k % 2], bank[2 + k % 2][:, :].rearrange("p (a b) -> p a b", a=2),
                                         ACT.Copy).then_inc(s_pth, 1)
                if last:
                    return
                act.wait_ge(s_nm, u + 1)
                if late(u, 4):
                    act.wait_ge(s_pt, u - 3)
                for hh in range(2):
                    e = nc.scalar.activation(prob[:, k % 4, hh, :], bank[k % 2][:, hh * WIN:(hh + 1) * WIN], ACT.Exp,
                                             bias=nmax[:, k % 4, hh:hh + 1])
                e.then_inc(s_p, 1)
                if (k == 3 or k == 4) and not (isinstance(t, int) and t + 1 >= TILES):
                    q_hi(t + 1, k - 3)
                if isinstance(t, int) and t == 0 and 1 <= k <= 6:
                    k_hi(k + 1)

            for t in (0, 1):
                for k in range(PAIRS):
                    step(t, k, False)
            with act.Fori(1, TILES // 2 - 1) as i:
                for par in (0, 1):
                    for k in range(PAIRS):
                        step(2 * i + par, k, False)
            for t in (TILES - 2, TILES - 1):
                for k in range(PAIRS):
                    step(t, k, False)
            for k in range(2):
                step(TILES, k, True)

        def attention_vector(dve):
            nc.vector.wait_ge(s_const, 16)
            nc.vector.tensor_copy(identb[:, :], ident).then_inc(s_band, 1)
            nc.vector.tensor_copy(band[:, :, :].rearrange("p (b t) w -> p b t w", b=BATCH),
                                  band_f32.rearrange("p (t w) -> p t w", t=TPB).unsqueeze(1)
                                  .broadcast_to([P, BATCH, TPB, WIN])).then_inc(s_band, 1)
            for b in range(BATCH):
                dve.wait_ge(s_x[b], 16)
            layernorm_stats(dve, 0, 0, TILES, 0, 0)

            def q_norm(t, par):
                if late(t, 2):
                    dve.wait_ge(s_tq, 2 * (t - 1))
                if isinstance(t, int):
                    xt, mean, rs = x[:, t:t + 1, :], meanvar[:, t, 0:1], rstd[:, t:t + 1]
                else:
                    xt, mean, rs = x[:, bass.ds(t, 1), :], meanvar[:, bass.ds(t, 1), 0], rstd[:, bass.ds(t, 1)]
                xt = xt.rearrange("p t (a b) -> p (t a) b", a=PAIRS).unsqueeze(2).broadcast_to([P, PAIRS, 4, 32])
                nc.vector.tensor_scalar(qn[:, par], xt, mean, rs, ALU.subtract, ALU.mult).then_inc(s_qn, 1)

            def q_lo(t, h):
                dve.wait_ge(s_ahi, 2 * t + h + 1)
                lo = qst[64:128, 4 * h:4 * h + 4, :]
                nc.vector.tensor_tensor(lo, bank[4 + h][64:128, :].rearrange("p (a b) -> p a b", a=4), f32(lo),
                                        ALU.subtract).then_inc(s_alo, 1)

            def k_lo(s):
                dve.wait_ge(s_khi, s + 1)
                for a in (32, 64):
                    lo = kst[a:a + 32, :, s * KSL:(s + 1) * KSL]
                    op = nc.vector.tensor_tensor(lo, kraw[a:a + 32, s % 2], f32(lo), ALU.subtract)
                op.then_inc(s_klo, 1)

            def o_sum(t, h):
                n = 2 * t + h
                dve.wait_ge(s_pv, 8 * t + 4 * h + 4)
                if late(t, 1):
                    dve.wait_ge(s_xa, n - 1)
                ov = bank[6 + h][:, 0:8 * VW].rearrange("p (a b) -> p a b", a=8)
                nc.vector.reciprocal(rden[:, h, :], ov[:, :, 3 * HD]).then_inc(s_rr, 1)
                nc.vector.tensor_reduce(osum[:, h], ov[:, :, 0:3 * HD].rearrange("p a (c d) -> p a d c", c=3),
                                        AX_X, ALU.add).then_inc(s_o, 1)
                dve.wait_ge(s_rr, n + 1)
                nc.vector.tensor_scalar(rdeng[:, h, :], rden[:, h, :], tg[:, 0:1], None, ALU.mult).then_inc(s_o, 1)

            q_norm(0, 0)
            k_lo(0)
            q_lo(0, 0)
            q_lo(0, 1)
            k_lo(1)
            dve.wait_ge(s_tg, 1)

            def step(t, k, par, last):
                u = 8 * t + k
                if not last:
                    dve.wait_ge(s_s, u + 1)
                    nc.vector.tensor_reduce(nmax[:, k % 4, :], bank[k % 2][:, :].rearrange("p (a b) -> p a b", a=2),
                                            AX_X, ALU.max, negate=True).then_inc(s_nm, 1)
                    if not (isinstance(t, int) and t + 1 >= TILES):
                        if k == 0:
                            q_norm(t + 1, 1 - par)
                        if k == 4 or k == 5:
                            q_lo(t + 1, k - 4)
                    if isinstance(t, int) and t == 0 and 1 <= k <= 6:
                        k_lo(k + 1)
                if late(u, 2) and not (isinstance(u, int) and u - 2 >= UNITS):
                    dve.wait_ge(s_pth, u - 1)
                    nc.vector.tensor_tensor(ptl[:, k % 2], bank[2 + k % 2][:, :].rearrange("p (a b) -> p a b", a=2),
                                            pth[:, k % 2], ALU.subtract).then_inc(s_ptl, 1)
                if k == 7 and not last:
                    o_sum(t, 0)
                if k == 3 and late(t, 1):
                    o_sum(t - 1, 1)

            for t in (0, 1):
                for k in range(PAIRS):
                    step(t, k, t, False)
            with dve.Fori(1, TILES // 2 - 1) as i:
                for par in (0, 1):
                    for k in range(PAIRS):
                        step(2 * i + par, k, par, False)
            for t in (TILES - 2, TILES - 1):
                for k in range(PAIRS):
                    step(t, k, t % 2, False)
            for k in range(4):
                step(TILES, k, 0, True)

        def attention_pool(pool):
            nc.gpsimd.memset(v3[:, :, :, 3 * HD:VW], 1.0).then_inc(s_v, 1)
            pool.wait_ge(s_vraw, 16)

            def v_split(g):
                a, b = ((0, 5), (5, 9), (9, 13), (13, 17))[g]
                raw = vraw[:, a:b, :].rearrange("p t (h d) -> p t h d", h=HEADS)
                part = [v3[:, a:b, :, j * HD:(j + 1) * HD] for j in range(3)]
                n = 1 + 4 * g
                nc.gpsimd.tensor_copy(part[0], raw).then_inc(s_v, 1)
                pool.wait_ge(s_v, n + 1)
                nc.gpsimd.tensor_tensor(raw, raw, part[0], ALU.subtract).then_inc(s_v, 1)
                pool.wait_ge(s_v, n + 2)
                nc.gpsimd.tensor_copy(part[1], raw).then_inc(s_v, 1)
                pool.wait_ge(s_v, n + 3)
                nc.gpsimd.tensor_tensor(part[2], raw, part[1], ALU.subtract).then_inc(s_v, 1)

            def q_mask(t, par):
                pool.wait_ge(s_alo, 2 * t + 2)
                if late(t, 2):
                    pool.wait_ge(s_s, 8 * (t - 1))
                for hh in range(2):
                    m = head_mask[:, hh:hh + 1].unsqueeze(2).broadcast_to([P, PAIRS, P])
                    nc.gpsimd.tensor_tensor(qm[:, par, hh], f32(qst[:, :, :]), m, ALU.mult).then_inc(s_qm, 1)

            def x_update(t, h):
                n = 2 * t + h
                pool.wait_ge(s_o, 2 * n + 2)
                nc.gpsimd.tensor_tensor(oscaled[:, h], osum[:, h],
                                        rdeng[:, h, :].unsqueeze(2).broadcast_to([P, PAIRS, HD]),
                                        ALU.mult).then_inc(s_os, 1)
                pool.wait_ge(s_os, n + 1)
                if isinstance(t, int):
                    xt = x[:, t, h * P:(h + 1) * P]
                else:
                    xt = x[:, bass.ds(t, 1), h * P:(h + 1) * P]
                nc.gpsimd.tensor_tensor(xt, xt, oscaled[:, h].rearrange("p a b -> p (a b)"), ALU.add).then_inc(s_xa, 1)

            def tile(t, par):
                if late(t, 1):
                    x_update(t - 1, 1)
                if not (isinstance(t, int) and t + 1 >= TILES):
                    q_mask(t + 1, 1 - par)
                x_update(t, 0)

            v_split(0)
            pool.wait_ge(s_const, 16)
            q_mask(0, 0)
            q_mask(1, 1)
            for g in (1, 2, 3):
                v_split(g)
            x_update(0, 0)
            tile(1, 1)
            with pool.Fori(1, TILES // 2 - 1) as i:
                for par in (0, 1):
                    tile(2 * i + par, par)
            for t in (TILES - 2, TILES - 1):
                tile(t, t % 2)
            x_update(TILES - 1, 1)

        def layernorm_stats(dve, n, t0, t1, base, sbase):
            ts = slice(t0, t1)
            s, q = s_ln[n], s_lns[n]
            for t in range(t0, t1):
                op = nc.vector.bn_stats(stats[:, t, :], x[:, t, :])
            op.then_inc(s, 1)
            dve.wait_ge(s, base + 1)
            for t in range(t0, t1):
                op = nc.vector.bn_aggr(meanvar[:, t, :], stats[:, t, :])
            op.then_inc(s, 1)
            dve.wait_ge(s, base + 2)
            nc.vector.tensor_scalar(lnv[:, ts], meanvar[:, ts, 1], EPS, None, ALU.add).then_inc(s, 1)
            dve.wait_ge(q, sbase + 1)
            nc.vector.reciprocal(lnr[:, ts], lns[:, ts]).then_inc(s, 1)
            dve.wait_ge(s, base + 4)
            nc.vector.tensor_tensor(lnt[:, ts], lnv[:, ts], lnr[:, ts], ALU.mult).then_inc(s, 1)
            dve.wait_ge(s, base + 5)
            nc.vector.tensor_tensor(lnu[:, ts], lnt[:, ts], lns[:, ts], ALU.add).then_inc(s, 1)
            dve.wait_ge(s, base + 6)
            nc.vector.reciprocal(lnw[:, ts], lnu[:, ts]).then_inc(s, 1)
            dve.wait_ge(s, base + 7)
            nc.vector.tensor_scalar(rstd[:, ts], lnw[:, ts], 2.0, None, ALU.mult).then_inc(s, 1)
            dve.wait_ge(s, base + 8)

        def layernorm_sqrt(act, n, base, t0=0, t1=TILES):
            act.wait_ge(s_ln[n], base + 3)
            nc.scalar.activation(lns[:, t0:t1], lnv[:, t0:t1], ACT.Sqrt).then_inc(s_lns[n], 1)

        def moe_prep_tensor(pe, L, m):
            ne = (E0, E1)[L]
            for b in range(BATCH):
                pe.wait_ge(m.xn, b + 1)
                if b >= 2:
                    pe.wait_ge(m.xl, 2 * (b - 1))
                for c in range(CH):
                    for j in range(TPB):
                        mm = pe.transpose(bank[2 * (b % 2) + c][:, j * P:(j + 1) * P],
                                          xn[:, TPB * b + j, c * P:(c + 1) * P], ident)
                    mm.then_inc(m.tr, 1)
            pe.wait_ge(m.rlo, 1)
            for t in range(TILES):
                if t % TPB == 0:
                    pe.wait_ge(m.xl, 2 * (t // TPB + 1))
                lo = bank[4 + t // 8][:, (t % 8) * 2 * ne:(t % 8 + 1) * 2 * ne]
                n = 0
                for c in range(CH):
                    for part in (xh, xl):
                        mm = pe.matmul(lo, part[:, c, t * P:(t + 1) * P], rwhl[:, c, 0:2 * ne],
                                       start=(n == 0), stop=(n == 3))
                        n += 1
            mm.then_inc(m.lg, 1)

        def moe_tensor(pe, L, m, nb):
            pe.wait_ge(m.lgl, 2)

            def gate_up(v, b, par):
                vp = b % 2
                if b == 0:
                    e1 = v // 4 + 1 if isinstance(v, int) else None
                    pe.wait_ge(m.wlo, e1 if e1 is not None else v_e[0] + 1)
                if late(v, 2):
                    pe.wait_ge(m.sil, v - 1)
                for half, ready in ((0, m.gate), (1, m.up)):
                    if half == 1 and late(v, 2):
                        pe.wait_ge(m.h, v - 1)
                    o = bank[2 * half + vp]
                    n = 0
                    for c in range(CH):
                        w = slice((CH * half + c) * FF, (CH * half + c + 1) * FF)
                        for wp, xp in ((wh, xh), (wh, xl), (wl, xh)):
                            mm = pe.matmul(o[:, :], wp[:, par, w], xp[:, c, b * SEQ:(b + 1) * SEQ],
                                           start=(n == 0), stop=(n == 5))
                            n += 1
                    mm.then_inc(ready, 1)

            def down(v, b, par):
                vp = b % 2
                pe.wait_ge(m.hl, v)
                if late(v, 3):
                    pe.wait_ge(m.acc, v - 2)
                for j in range(TPB):
                    o = bank[4 + 2 * vp + j // 2][:, (j % 2) * DIM:(j % 2 + 1) * DIM]
                    n = 0
                    for hp, wp in ((hidh, wh), (hidh, wl), (hidl, wh)):
                        mm = pe.matmul(o, hp[:, vp, j * P:(j + 1) * P], wp[:, par, 2 * CH * FF:WCOLS],
                                       start=(n == 0), stop=(n == 2))
                        n += 1
                mm.then_inc(m.y, 1)

            v_e = [None]

            def body(e, par):
                v_e[0] = e
                for b in range(4):
                    gate_up(4 * e + b, b, par)
                    if late(4 * e + b, 1):
                        down(4 * e + b, (b - 1) % 4, par if b else 1 - par)

            body(0, 0)
            body(1, 1)
            with pe.Fori(1, (nb - 1) // 2) as i:
                body(2 * i, 0)
                body(2 * i + 1, 1)
            for e in range(2 * ((nb - 1) // 2), nb):
                body(e, e % 2)
            down(4 * nb, 3, (nb - 1) % 2)

        def moe_scalar(act, L, m, nb):
            def weights_hi(e, par, loaded):
                act.wait_ge(m.wload[par], loaded)
                if late(e, 2):
                    act.wait_ge(m.y, 4 * (e - 1))
                nc.scalar.activation(wh[:, par], wraw[:, par], ACT.Copy).then_inc(m.whi, 1)

            def step(v, b):
                vp = b % 2
                act.wait_ge(m.gate, v + 1)
                if late(v, 2):
                    act.wait_ge(m.h, v - 1)
                nc.scalar.activation(sil[:, vp], bank[vp][:, :], ACT.Silu).then_inc(m.sil, 1)
                act.wait_ge(m.h, v + 1)
                if late(v, 2):
                    act.wait_ge(m.y, v - 1)
                nc.scalar.activation(hidh[:, vp], hid[:, vp], ACT.Copy).then_inc(m.hh, 1)

            def body(e, par, loaded):
                for b in range(4):
                    step(4 * e + b, b)
                    if b == 2 and not (isinstance(e, int) and (e + 1 >= nb or e == 0)):
                        weights_hi(e + 1, 1 - par, loaded)

            weights_hi(0, 0, 16)
            weights_hi(1, 1, 16)
            body(0, 0, 16)
            body(1, 1, 32)
            with act.Fori(1, (nb - 1) // 2) as i:
                body(2 * i, 0, 16 * i + 16)
                body(2 * i + 1, 1, 16 * i + 32)
            for e in range(2 * ((nb - 1) // 2), nb):
                body(e, e % 2, 16 * ((e + 1) // 2 + 1))

        def moe_vector(dve, L, m, nb):
            def add(v, e, b):
                vp = b % 2
                dve.wait_ge(m.y, v + 1)
                if late(v, 4):
                    dve.wait_ge(m.acc, v - 3)
                for j in range(TPB):
                    t = TPB * b + j
                    w = cw[:, t, e:e + 1] if isinstance(e, int) else cw[:, t, bass.ds(e, 1)]
                    op = nc.vector.scalar_tensor_tensor(
                        out=x[:, t, :], in0=bank[4 + 2 * vp + j // 2][:, (j % 2) * DIM:(j % 2 + 1) * DIM],
                        scalar=w, in1=x[:, t, :], op0=ALU.mult, op1=ALU.add)
                op.then_inc(m.acc, 1)

            def step(v, e, b):
                vp = b % 2
                dve.wait_ge(m.up, v + 1)
                dve.wait_ge(m.sil, v + 1)
                if late(v, 2):
                    dve.wait_ge(m.hl, v - 1)
                nc.vector.tensor_tensor(hid[:, vp], sil[:, vp], bank[2 + vp][:, :], ALU.mult).then_inc(m.h, 1)
                dve.wait_ge(m.hh, v + 1)
                nc.vector.tensor_tensor(hidl[:, vp], hid[:, vp], f32(hidh[:, vp]), ALU.subtract).then_inc(m.hl, 1)
                if late(v, 1):
                    add(v - 1, e if b else e - 1, (b - 1) % 4)

            for e in range(2):
                for b in range(4):
                    step(4 * e + b, e, b)
            with dve.Fori(1, (nb - 1) // 2) as i:
                for e in range(2):
                    for b in range(4):
                        step(8 * i + 4 * e + b, 2 * i + e, b)
            for e in range(2 * ((nb - 1) // 2), nb):
                for b in range(4):
                    step(4 * e + b, e, b)
            add(4 * nb - 1, nb - 1, 3)

        def moe_pool(pool, L, m, nb):
            def low(e, par):
                pool.wait_ge(m.whi, e + 1)
                nc.gpsimd.tensor_tensor(wl[:, par], wraw[:, par], f32(wh[:, par]), ALU.subtract).then_inc(m.wlo, 1)

            with pool.Fori(0, nb // 2) as i:
                for par in range(2):
                    low(2 * i + par, par)
            if nb % 2:
                low(nb - 1, 0)

        def moe_sync(sp, L, m, nb, w_in):
            wv = w_in.rearrange("e p c -> p e c")

            def load(e, par):
                if late(e, 2):
                    sp.wait_ge(m.wlo, e - 1)
                src = wv[:, e, :] if isinstance(e, int) else wv[:, bass.ds(e, 1), :]
                sp.dma_start(wraw[:, par], src).then_inc(m.wload[par], 16)

            load(0, 0)
            load(1, 1)
            with sp.Fori(1, nb // 2) as i:
                load(2 * i, 0)
                load(2 * i + 1, 1)
            if nb % 2:
                load(nb - 1, 0)

        def moe_prep_vector(dve, L, m):
            n = 1 + 2 * L
            ne = (E0, E1)[L]
            layernorm_stats(dve, n, 0, TILES, 0, 0)
            for b in range(BATCH):
                for j in range(TPB):
                    t = TPB * b + j
                    op = nc.vector.tensor_scalar(xn[:, t, :], x[:, t, :], meanvar[:, t, 0:1], rstd[:, t:t + 1],
                                                 ALU.subtract, ALU.mult)
                op.then_inc(m.xn, 1)
            dve.wait_ge(m.rhi, 1)
            nc.vector.tensor_tensor(rwhl[:, :, ne:2 * ne], rraw[:, :, 0:ne], f32(rwhl[:, :, 0:ne]),
                                    ALU.subtract).then_inc(m.rlo, 1)
            for b in range(BATCH):
                for c in range(CH):
                    dve.wait_ge(m.xh, 2 * b + c + 1)
                    cols = slice(b * SEQ, (b + 1) * SEQ)
                    nc.vector.tensor_tensor(xl[:, c, cols], bank[2 * (b % 2) + c][:, :], f32(xh[:, c, cols]),
                                            ALU.subtract).then_inc(m.xl, 1)

        def moe_prep_scalar(act, L, m):
            ne = (E0, E1)[L]
            layernorm_sqrt(act, 1 + 2 * L, 0)
            act.wait_ge(m.rload, 16 + 16 * L)
            nc.scalar.activation(rwhl[:, :, 0:ne], rraw[:, :, 0:ne], ACT.Copy).then_inc(m.rhi, 1)
            for b in range(BATCH):
                for c in range(CH):
                    act.wait_ge(m.tr, 2 * b + c + 1)
                    nc.scalar.activation(xh[:, c, b * SEQ:(b + 1) * SEQ], bank[2 * (b % 2) + c][:, :],
                                         ACT.Copy).then_inc(m.xh, 1)
            act.wait_ge(m.lg, 1)
            for h in range(2):
                lv = bank[4 + h][:, 0:8 * 2 * ne].rearrange("p (t e) -> p t e", t=8)
                op = nc.scalar.activation(lgl[:, 8 * h:8 * h + 8, 0:ne], lv[:, :, ne:2 * ne], ACT.Copy)
                if h == 1:
                    op.then_inc(m.lgl, 1)

        class Chain:

            def __init__(self, eng, s):
                self.eng, self.s, self.n = eng, s, 0

            def __call__(self, op):
                op.then_inc(self.s, 1)
                self.n += 1
                self.eng.wait_ge(self.s, self.n)

        def ranks(link, vals):
            for g in range(8):
                nc.vector.memset(rank[:, :, g:g + 1], float(7 - g)) if g < 7 else link(
                    nc.vector.memset(rank[:, :, g:g + 1], 0.0))
            for k in range(1, 8):
                w = 8 - k
                link(nc.vector.tensor_tensor(cmp[:, :, 0:w], vals[:, :, 0:w], vals[:, :, k:8], ALU.is_ge))
                link(nc.vector.tensor_tensor(rank[:, :, k:8], rank[:, :, k:8], cmp[:, :, 0:w], ALU.add))
                link(nc.vector.tensor_tensor(rank[:, :, 0:w], rank[:, :, 0:w], cmp[:, :, 0:w], ALU.subtract))

        def logits_sum(dve, link, m, ne):
            dve.wait_ge(m.lgl, 1)
            for h in range(2):
                lv = bank[4 + h][:, 0:8 * 2 * ne].rearrange("p (t e) -> p t e", t=8)
                op = nc.vector.tensor_tensor(lg[:, 8 * h:8 * h + 8, 0:ne], lv[:, :, 0:ne],
                                             lgl[:, 8 * h:8 * h + 8, 0:ne], ALU.add)
            op.then_inc(m.lgl, 1)
            dve.wait_ge(m.lgl, 2)

        def over_experts(v, n):
            return v.unsqueeze(2).broadcast_to([P, TILES, n])

        def route0_vector(dve, m):
            link = Chain(dve, m.rs)
            logits_sum(dve, link, m, E0)
            dve.wait_ge(m.ra, 1)
            sg = sc[:, :, :].rearrange("p t (g k) -> p t g k", g=GROUPS0)
            link(nc.vector.tensor_reduce(gs[:, :, :], sg, AX_X, ALU.add))
            ranks(link, gs)
            link(nc.vector.tensor_scalar(cmp[:, :, :], rank[:, :, :], float(TOPG0) - 0.5, None, ALU.is_lt))
            link(nc.vector.tensor_tensor(msc[:, :, :].rearrange("p t (g k) -> p t g k", g=GROUPS0), sg,
                                         cmp[:, :, :].unsqueeze(3).broadcast_to([P, TILES, GROUPS0, E0 // GROUPS0]),
                                         ALU.mult))
            for t in range(TILES):
                op = nc.vector.max(top8[:, t, :], msc[:, t, :])
            link(op)
            for t in range(TILES):
                op = nc.vector.match_replace(out=rep[:, t, :], in_to_replace=top8[:, t, :], in_values=msc[:, t, :],
                                             imm_value=-1.0)
            link(op)
            link(nc.vector.tensor_tensor(selw[:, :, :], rep[:, :, :], msc[:, :, :], ALU.not_equal))
            link(nc.vector.tensor_tensor(selw[:, :, :], selw[:, :, :], msc[:, :, :], ALU.mult))
            link(nc.vector.tensor_reduce(rsum[:, :], selw[:, :, :], AX_X, ALU.add))
            link(nc.vector.tensor_scalar(rsum[:, :], rsum[:, :], 1e-12, None, ALU.max))
            link(nc.vector.reciprocal(rrec[:, :], rsum[:, :]))
            link(nc.vector.tensor_scalar(rrec[:, :], rrec[:, :], tg[:, 2:3], None, ALU.mult))
            link(nc.vector.tensor_tensor(cw[:, :, 0:E0], selw[:, :, :], over_experts(rrec[:, :], E0), ALU.mult))
            link(nc.vector.memset(cw[:, :, E0:NB0], 1.0))
            link(nc.vector.tensor_scalar(cw[:, :, E0:NB0], cw[:, :, E0:NB0], tg[:, 2:3], None, ALU.mult))

        def route0_scalar(act, m):
            act.wait_ge(m.lgl, 2)
            nc.scalar.activation(sc[:, :, :], lg[:, :, :], ACT.Sigmoid).then_inc(m.ra, 1)

        def route1_vector(dve, m):
            link = Chain(dve, m.rs)
            logits_sum(dve, link, m, E1)
            link(nc.vector.tensor_reduce(rmx[:, :], lg[:, :, 0:E1], AX_X, ALU.max))
            link(nc.vector.tensor_tensor(msc[:, :, 0:E1], lg[:, :, 0:E1], over_experts(rmx[:, :], E1), ALU.subtract))
            dve.wait_ge(m.ra, 1)
            link(nc.vector.tensor_reduce(rsum[:, :], rep[:, :, 0:E1], AX_X, ALU.add))
            link(nc.vector.reciprocal(rrec[:, :], rsum[:, :]))
            link(nc.vector.tensor_tensor(sc[:, :, 0:E1], rep[:, :, 0:E1], over_experts(rrec[:, :], E1), ALU.mult))
            link(nc.vector.tensor_tensor(gs[:, :, :], sc[:, :, 0:E1],
                                         rbias[:, :].unsqueeze(1).broadcast_to([P, TILES, E1]), ALU.add))
            ranks(link, gs)
            link(nc.vector.tensor_scalar(cmp[:, :, :], rank[:, :, :], float(TOP1) - 0.5, None, ALU.is_lt))
            link(nc.vector.tensor_tensor(selw[:, :, 0:E1], cmp[:, :, :], sc[:, :, 0:E1], ALU.mult))
            link(nc.vector.tensor_scalar(selw[:, :, 0:E1], selw[:, :, 0:E1], tg[:, 3:4], None, ALU.mult))
            link(nc.vector.tensor_copy(cw[:, :, 0:2 * E1].rearrange("p t (e k) -> p t e k", k=2),
                                       selw[:, :, 0:E1].unsqueeze(3).broadcast_to([P, TILES, E1, 2])))
            link(nc.vector.memset(cw[:, :, 2 * E1:NB1], 1.0))
            link(nc.vector.tensor_scalar(cw[:, :, 2 * E1:NB1], cw[:, :, 2 * E1:NB1], tg[:, 3:4], None, ALU.mult))

        def route1_scalar(act, m):
            act.wait_ge(m.rs, 2)
            nc.scalar.activation(rep[:, :, 0:E1], msc[:, :, 0:E1], ACT.Exp).then_inc(m.ra, 1)

        A = s_a1

        def sync_a1(sp):
            sp.wait_ge(moe[0].acc, 4 * NB0)
            sp.dma_start(wsim[:, :, :], wsim_in).then_inc(A["par"], 16)
            sp.dma_start(w1row[:, :], w1row_in.broadcast_to([P, DIM])).then_inc(A["par"], 16)
            sp.dma_start(bsim[:, :], bsim_in.broadcast_to([P, 1])).then_inc(A["par"], 16)
            sp.dma_start(bqv[:, :], bqv_in.broadcast_to([P, DIM])).then_inc(A["par"], 16)
            sp.dma_start(wqv[:, :, :], wqv_in).then_inc(A["wq"], 16)
            for b in range(BATCH):
                if b:
                    sp.wait_ge(A["clo"], b)
                    sp.wait_ge(A["tlo"], b)
                sp.dma_start(craw[:, :, :], ctxt_in[:, :, b * SEQ:(b + 1) * SEQ]).then_inc(A["ctx_t"], 16)
                sp.dma_start(traw[:, :, :], ctx_in[:, b * TPB:(b + 1) * TPB, :]).then_inc(A["ctx"], 16)

        def tensor_a1(pe):
            for b in range(BATCH):
                n = b + 1
                pe.wait_ge(A["xn"], n)
                if b:
                    pe.wait_ge(A["prod"], 2 * b)
                for c in range(CH):
                    for j in range(TPB):
                        mm = pe.transpose(bank[4 + c][:, j * P:(j + 1) * P], xn[:, TPB * b + j, c * P:(c + 1) * P],
                                          ident)
                    mm.then_inc(A["tr"], 1)
                pe.wait_ge(A["alo"], 2 * n)
                pe.wait_ge(A["clo"], n)
                if b:
                    pe.wait_ge(A["x"], 4 * b)
                for j in range(TPB):
                    k = 0
                    for c in range(CH):
                        for ap_, cp in ((aench, ch_), (aench, cl_), (aencl, ch_)):
                            mm = pe.matmul(bank[j][:, :], ap_[:, c, j * P:(j + 1) * P], cp[:, c, :],
                                           start=(k == 0), stop=(k == 5))
                            k += 1
                    mm.then_inc(A["sim"], 1)
                for jc in range(TPB):
                    pe.wait_ge(A["pn"], 4 * n)
                    for j in range(TPB):
                        mm = pe.transpose(bank[jc][:, j * P:(j + 1) * P], prob1[:, j, jc * P:(jc + 1) * P], ident)
                    mm.then_inc(A["pt"], 1)
                pe.wait_ge(A["batt"], n)
                for c in range(CH):
                    for j in range(TPB):
                        mm = pe.matmul(bank[6][:, c:c + 1], xn[:, TPB * b + j, c * P:(c + 1) * P], batt[:, j:j + 1],
                                       start=(j == 0), stop=(j == TPB - 1))
                mm.then_inc(A["hb"], 1)
                pe.wait_ge(A["elo"], 2 * n)
                pe.wait_ge(A["tlo"], n)
                pe.wait_ge(A["a"], 2 * n)
                for c in range(CH):
                    k = 0
                    for jc in range(TPB):
                        if c == 0:
                            pe.wait_ge(A["ptl"], 4 * b + jc + 1)
                        for tp, pp in ((th_, p1th), (th_, p1tl), (tl_, p1th)):
                            mm = pe.matmul(bank[4 + c][:, :], tp[:, jc, c * P:(c + 1) * P], pp[:, jc, :],
                                           start=(k == 0), stop=(k == 11))
                            k += 1
                    mm.then_inc(A["hq"], 1)
                pe.wait_ge(A["prl"], 2 * n)
                pe.wait_ge(A["hql"], 2 * n)
                pe.wait_ge(A["wlo"], n)
                for j in range(TPB):
                    k = 0
                    for g, (fh, fl) in enumerate(((ench, encl), (hqh, hql), (prodh, prodl))):
                        for c in range(CH):
                            for fp, wp in ((fh, wqh), (fh, wql), (fl, wqh)):
                                mm = pe.matmul(bank[j][:, 0:DIM], fp[:, c, j * P:(j + 1) * P], wp[:, CH * g + c, :],
                                               start=(k == 0), stop=(k == 17))
                                k += 1
                    mm.then_inc(A["o"], 1)

        def scalar_a1(act):
            layernorm_sqrt(act, 2, 0)
            for b in range(BATCH):
                n = b + 1
                if b:
                    act.wait_ge(A["o"], 4 * b)
                act.wait_ge(A["ctx_t"], 16 * n)
                nc.scalar.activation(ch_[:, :, :], craw[:, :, :], ACT.Copy).then_inc(A["chi"], 1)
                act.wait_ge(A["ctx"], 16 * n)
                nc.scalar.activation(th_[:, :, :], traw[:, :, :], ACT.Copy).then_inc(A["thi"], 1)
                for c in range(CH):
                    act.wait_ge(A["tr"], 2 * b + c + 1)
                    nc.scalar.activation(ench[:, c, :], bank[4 + c][:, :], ACT.Copy).then_inc(A["ehi"], 1)
                    nc.scalar.activation(enc[:, c, :], bank[4 + c][:, :], ACT.Copy).then_inc(A["enc"], 1)
                    act.wait_ge(A["a"], 2 * b + c + 1)
                    nc.scalar.activation(aench[:, c, :], aenc[:, c, :], ACT.Copy).then_inc(A["ahi"], 1)
                for j in range(TPB):
                    act.wait_ge(A["nm"], 4 * b + j + 1)
                    nc.scalar.activation(prob1[:, j, :], bank[j][:, :], ACT.Exp, bias=nm1[:, j:j + 1],
                                         accum_out=den1[:, j:j + 1]).then_inc(A["p"], 1)
                act.wait_ge(A["ngmx"], n)
                nc.scalar.activation(eb[:, :], msim[:, :], ACT.Exp, bias=ngmx1[:, :],
                                     accum_out=ebs[:, :]).then_inc(A["eb"], 1)
                for jc in range(TPB):
                    act.wait_ge(A["pt"], 4 * b + jc + 1)
                    nc.scalar.activation(p1th[:, jc, :], bank[jc][:, :], ACT.Copy).then_inc(A["pth"], 1)
                if b == 0:
                    act.wait_ge(A["wq"], 16)
                    nc.scalar.activation(wqh[:, CH:3 * CH, :], wqv[:, CH:3 * CH, :], ACT.Copy).then_inc(A["wqs"], 1)
                act.wait_ge(A["w14"], n)
                nc.scalar.activation(wqh[:, 0:CH, :], w14[:, :, :], ACT.Copy).then_inc(A["whi"], 1)
                for c in range(CH):
                    act.wait_ge(A["hq"], 2 * b + c + 1)
                    nc.scalar.activation(hqh[:, c, :], bank[4 + c][:, :], ACT.Copy).then_inc(A["hqh"], 1)
                    act.wait_ge(A["prod"], 2 * b + c + 1)
                    nc.scalar.activation(prodh[:, c, :], prod[:, c, :], ACT.Copy).then_inc(A["prh"], 1)

        def vector_a1(dve):
            layernorm_stats(dve, 2, 0, TILES, 0, 0)
            for b in range(BATCH):
                for j in range(TPB):
                    t = TPB * b + j
                    op = nc.vector.tensor_scalar(xn[:, t, :], x[:, t, :], meanvar[:, t, 0:1], rstd[:, t:t + 1],
                                                 ALU.subtract, ALU.mult)
                op.then_inc(A["xn"], 1)
            dve.wait_ge(A["par"], 64)
            nc.vector.tensor_scalar(bqvg[:, :], bqv[:, :], tg[:, 1:2], None, ALU.mult).then_inc(A["bq"], 1)
            dve.wait_ge(A["xn"], BATCH)
            for b in range(BATCH):
                n = b + 1
                dve.wait_ge(A["chi"], n)
                nc.vector.tensor_tensor(cl_[:, :, :], craw[:, :, :], f32(ch_[:, :, :]), ALU.subtract).then_inc(A["clo"], 1)
                for c in range(CH):
                    dve.wait_ge(A["enc"], 2 * b + c + 1)
                    nc.vector.tensor_scalar(aenc[:, c, :], bank[4 + c][:, :], wsim[:, 1, c:c + 1], wsim[:, 0, c:c + 1],
                                            ALU.mult, ALU.add).then_inc(A["a"], 1)
                    nc.vector.tensor_tensor(encl[:, c, :], enc[:, c, :], f32(ench[:, c, :]),
                                            ALU.subtract).then_inc(A["elo"], 1)
                    dve.wait_ge(A["ahi"], 2 * b + c + 1)
                    nc.vector.tensor_tensor(aencl[:, c, :], aenc[:, c, :], f32(aench[:, c, :]),
                                            ALU.subtract).then_inc(A["alo"], 1)
                dve.wait_ge(A["thi"], n)
                nc.vector.tensor_tensor(tl_[:, :, :], traw[:, :, :], f32(th_[:, :, :]), ALU.subtract).then_inc(A["tlo"], 1)
                if b:
                    dve.wait_ge(A["msim"], b)
                for j in range(TPB):
                    if 4 * b + j:
                        dve.wait_ge(A["r"], 4 * b + j)
                    nc.vector.tensor_tensor_reduce(out=junk[:, :], in0=xn[:, TPB * b + j, :], in1=w1row[:, :], scale=1.0,
                                                   scalar=bsim[:, 0:1], op0=ALU.mult, op1=ALU.add,
                                                   accum_out=rterm[:, j:j + 1]).then_inc(A["r"], 1)
                for j in range(TPB):
                    dve.wait_ge(A["sim"], 4 * b + j + 1)
                    nc.vector.tensor_reduce(nm1[:, j:j + 1], bank[j][:, :], AX_X, ALU.max, negate=True).then_inc(A["nm"], 1)
                dve.wait_ge(A["nm"], 4 * n)
                dve.wait_ge(A["r"], 4 * n)
                nc.vector.tensor_tensor(msim[:, :], rterm[:, :], nm1[:, :], ALU.subtract).then_inc(A["msim"], 1)
                dve.wait_ge(A["msim"], n)
                nc.vector.tensor_reduce(mx1[:, :], msim[:, :], AX_X, ALU.max).then_inc(A["mx"], 1)
                for j in range(TPB):
                    dve.wait_ge(A["p"], 4 * b + j + 1)
                    nc.vector.reciprocal(rd1[:, j:j + 1], den1[:, j:j + 1]).then_inc(A["rd"], 1)
                    dve.wait_ge(A["rd"], 4 * b + j + 1)
                    nc.vector.tensor_scalar(prob1[:, j, :], prob1[:, j, :], rd1[:, j:j + 1], None,
                                            ALU.mult).then_inc(A["pn"], 1)
                dve.wait_ge(A["gmx"], n)
                nc.vector.tensor_scalar(ngmx1[:, :], gmx1[:, :], -1.0, None, ALU.mult).then_inc(A["ngmx"], 1)
                dve.wait_ge(A["ebt"], n)
                nc.vector.reciprocal(ebr[:, :], ebt[:, :]).then_inc(A["ebr"], 1)
                dve.wait_ge(A["ebr"], n)
                nc.vector.tensor_scalar(batt[:, :], eb[:, :], ebr[:, 0:1], None, ALU.mult).then_inc(A["batt"], 1)
                for jc in range(TPB):
                    dve.wait_ge(A["pth"], 4 * b + jc + 1)
                    nc.vector.tensor_tensor(p1tl[:, jc, :], bank[jc][:, :], f32(p1th[:, jc, :]),
                                            ALU.subtract).then_inc(A["ptl"], 1)
                dve.wait_ge(A["hb"], n)
                nc.vector.tensor_copy(hbar[:, :], bank[6][:, 0:CH]).then_inc(A["hbc"], 1)
                dve.wait_ge(A["hbc"], n)
                dve.wait_ge(A["wq"], 16)
                for c in range(CH):
                    op = nc.vector.scalar_tensor_tensor(out=w14[:, c, :], in0=wqv[:, 3 * CH + c, :], scalar=hbar[:, c:c + 1],
                                                        in1=wqv[:, c, :], op0=ALU.mult, op1=ALU.add)
                op.then_inc(A["w14"], 1)
                if b == 0:
                    dve.wait_ge(A["wqs"], 1)
                    nc.vector.tensor_tensor(wql[:, CH:3 * CH, :], wqv[:, CH:3 * CH, :], f32(wqh[:, CH:3 * CH, :]),
                                            ALU.subtract)
                dve.wait_ge(A["whi"], n)
                nc.vector.tensor_tensor(wql[:, 0:CH, :], w14[:, :, :], f32(wqh[:, 0:CH, :]),
                                        ALU.subtract).then_inc(A["wlo"], 1)
                for c in range(CH):
                    dve.wait_ge(A["hqh"], 2 * b + c + 1)
                    nc.vector.tensor_tensor(hql[:, c, :], bank[4 + c][:, :], f32(hqh[:, c, :]),
                                            ALU.subtract).then_inc(A["hql"], 1)
                    nc.vector.tensor_tensor(prod[:, c, :], enc[:, c, :], bank[4 + c][:, :], ALU.mult).then_inc(A["prod"], 1)
                    dve.wait_ge(A["prh"], 2 * b + c + 1)
                    nc.vector.tensor_tensor(prodl[:, c, :], prod[:, c, :], f32(prodh[:, c, :]),
                                            ALU.subtract).then_inc(A["prl"], 1)
                dve.wait_ge(A["xb"], TILES)
                for j in range(TPB):
                    t = TPB * b + j
                    dve.wait_ge(A["o"], t + 1)
                    nc.vector.scalar_tensor_tensor(out=x[:, t, :], in0=bank[j][:, 0:DIM], scalar=tg[:, 1:2],
                                                   in1=x[:, t, :], op0=ALU.mult, op1=ALU.add).then_inc(A["x"], 1)

        def pool_a1(pool):
            pool.wait_ge(A["bq"], 1)
            pool.wait_ge(A["xn"], BATCH)
            for t in range(TILES):
                nc.gpsimd.tensor_tensor(x[:, t, :], x[:, t, :], bqvg[:, :], ALU.add).then_inc(A["xb"], 1)
            for b in range(BATCH):
                pool.wait_ge(A["mx"], b + 1)
                nc.gpsimd.partition_all_reduce(gmx1[:, :], mx1[:, :], P, RMAX).then_inc(A["gmx"], 1)
                pool.wait_ge(A["eb"], b + 1)
                nc.gpsimd.partition_all_reduce(ebt[:, :], ebs[:, :], P, RADD).then_inc(A["ebt"], 1)

        @block.sync
        def _(sp):
            sp.dma_start(consts[:, :], consts_in).then_inc(s_const, 16)
            sp.dma_start(gates[:, :], gates_in.broadcast_to([P, 4])).then_inc(s_gates, 16)
            for b in range(BATCH):
                sp.dma_start(x[:, b * TPB:(b + 1) * TPB, :], x_in[:, b * TPB:(b + 1) * TPB, :]).then_inc(s_x[b], 16)
            for s in range(KSLICES):
                if s >= 2:
                    sp.wait_ge(s_klo, s - 1)
                for r in range(4):
                    sp.dma_start(kraw[32 * r:32 * r + 32, s % 2], kt_in[:, :, s * KSL:(s + 1) * KSL]
                                 ).then_inc(s_kraw[s % 2], 16)
                if s == 1:
                    sp.dma_start(vraw[:, :, :], v_in).then_inc(s_vraw, 16)
            for L, (nb, w_in, rw_in) in enumerate(((NB0, w0_in, rw0_in), (NB1, w1_in, rw1_in))):
                m = moe[L]
                if L == 0:
                    sp.wait_ge(s_xa, 2 * TILES)
                    sp.wait_ge(s_pv, UNITS)
                    sp.dma_start(rraw[:, :, :], rw_in).then_inc(m.rload, 16)
                else:
                    sp.wait_ge(A["x"], TILES)
                    sp.dma_start(rraw[:, :, 0:E1], rw_in).then_inc(m.rload, 16)
                    sp.dma_start(rbias[:, :], rbias1_in.broadcast_to([P, E1])).then_inc(m.rload, 16)
                moe_sync(sp, L, m, nb, w_in)
                if L == 0:
                    sync_a1(sp)
            for b in range(BATCH):
                sp.wait_ge(moe[1].acc, 4 * (NB1 - 1) + b + 1)
                sp.dma_start(out[:, b * TPB:(b + 1) * TPB, :], x[:, b * TPB:(b + 1) * TPB, :]).then_inc(s_out, 16)
            sp.wait_ge(s_out, 16 * BATCH)

        @block.tensor
        def _(pe):
            attention_tensor(pe)
            moe_prep_tensor(pe, 0, moe[0])
            moe_tensor(pe, 0, moe[0], NB0)
            tensor_a1(pe)
            moe_prep_tensor(pe, 1, moe[1])
            moe_tensor(pe, 1, moe[1], NB1)

        @block.scalar
        def _(act):
            attention_scalar(act)
            moe_prep_scalar(act, 0, moe[0])
            route0_scalar(act, moe[0])
            moe_scalar(act, 0, moe[0], NB0)
            scalar_a1(act)
            moe_prep_scalar(act, 1, moe[1])
            route1_scalar(act, moe[1])
            moe_scalar(act, 1, moe[1], NB1)

        @block.vector
        def _(dve):
            attention_vector(dve)
            dve.wait_ge(s_xa, 2 * TILES)
            moe_prep_vector(dve, 0, moe[0])
            route0_vector(dve, moe[0])
            moe_vector(dve, 0, moe[0], NB0)
            dve.wait_ge(moe[0].acc, 4 * NB0)
            vector_a1(dve)
            dve.wait_ge(A["x"], TILES)
            moe_prep_vector(dve, 1, moe[1])
            route1_vector(dve, moe[1])
            moe_vector(dve, 1, moe[1], NB1)

        @block.gpsimd
        def _(pool):
            attention_pool(pool)
            moe_pool(pool, 0, moe[0], NB0)
            pool_a1(pool)
            moe_pool(pool, 1, moe[1], NB1)


def _weights(gate, up, down):
    import numpy as np

    def cols(w):
        return w.T.reshape(CH, P, FF).transpose(1, 0, 2).reshape(P, CH * FF)
    return [np.concatenate([cols(gate[s:s + FF]), cols(up[s:s + FF]), down[:, s:s + FF].T], axis=1)
            for s in range(0, gate.shape[0], FF)]


def kernel(**inputs):
    import numpy as np
    import concourse.bacc as bacc
    from concourse import mybir as mb
    from concourse.bass_utils import run_bass_kernel_spmd as run

    a = {k: np.asarray(v) for k, v in inputs.items()}
    f = np.float32

    def by_tile(v):
        return v.reshape(-1, P, DIM).transpose(1, 0, 2)

    def by_chunk(w):
        return w.reshape(-1, P, w.shape[1]).transpose(1, 0, 2)

    tokens = a["ctx_1024"].reshape(TOKENS, DIM)
    padded = np.pad(tokens, ((BAND, BAND), (0, 0)))
    kt = padded.T.reshape(PAIRS, 32, KCOLS).transpose(1, 0, 2)
    rows, keys = np.arange(P)[:, None], np.arange(WIN)[None, :]
    band = np.abs(keys - BAND - rows) <= BAND
    masks = [band & ~((j == 0) & (keys < BAND)) & ~((j == TPB - 1) & (keys >= P + BAND)) for j in range(TPB)]
    head = np.stack([(np.arange(P) % 32) < 16, (np.arange(P) % 32) >= 16], 1)
    consts = np.concatenate([np.eye(P), head] + [np.where(m, 0.0, MASKED) for m in masks], 1).astype(f)
    w0 = np.stack([_weights(a["L0_ffn_expert_gate"][e], a["L0_ffn_expert_up"][e], a["L0_ffn_expert_down"][e])[0]
                   for e in range(E0)]
                  + _weights(a["L0_ffn_shared_gate_w"], a["L0_ffn_shared_up_w"], a["L0_ffn_shared_down_w"]))
    w1 = np.stack(sum([_weights(a["L1_ffn_w1"][e], a["L1_ffn_w3"][e], a["L1_ffn_w2"][e]) for e in range(E1)], [])
                  + _weights(a["L1_ffn_sw1"], a["L1_ffn_sw3"], a["L1_ffn_sw2"]))
    wsim = a["L1_xattn_w_sim"].reshape(3, CH, P).transpose(2, 0, 1)[:, 1:3]
    arrays = {
        "x": by_tile(a["x"]), "kt": kt, "v": by_tile(padded), "ctx": by_tile(tokens), "ctxt": by_chunk(tokens.T),
        "consts": consts, "gates": np.concatenate([a["g_xattn"], a["g_ffn"]])[None],
        "rw0": by_chunk(a["L0_ffn_gate_w"].T), "w0": w0, "wsim": wsim, "w1row": a["L1_xattn_w_sim"][None, 0:DIM],
        "bsim": a["L1_xattn_b_sim"][None], "wqv": by_chunk(a["L1_xattn_W_qv"]), "bqv": a["L1_xattn_b_qv"][None],
        "rw1": by_chunk(a["L1_ffn_gate_w"].T), "rbias1": a["L1_ffn_gate_bias"][None], "w1": w1,
    }
    arrays = {f"in_{k}": np.ascontiguousarray(v) for k, v in arrays.items()}
    nc = bacc.Bacc("TRN2", target_bir_lowering=False, num_devices=1)
    args = [nc.dram_tensor(k, v.shape, mb.dt.from_np(v.dtype), kind="ExternalInput").ap() for k, v in arrays.items()]
    args.append(nc.dram_tensor("out", (P, TILES, DIM), mb.dt.float32, kind="ExternalOutput").ap())
    gated_xattn_moe_kernel(nc, *args)
    r = run(nc, [arrays], core_ids=[0])
    return np.asarray(r.results[0]["out"]).transpose(1, 0, 2).reshape(BATCH, SEQ, DIM)
```

```python
from contextlib import ExitStack

import concourse.bass as bass
from concourse import mybir

P = 128
BATCH, SEQ, DIM = 4, 512, 256
TOKENS = BATCH * SEQ
TILES = TOKENS // P
TPB = SEQ // P
CH = DIM // P
HEADS, HD = 16, 16
PAIRS = HEADS // 2
BAND = 64
WIN = P + 2 * BAND
KCOLS = TOKENS + 2 * BAND
KPIECES = 4
KPC = KCOLS // KPIECES
VGROUPS = ((0, 5), (5, 9), (9, 13), (13, 17))
VTILES = TILES + 1
VW = 3 * HD + 1
MASKED = -1e9
EPS = 1e-5
FF = 128
WCOLS = 2 * CH * FF + DIM
E0, TOP0, GROUPS0, TOPG0 = 32, 8, 8, 4
E1, TOP1 = 8, 2
SH0, SH1 = 1, 4
NB0 = SH0 + E0
NB1 = SH1 + 2 * E1

ALU = mybir.AluOpType
ACT = mybir.ActivationFunctionType
AX_X = mybir.AxisListType.X
F32 = mybir.dt.float32
F32R = mybir.dt.float32r
BF16 = mybir.dt.bfloat16
F16 = mybir.dt.float16
RMAX = bass.bass_isa.ReduceOp.max
RADD = bass.bass_isa.ReduceOp.add


def f32(ap):
    return ap.bitcast(F32)


def late(t, n):
    return not isinstance(t, int) or t >= n


def gated_xattn_moe_kernel(nc, x_in, kt_in, v_in, ctx_in, ctxt_in, consts_in, gates_in, rw0_in, w0_in,
                           wsim_in, w1row_in, bsim_in, wqv_in, bqv_in, rw1_in, rbias1_in, w1_in, out):
    ctx = ExitStack()
    with ctx:
        def sb(name, shape, dt, scope=ctx):
            return scope.enter_context(nc.sbuf_tensor(name, shape, dt))

        def sem(name):
            return ctx.enter_context(nc.semaphore(name))

        bank = [ctx.enter_context(nc.psum_tensor(f"bank{i}", [P, 512], F32)) for i in range(8)]

        x = sb("x", [P, TILES, DIM], F32)
        consts = sb("consts", [P, P + 2 + TPB * WIN], F32)
        ident = consts[:, 0:P]
        head_mask = consts[:, P:P + 2]
        band_f32 = consts[:, P + 2:P + 2 + TPB * WIN]
        gates = sb("gates", [P, 4], F32)
        tg = sb("tg", [P, 4], F32)
        stats = sb("stats", [P, TILES, 6], F32)
        meanvar = sb("meanvar", [P, TILES, 2], F32)
        varp = sb("varp", [P, TILES], F32)
        minus_half = sb("minus_half", [P, TPB], F32)
        rstd = sb("rstd", [P, TILES], F32)

        a0 = ExitStack()
        kst = sb("kst", [P, PAIRS, KCOLS], F32R, a0)
        kraw = sb("kraw", [P, 2, 2, KPC], F32, a0)
        khl = sb("khl", [P, 2, 2, 2, KPC], F32R, a0)
        v3 = sb("v3", [P, VTILES, HEADS, VW], BF16, a0)
        vraw = sb("vraw", [P, 2, 5, DIM], F32, a0)
        band = sb("band", [P, TILES, WIN], BF16, a0)
        identb = sb("identb", [P, P], BF16, a0)
        qn = sb("qn", [P, 2, PAIRS, 4, 32], F32, a0)
        qst = sb("qst", [P, PAIRS, P], F32R, a0)
        qm = sb("qm", [P, 2, 2, PAIRS, P], F32R, a0)
        nmax = sb("nmax", [P, 4, 2], F32, a0)
        prob = sb("prob", [P, 4, 2, WIN], F32, a0)
        pth = sb("pth", [P, 2, 2, WIN], F16, a0)
        ptl = sb("ptl", [P, 2, 2, WIN], F16, a0)
        rden = sb("rden", [P, 2, PAIRS], F32, a0)
        rdeng = sb("rdeng", [P, 2, PAIRS], F32, a0)
        osum = sb("osum", [P, 2, PAIRS, HD], F32, a0)
        oscaled = sb("oscaled", [P, 2, PAIRS, HD], F32, a0)
        a0.close()

        xn = sb("xn", [P, TILES, DIM], F32)

        rt = ExitStack()
        xh = sb("xh", [P, CH, TOKENS], F32R, rt)
        xl = sb("xl", [P, CH, TOKENS], F32R, rt)
        wraw = sb("wraw", [P, 2, WCOLS], F32, rt)
        wh = sb("wh", [P, 2, WCOLS], F32R, rt)
        wl = sb("wl", [P, 2, WCOLS], F32R, rt)
        sil = sb("sil", [P, 2, 512], F32, rt)
        hid = sb("hid", [P, 2, 512], F32, rt)
        hidh = sb("hidh", [P, 2, 512], F32R, rt)
        hidl = sb("hidl", [P, 2, 512], F32R, rt)
        cw = sb("cw", [P, TILES, NB0], F32, rt)
        rraw = sb("rraw", [P, CH, E0], F32, rt)
        rwhl = sb("rwhl", [P, CH, 2 * E0], F32R, rt)
        rbias = sb("rbias", [P, E1], F32, rt)
        lgl = sb("lgl", [P, TILES, E0], F32, rt)
        lg = sb("lg", [P, TILES, E0], F32, rt)
        sc = sb("sc", [P, TILES, E0], F32, rt)
        msc = sb("msc", [P, TILES, E0], F32, rt)
        rep = sb("rep", [P, TILES, E0], F32, rt)
        selw = sb("selw", [P, TILES, E0], F32, rt)
        gs = sb("gs", [P, TILES, 8], F32, rt)
        rank = sb("rank", [P, TILES, 8], F32, rt)
        cmp = sb("cmp", [P, TILES, 8], F32, rt)
        top8 = sb("top8", [P, TILES, 8], F32, rt)
        rsum = sb("rsum", [P, TILES], F32, rt)
        rrec = sb("rrec", [P, TILES], F32, rt)
        rmx = sb("rmx", [P, TILES], F32, rt)
        rt.close()

        a1 = ExitStack()
        craw = sb("craw", [P, CH, SEQ], F32, a1)
        ctxh = sb("ctxh", [P, CH, SEQ], F32R, a1)
        ctxl = sb("ctxl", [P, CH, SEQ], F32R, a1)
        traw = sb("traw", [P, TPB, DIM], F32, a1)
        tokh = sb("tokh", [P, TPB, DIM], F32R, a1)
        tokl = sb("tokl", [P, TPB, DIM], F32R, a1)
        enc = sb("enc", [P, 2, CH, SEQ], F32, a1)
        ench = sb("ench", [P, 2, CH, SEQ], F32R, a1)
        encl = sb("encl", [P, 2, CH, SEQ], F32R, a1)
        aenc = sb("aenc", [P, CH, SEQ], F32, a1)
        aench = sb("aench", [P, CH, SEQ], F32R, a1)
        aencl = sb("aencl", [P, CH, SEQ], F32R, a1)
        prob1 = sb("prob1", [P, TPB, SEQ], F32, a1)
        p1th = sb("p1th", [P, TPB, SEQ], F32R, a1)
        p1tl = sb("p1tl", [P, TPB, SEQ], F32R, a1)
        hqh = sb("hqh", [P, CH, SEQ], F32R, a1)
        hql = sb("hql", [P, CH, SEQ], F32R, a1)
        prod = sb("prod", [P, CH, SEQ], F32, a1)
        prodh = sb("prodh", [P, CH, SEQ], F32R, a1)
        prodl = sb("prodl", [P, CH, SEQ], F32R, a1)
        wqv = sb("wqv", [P, 4 * CH, DIM], F32, a1)
        wqh = sb("wqh", [P, 3 * CH, DIM], F32R, a1)
        wql = sb("wql", [P, 3 * CH, DIM], F32R, a1)
        w14 = sb("w14", [P, CH, DIM], F32, a1)
        wsim = sb("wsim", [P, 2, CH], F32, a1)
        w1row = sb("w1row", [P, DIM], F32, a1)
        bqv = sb("bqv", [P, DIM], F32, a1)
        bqvg = sb("bqvg", [P, DIM], F32, a1)
        bsim = sb("bsim", [P, 1], F32, a1)
        junk = sb("junk", [P, DIM], F32, a1)
        rterm = sb("rterm", [P, TPB], F32, a1)
        nm1 = sb("nm1", [P, TPB], F32, a1)
        den1 = sb("den1", [P, TPB], F32, a1)
        rd1 = sb("rd1", [P, TPB], F32, a1)
        msim = sb("msim", [P, TPB], F32, a1)
        mx1 = sb("mx1", [P, 1], F32, a1)
        gmx1 = sb("gmx1", [P, 1], F32, a1)
        ngmx1 = sb("ngmx1", [P, 1], F32, a1)
        eb = sb("eb", [P, TPB], F32, a1)
        ebs = sb("ebs", [P, 1], F32, a1)
        ebt = sb("ebt", [P, 1], F32, a1)
        ebr = sb("ebr", [P, 1], F32, a1)
        batt = sb("batt", [P, TPB], F32, a1)
        hbar = sb("hbar", [P, CH], F32, a1)
        a1.close()

        s_const = sem("const_loaded")
        s_gates = sem("gates_loaded")
        s_x = [sem(f"x_loaded{b}") for b in range(BATCH)]
        s_kraw = [sem(f"kraw_loaded{i}") for i in range(2)]
        s_vraw = [sem(f"vraw_loaded{i}") for i in range(2)]
        s_tg = sem("tanh_ready")
        s_band = sem("band_ready")
        s_ln = [sem(f"ln_stats{i}") for i in range(4)]
        s_lnp = [sem(f"ln_rsqrt{i}") for i in range(4)]
        s_fill = sem("pool_filled")
        s_khi = sem("k_hi")
        s_klo = sem("k_lo")
        s_kst = [sem(f"k_stacked{i}") for i in range(KPIECES)]
        s_va = sem("v_parts_act")
        s_vd = sem("v_parts_dve")
        s_qn = sem("qn_ready")
        s_tq = sem("q_transposed")
        s_ahi = sem("q_hi")
        s_alo = sem("q_lo")
        s_qm = sem("q_masked")
        s_s = sem("scores_ready")
        s_nm = sem("max_ready")
        s_p = sem("probs_ready")
        s_pt = sem("probs_transposed")
        s_pth = sem("pt_hi")
        s_ptl = sem("pt_lo")
        s_pv = sem("pv_done")
        s_rr = sem("rden_ready")
        s_o = sem("o_summed")
        s_os = sem("o_scaled")
        s_xa = sem("x_attended")

        class Moe:

            def __init__(self, n):
                def s(name):
                    return sem(f"{name}{n}")
                self.rload = s("router_loaded")
                self.rhi = s("router_hi")
                self.rlo = s("router_lo")
                self.xn = s("xn_ready")
                self.tr = s("xn_transposed")
                self.xh = s("xh_ready")
                self.xl = s("xl_ready")
                self.lg = s("logits_ready")
                self.lgl = s("logits_low_copied")
                self.rs = s("route_step")
                self.ra = s("route_act")
                self.cw = s("cw_ready")
                self.wload = [s(f"w_loaded_{i}_") for i in range(2)]
                self.whi = s("w_hi")
                self.wlo = s("w_lo")
                self.gate = s("gate_ready")
                self.up = s("up_ready")
                self.sil = s("silu_ready")
                self.h = s("h_ready")
                self.hh = s("h_hi")
                self.hl = s("h_lo")
                self.y = s("y_ready")
                self.acc = s("y_added")

        moe = [Moe(0), Moe(1)]
        s_a1 = {n: sem("a1_" + n) for n in (
            "par", "bq", "wq", "wqs", "wq2", "ctx_t", "ctx", "chi", "clo", "thi", "tlo", "xn", "tr", "enc", "ehi", "elo",
            "a", "ahi", "alo", "r", "sim", "nm", "p", "rd", "pn", "pt", "pth", "ptl", "msim", "mx", "gmx", "ngmx", "eb", "ebt",
            "ebr", "batt", "hb", "hbc", "w14", "whi", "wlo", "hq", "hqh", "hql", "prod", "prh", "prl", "xb", "o", "x")}
        s_out = sem("out_stored")

        block = ctx.enter_context(nc.Block())

        UNITS = TILES * PAIRS

        def q_transpose(pe, t, h, par):
            if h == 0:
                pe.wait_ge(s_qn, t + 1)
            if late(t, 1):
                pe.wait_ge(s_alo, 2 * (t - 1) + h + 1)
            for j in range(4):
                pr = 4 * h + j
                src = qn[:, par, pr].rearrange("p a b -> p (a b)")
                mm = pe.transpose(bank[4 + h][:, j * P:(j + 1) * P], src, ident)
            mm.then_inc(s_tq, 1)

        def attention_tensor(pe):
            pe.wait_ge(s_const, 16)
            q_transpose(pe, 0, 0, 0)
            q_transpose(pe, 0, 1, 0)

            def step(t, k, par, last):
                u = 8 * t + k
                if not last:
                    if k == 0:
                        pe.wait_ge(s_qm, 2 * t + 2)
                    if isinstance(t, int) and t == 0 and k == 0:
                        pe.wait_ge(s_kst[0], 256)
                        pe.wait_ge(s_band, 2)
                    if late(u, 2):
                        pe.wait_ge(s_p, u - 1)
                    sp = bank[u % 2] if isinstance(u, int) else bank[k % 2]
                    if isinstance(t, int):
                        msk = band[:, t:t + 1, :].broadcast_to([P, 2, WIN])
                    else:
                        msk = band[:, bass.ds(t, 1), :].broadcast_to([P, 2, WIN])
                    pe.matmul(sp[:, :], identb[:, :], msk, start=True, stop=False, skip_group_check=True)
                    for hh in range(2):
                        ks = kst[:, k, 128 * t:128 * t + WIN] if isinstance(t, int) else kst[:, k, bass.ds(128 * t, WIN)]
                        mm = pe.matmul(sp[:, hh * WIN:(hh + 1) * WIN], qm[:, par, hh, k, :], ks,
                                       start=False, stop=True, skip_group_check=True)
                    mm.then_inc(s_s, 1)
                    if (k == 2 or k == 3) and not (isinstance(t, int) and t + 1 >= TILES):
                        q_transpose(pe, t + 1, k - 2, 1 - par)
                if late(u, 2) and not (isinstance(u, int) and u - 2 >= UNITS):
                    pe.wait_ge(s_p, u - 1)
                    if late(u, 4):
                        pe.wait_ge(s_ptl, u - 3)
                    for hh in range(2):
                        for kb in range(2):
                            mm = pe.transpose(bank[2 + k % 2][:, hh * WIN + kb * P:hh * WIN + kb * P + P],
                                              prob[:, (k + 2) % 4, hh, kb * P:(kb + 1) * P], ident)
                    mm.then_inc(s_pt, 1)
                if late(u, 3):
                    kk = (k - 3) % PAIRS
                    tt = t if k >= 3 else t - 1
                    pe.wait_ge(s_ptl, u - 2)
                    if k == 3 or k == 7:
                        if late(tt, 1):
                            pe.wait_ge(s_o, 2 * (2 * (tt - 1) + kk // 4 + 1))
                        if isinstance(t, int) and t == 0:
                            pe.wait_ge(s_fill, 2)
                            pe.wait_ge(s_vd, 2)
                    for hh in range(2):
                        head = 2 * kk + hh
                        o = bank[6 + kk // 4][:, (head % 8) * VW:(head % 8 + 1) * VW]
                        n = 0
                        for kb in range(2):
                            if isinstance(tt, int):
                                vv = v3[:, tt + kb, head, :]
                            else:
                                vv = v3[:, bass.ds(tt + kb, 1), head, :]
                            for part in (pth, ptl):
                                mm = pe.matmul(o, part[:, (k + 1) % 2, hh, kb * P:(kb + 1) * P], vv,
                                               start=(n == 0), stop=(n == 3))
                                n += 1
                    mm.then_inc(s_pv, 1)

            for t in (0, 1):
                for k in range(PAIRS):
                    step(t, k, t, False)
            for piece in range(1, KPIECES):
                pe.wait_ge(s_kst[piece], 256)
            pe.wait_ge(s_vd, 2 * len(VGROUPS))
            pe.wait_ge(s_band, 3)
            with pe.Fori(1, TILES // 2 - 1) as i:
                for par in (0, 1):
                    for k in range(PAIRS):
                        step(2 * i + par, k, par, False)
            for t in (TILES - 2, TILES - 1):
                for k in range(PAIRS):
                    step(t, k, t % 2, False)
            for k in range(3):
                step(TILES, k, 0, True)

        def q_hi(t, h):
            nc.scalar.wait_ge(s_tq, 2 * t + h + 1)
            if late(t, 1):
                nc.scalar.wait_ge(s_qm, 2 * t)
            nc.scalar.activation(qst[:, 4 * h:4 * h + 4, :], bank[4 + h][:, :].rearrange("p (a b) -> p a b", a=4),
                                 ACT.Copy).then_inc(s_ahi, 1)

        def k_hi(s):
            nc.scalar.wait_ge(s_kraw[s % 2], 16 * (s // 2 + 1))
            if s >= 2:
                nc.scalar.wait_ge(s_kst[s - 2], 256)
            nc.scalar.activation(khl[:, s % 2, 0], kraw[:, s % 2], ACT.Copy).then_inc(s_khi, 1)

        def v_part(g, j):
            a, b = VGROUPS[g]
            return v3[:, a:b, :, j * HD:(j + 1) * HD]

        def v_raw(g):
            a, b = VGROUPS[g]
            return vraw[:, g % 2, 0:b - a, :].rearrange("p t (h d) -> p t h d", h=HEADS)

        def v_act(g, j):
            if j == 0:
                nc.scalar.wait_ge(s_vraw[g % 2], 16 * (g // 2 + 1))
            else:
                nc.scalar.wait_ge(s_vd, 2 * g + 1)
            nc.scalar.activation(v_part(g, j), v_raw(g), ACT.Copy).then_inc(s_va, 1)

        def v_dve(g, j):
            nc.vector.wait_ge(s_va, 2 * g + j + 1)
            if j == 0:
                nc.vector.tensor_tensor(v_raw(g), v_raw(g), v_part(g, 0), ALU.subtract).then_inc(s_vd, 1)
            else:
                nc.vector.tensor_tensor(v_part(g, 2), v_raw(g), v_part(g, 1), ALU.subtract).then_inc(s_vd, 1)

        V_STEPS = {1: ((1, 0),), 2: ((1, 1), (2, 0)), 3: ((2, 1), (3, 0)), 4: ((3, 1),)}
        K_STEPS = {4: 1, 5: 2, 6: 3}

        def attention_scalar(act):
            k_hi(0)
            v_act(0, 0)
            act.wait_ge(s_gates, 16)
            nc.scalar.activation(tg[:, :], gates[:, :], ACT.Tanh).then_inc(s_tg, 1)
            q_hi(0, 0)
            q_hi(0, 1)
            v_act(0, 1)

            def step(t, k, last):
                u = 8 * t + k
                if late(u, 2) and not (isinstance(u, int) and u - 2 >= UNITS):
                    act.wait_ge(s_pt, u - 1)
                    if late(u, 4):
                        act.wait_ge(s_pv, u - 3)
                    nc.scalar.activation(pth[:, k % 2], bank[2 + k % 2][:, :].rearrange("p (a b) -> p a b", a=2),
                                         ACT.Copy).then_inc(s_pth, 1)
                if last:
                    return
                act.wait_ge(s_nm, u + 1)
                if late(u, 4):
                    act.wait_ge(s_pt, u - 3)
                for hh in range(2):
                    e = nc.scalar.activation(prob[:, k % 4, hh, :], bank[k % 2][:, hh * WIN:(hh + 1) * WIN], ACT.Exp,
                                             bias=nmax[:, k % 4, hh:hh + 1])
                e.then_inc(s_p, 1)
                if (k == 3 or k == 4) and not (isinstance(t, int) and t + 1 >= TILES):
                    q_hi(t + 1, k - 3)
                if isinstance(t, int) and t == 0:
                    for g, j in V_STEPS.get(k, ()):
                        v_act(g, j)
                    if k in K_STEPS:
                        k_hi(K_STEPS[k])

            for t in (0, 1):
                for k in range(PAIRS):
                    step(t, k, False)
            with act.Fori(1, TILES // 2 - 1) as i:
                for par in (0, 1):
                    for k in range(PAIRS):
                        step(2 * i + par, k, False)
            for t in (TILES - 2, TILES - 1):
                for k in range(PAIRS):
                    step(t, k, False)
            for k in range(2):
                step(TILES, k, True)

        def attention_vector(dve):
            def q_norm(t, par):
                if late(t, 2):
                    dve.wait_ge(s_tq, 2 * (t - 1))
                if isinstance(t, int):
                    xt, mean, rs = x[:, t:t + 1, :], meanvar[:, t, 0:1], rstd[:, t:t + 1]
                else:
                    xt, mean, rs = x[:, bass.ds(t, 1), :], meanvar[:, bass.ds(t, 1), 0], rstd[:, bass.ds(t, 1)]
                xt = xt.rearrange("p t (a b) -> p (t a) b", a=PAIRS).unsqueeze(2).broadcast_to([P, PAIRS, 4, 32])
                nc.vector.tensor_scalar(qn[:, par], xt, mean, rs, ALU.subtract, ALU.mult).then_inc(s_qn, 1)

            def q_lo(t, h):
                dve.wait_ge(s_ahi, 2 * t + h + 1)
                lo = qst[64:128, 4 * h:4 * h + 4, :]
                nc.vector.tensor_tensor(lo, bank[4 + h][64:128, :].rearrange("p (a b) -> p a b", a=4), f32(lo),
                                        ALU.subtract).then_inc(s_alo, 1)

            def k_lo(s):
                dve.wait_ge(s_khi, s + 1)
                nc.vector.tensor_tensor(khl[:, s % 2, 1], kraw[:, s % 2], f32(khl[:, s % 2, 0]),
                                        ALU.subtract).then_inc(s_klo, 1)

            def o_sum(t, h):
                n = 2 * t + h
                dve.wait_ge(s_pv, 8 * t + 4 * h + 4)
                if late(t, 1):
                    dve.wait_ge(s_xa, n - 1)
                ov = bank[6 + h][:, 0:8 * VW].rearrange("p (a b) -> p a b", a=8)
                nc.vector.reciprocal(rden[:, h, :], ov[:, :, 3 * HD]).then_inc(s_rr, 1)
                nc.vector.tensor_reduce(osum[:, h], ov[:, :, 0:3 * HD].rearrange("p a (c d) -> p a d c", c=3),
                                        AX_X, ALU.add).then_inc(s_o, 1)
                dve.wait_ge(s_rr, n + 1)
                nc.vector.tensor_scalar(rdeng[:, h, :], rden[:, h, :], tg[:, 0:1], None, ALU.mult).then_inc(s_o, 1)

            k_lo(0)
            v_dve(0, 0)
            ln_stats(dve, 0, 0)
            dve.wait_ge(s_lnp[0], 2)
            q_norm(0, 0)
            q_lo(0, 0)
            q_lo(0, 1)
            v_dve(0, 1)
            dve.wait_ge(s_tg, 1)

            def step(t, k, par, last):
                u = 8 * t + k
                if not last:
                    dve.wait_ge(s_s, u + 1)
                    nc.vector.tensor_reduce(nmax[:, k % 4, :], bank[k % 2][:, :].rearrange("p (a b) -> p a b", a=2),
                                            AX_X, ALU.max, negate=True).then_inc(s_nm, 1)
                    if not (isinstance(t, int) and t + 1 >= TILES):
                        if k == 0:
                            q_norm(t + 1, 1 - par)
                        if k == 4 or k == 5:
                            q_lo(t + 1, k - 4)
                    if isinstance(t, int) and t == 0:
                        for g, j in V_STEPS.get(k, ()):
                            v_dve(g, j)
                        if k in K_STEPS:
                            k_lo(K_STEPS[k])
                    if isinstance(t, int) and t == 1 and k in (1, 2, 5):
                        ln_stats(dve, 0, {1: 1, 2: 2, 5: 3}[k])
                if late(u, 2) and not (isinstance(u, int) and u - 2 >= UNITS):
                    dve.wait_ge(s_pth, u - 1)
                    nc.vector.tensor_tensor(ptl[:, k % 2], bank[2 + k % 2][:, :].rearrange("p (a b) -> p a b", a=2),
                                            pth[:, k % 2], ALU.subtract).then_inc(s_ptl, 1)
                if k == 7 and not last:
                    o_sum(t, 0)
                if k == 3 and late(t, 1):
                    o_sum(t - 1, 1)

            for t in (0, 1):
                for k in range(PAIRS):
                    step(t, k, t, False)
            dve.wait_ge(s_lnp[0], 2 * BATCH)
            with dve.Fori(1, TILES // 2 - 1) as i:
                for par in (0, 1):
                    for k in range(PAIRS):
                        step(2 * i + par, k, par, False)
            for t in (TILES - 2, TILES - 1):
                for k in range(PAIRS):
                    step(t, k, t % 2, False)
            for k in range(4):
                step(TILES, k, 0, True)

        def attention_pool(pool):
            nc.gpsimd.memset(minus_half[:, :], -0.5).then_inc(s_fill, 1)
            nc.gpsimd.memset(v3[:, :, :, 3 * HD:VW], 1.0).then_inc(s_fill, 1)

            def q_mask(t, par):
                pool.wait_ge(s_alo, 2 * t + 2)
                if late(t, 2):
                    pool.wait_ge(s_s, 8 * (t - 1))
                for hh in range(2):
                    m = head_mask[:, hh:hh + 1].unsqueeze(2).broadcast_to([P, PAIRS, P])
                    nc.gpsimd.tensor_tensor(qm[:, par, hh], f32(qst[:, :, :]), m, ALU.mult).then_inc(s_qm, 1)

            def x_update(t, h):
                n = 2 * t + h
                pool.wait_ge(s_o, 2 * n + 2)
                nc.gpsimd.tensor_tensor(oscaled[:, h], osum[:, h],
                                        rdeng[:, h, :].unsqueeze(2).broadcast_to([P, PAIRS, HD]),
                                        ALU.mult).then_inc(s_os, 1)
                pool.wait_ge(s_os, n + 1)
                if isinstance(t, int):
                    xt = x[:, t, h * P:(h + 1) * P]
                else:
                    xt = x[:, bass.ds(t, 1), h * P:(h + 1) * P]
                nc.gpsimd.tensor_tensor(xt, xt, oscaled[:, h].rearrange("p a b -> p (a b)"), ALU.add).then_inc(s_xa, 1)

            def tile(t, par):
                if late(t, 1):
                    x_update(t - 1, 1)
                if not (isinstance(t, int) and t + 1 >= TILES):
                    q_mask(t + 1, 1 - par)
                x_update(t, 0)

            def bands(b0, b1):
                nc.gpsimd.tensor_copy(band[:, TPB * b0:TPB * b1, :].rearrange("p (b t) w -> p b t w", t=TPB),
                                      band_f32.rearrange("p (t w) -> p t w", t=TPB).unsqueeze(1)
                                      .broadcast_to([P, b1 - b0, TPB, WIN])).then_inc(s_band, 1)

            pool.wait_ge(s_fill, 1)
            ln_rsqrt(pool, 0, 0)
            pool.wait_ge(s_const, 16)
            nc.gpsimd.tensor_copy(identb[:, :], ident).then_inc(s_band, 1)
            bands(0, 1)
            q_mask(0, 0)
            bands(1, BATCH)
            q_mask(1, 1)
            x_update(0, 0)
            x_update(0, 1)
            q_mask(2, 0)
            for b in (1, 2, 3):
                ln_rsqrt(pool, 0, b)
            x_update(1, 0)
            with pool.Fori(1, TILES // 2 - 1) as i:
                for par in (0, 1):
                    tile(2 * i + par, par)
            for t in (TILES - 2, TILES - 1):
                tile(t, t % 2)
            x_update(TILES - 1, 1)

        def ln_stats(dve, n, b):
            if n == 0:
                dve.wait_ge(s_x[b], 16)
            for t in range(TPB * b, TPB * b + TPB):
                op = nc.vector.bn_stats(stats[:, t, :], x[:, t, :])
            op.then_inc(s_ln[n], 1)
            dve.wait_ge(s_ln[n], 2 * b + 1)
            for t in range(TPB * b, TPB * b + TPB):
                op = nc.vector.bn_aggr(meanvar[:, t, :], stats[:, t, :])
            op.then_inc(s_ln[n], 1)

        def ln_rsqrt(pool, n, b):
            ts = slice(TPB * b, TPB * b + TPB)
            pool.wait_ge(s_ln[n], 2 * b + 2)
            nc.gpsimd.tensor_scalar(varp[:, ts], meanvar[:, ts, 1], EPS, None, ALU.add).then_inc(s_lnp[n], 1)
            pool.wait_ge(s_lnp[n], 2 * b + 1)
            nc.gpsimd.tensor_tensor(rstd[:, ts], varp[:, ts], minus_half[:, :], ALU.pow).then_inc(s_lnp[n], 1)

        def ln_norm(dve, n, b, ready):
            dve.wait_ge(s_lnp[n], 2 * b + 2)
            for t in range(TPB * b, TPB * b + TPB):
                op = nc.vector.tensor_scalar(xn[:, t, :], x[:, t, :], meanvar[:, t, 0:1], rstd[:, t:t + 1],
                                             ALU.subtract, ALU.mult)
            op.then_inc(ready, 1)

        def moe_prep_tensor(pe, L, m):
            ne = (E0, E1)[L]

            def transposes(b):
                pe.wait_ge(m.xn, b + 1)
                if b >= 2:
                    pe.wait_ge(m.xl, 2 * (b - 1))
                for c in range(CH):
                    for j in range(TPB):
                        mm = pe.transpose(bank[2 * (b % 2) + c][:, j * P:(j + 1) * P],
                                          xn[:, TPB * b + j, c * P:(c + 1) * P], ident)
                    mm.then_inc(m.tr, 1)

            def logits(b):
                pe.wait_ge(m.xl, 2 * (b + 1))
                for t in range(TPB * b, TPB * b + TPB):
                    lo = bank[4 + t // 8][:, (t % 8) * 2 * ne:(t % 8 + 1) * 2 * ne]
                    n = 0
                    for c in range(CH):
                        for part in (xh, xl):
                            mm = pe.matmul(lo, part[:, c, t * P:(t + 1) * P], rwhl[:, c, 0:2 * ne],
                                           start=(n == 0), stop=(n == 3))
                            n += 1
                mm.then_inc(m.lg, 1)

            transposes(0)
            pe.wait_ge(m.rlo, 1)
            for b in range(1, BATCH):
                transposes(b)
                logits(b - 1)
            logits(BATCH - 1)

        def moe_tensor(pe, L, m, nb):
            def gate_up(v, b, par):
                vp = b % 2
                if b == 0:
                    e1 = v // 4 + 1 if isinstance(v, int) else None
                    pe.wait_ge(m.wlo, e1 if e1 is not None else v_e[0] + 1)
                if late(v, 2):
                    pe.wait_ge(m.sil, v - 1)
                for half, ready in ((0, m.gate), (1, m.up)):
                    if half == 1 and late(v, 2):
                        pe.wait_ge(m.h, v - 1)
                    o = bank[2 * half + vp]
                    n = 0
                    for c in range(CH):
                        w = slice((CH * half + c) * FF, (CH * half + c + 1) * FF)
                        for wp, xp in ((wh, xh), (wh, xl), (wl, xh)):
                            mm = pe.matmul(o[:, :], wp[:, par, w], xp[:, c, b * SEQ:(b + 1) * SEQ],
                                           start=(n == 0), stop=(n == 5))
                            n += 1
                    mm.then_inc(ready, 1)

            def down(v, b, par):
                vp = b % 2
                if isinstance(v, int) and v == 1:
                    pe.wait_ge(m.lgl, 2)
                pe.wait_ge(m.hl, v)
                if late(v, 3):
                    pe.wait_ge(m.acc, v - 2)
                for j in range(TPB):
                    o = bank[4 + 2 * vp + j // 2][:, (j % 2) * DIM:(j % 2 + 1) * DIM]
                    n = 0
                    for hp, wp in ((hidh, wh), (hidh, wl), (hidl, wh)):
                        mm = pe.matmul(o, hp[:, vp, j * P:(j + 1) * P], wp[:, par, 2 * CH * FF:WCOLS],
                                       start=(n == 0), stop=(n == 2))
                        n += 1
                mm.then_inc(m.y, 1)

            v_e = [None]

            def body(e, par):
                v_e[0] = e
                for b in range(4):
                    gate_up(4 * e + b, b, par)
                    if late(4 * e + b, 1):
                        down(4 * e + b, (b - 1) % 4, par if b else 1 - par)

            body(0, 0)
            body(1, 1)
            with pe.Fori(1, (nb - 1) // 2) as i:
                body(2 * i, 0)
                body(2 * i + 1, 1)
            for e in range(2 * ((nb - 1) // 2), nb):
                body(e, e % 2)
            down(4 * nb, 3, (nb - 1) % 2)

        def moe_scalar(act, L, m, nb):
            def weights_hi(e, par, loaded):
                act.wait_ge(m.wload[par], loaded)
                if late(e, 2):
                    act.wait_ge(m.y, 4 * (e - 1))
                nc.scalar.activation(wh[:, par], wraw[:, par], ACT.Copy).then_inc(m.whi, 1)

            def step(v, b):
                vp = b % 2
                act.wait_ge(m.gate, v + 1)
                if late(v, 2):
                    act.wait_ge(m.h, v - 1)
                nc.scalar.activation(sil[:, vp], bank[vp][:, :], ACT.Silu).then_inc(m.sil, 1)
                act.wait_ge(m.h, v + 1)
                if late(v, 2):
                    act.wait_ge(m.y, v - 1)
                nc.scalar.activation(hidh[:, vp], hid[:, vp], ACT.Copy).then_inc(m.hh, 1)

            def body(e, par, loaded):
                for b in range(4):
                    step(4 * e + b, b)
                    if b == 2 and not (isinstance(e, int) and (e + 1 >= nb or e == 0)):
                        weights_hi(e + 1, 1 - par, loaded)

            weights_hi(0, 0, 16)
            weights_hi(1, 1, 16)
            body(0, 0, 16)
            body(1, 1, 32)
            with act.Fori(1, (nb - 1) // 2) as i:
                body(2 * i, 0, 16 * i + 16)
                body(2 * i + 1, 1, 16 * i + 32)
            for e in range(2 * ((nb - 1) // 2), nb):
                body(e, e % 2, 16 * ((e + 1) // 2 + 1))

        def moe_vector(dve, L, m, nb, routing):
            def add(v, e, b):
                vp = b % 2
                dve.wait_ge(m.y, v + 1)
                if late(v, 4):
                    dve.wait_ge(m.acc, v - 3)
                for j in range(TPB):
                    t = TPB * b + j
                    w = cw[:, t, e:e + 1] if isinstance(e, int) else cw[:, t, bass.ds(e, 1)]
                    op = nc.vector.scalar_tensor_tensor(
                        out=x[:, t, :], in0=bank[4 + 2 * vp + j // 2][:, (j % 2) * DIM:(j % 2 + 1) * DIM],
                        scalar=w, in1=x[:, t, :], op0=ALU.mult, op1=ALU.add)
                op.then_inc(m.acc, 1)

            def step(v, e, b):
                vp = b % 2
                dve.wait_ge(m.up, v + 1)
                dve.wait_ge(m.sil, v + 1)
                if late(v, 2):
                    dve.wait_ge(m.hl, v - 1)
                nc.vector.tensor_tensor(hid[:, vp], sil[:, vp], bank[2 + vp][:, :], ALU.mult).then_inc(m.h, 1)
                dve.wait_ge(m.hh, v + 1)
                nc.vector.tensor_tensor(hidl[:, vp], hid[:, vp], f32(hidh[:, vp]), ALU.subtract).then_inc(m.hl, 1)
                if late(v, 1):
                    add(v - 1, e if b else e - 1, (b - 1) % 4)

            for e in range(2):
                for b in range(4):
                    step(4 * e + b, e, b)
                    if e == 0:
                        routing[b]()
            with dve.Fori(1, (nb - 1) // 2) as i:
                for e in range(2):
                    for b in range(4):
                        step(8 * i + 4 * e + b, 2 * i + e, b)
            for e in range(2 * ((nb - 1) // 2), nb):
                for b in range(4):
                    step(4 * e + b, e, b)
            add(4 * nb - 1, nb - 1, 3)

        def moe_pool(pool, L, m, nb):
            def low(e, par):
                pool.wait_ge(m.whi, e + 1)
                nc.gpsimd.tensor_tensor(wl[:, par], wraw[:, par], f32(wh[:, par]), ALU.subtract).then_inc(m.wlo, 1)

            with pool.Fori(0, nb // 2) as i:
                for par in range(2):
                    low(2 * i + par, par)
            if nb % 2:
                low(nb - 1, 0)

        def moe_sync(sp, L, m, nb, w_in):
            wv = w_in.rearrange("e p c -> p e c")

            def load(e, par):
                if late(e, 2):
                    sp.wait_ge(m.wlo, e - 1)
                src = wv[:, e, :] if isinstance(e, int) else wv[:, bass.ds(e, 1), :]
                sp.dma_start(wraw[:, par], src).then_inc(m.wload[par], 16)

            load(0, 0)
            load(1, 1)
            with sp.Fori(1, nb // 2) as i:
                load(2 * i, 0)
                load(2 * i + 1, 1)
            if nb % 2:
                load(nb - 1, 0)

        def moe_prep_vector(dve, L, m):
            n = 1 + 2 * L
            ne = (E0, E1)[L]
            ln_stats(dve, n, 0)
            ln_stats(dve, n, 1)
            ln_norm(dve, n, 0, m.xn)
            dve.wait_ge(m.rhi, 1)
            nc.vector.tensor_tensor(rwhl[:, :, ne:2 * ne], rraw[:, :, 0:ne], f32(rwhl[:, :, 0:ne]),
                                    ALU.subtract).then_inc(m.rlo, 1)
            for b in range(BATCH):
                if b + 2 < BATCH:
                    ln_stats(dve, n, b + 2)
                if b + 1 < BATCH:
                    ln_norm(dve, n, b + 1, m.xn)
                for c in range(CH):
                    dve.wait_ge(m.xh, 2 * b + c + 1)
                    cols = slice(b * SEQ, (b + 1) * SEQ)
                    nc.vector.tensor_tensor(xl[:, c, cols], bank[2 * (b % 2) + c][:, :], f32(xh[:, c, cols]),
                                            ALU.subtract).then_inc(m.xl, 1)

        def moe_prep_scalar(act, L, m):
            ne = (E0, E1)[L]
            act.wait_ge(m.rload, 16 + 16 * L)
            nc.scalar.activation(rwhl[:, :, 0:ne], rraw[:, :, 0:ne], ACT.Copy).then_inc(m.rhi, 1)
            for b in range(BATCH):
                for c in range(CH):
                    act.wait_ge(m.tr, 2 * b + c + 1)
                    nc.scalar.activation(xh[:, c, b * SEQ:(b + 1) * SEQ], bank[2 * (b % 2) + c][:, :],
                                         ACT.Copy).then_inc(m.xh, 1)
            act.wait_ge(m.lg, BATCH)
            for h in range(2):
                lv = bank[4 + h][:, 0:8 * 2 * ne].rearrange("p (t e) -> p t e", t=8)
                op = nc.scalar.activation(lgl[:, 8 * h:8 * h + 8, 0:ne], lv[:, :, ne:2 * ne], ACT.Copy)
                if h == 1:
                    op.then_inc(m.lgl, 1)

        class Chain:

            def __init__(self, eng, s):
                self.eng, self.s, self.n = eng, s, 0

            def __call__(self, op):
                op.then_inc(self.s, 1)
                self.n += 1
                self.eng.wait_ge(self.s, self.n)

        def ranks(link, vals):
            for g in range(8):
                nc.vector.memset(rank[:, :, g:g + 1], float(7 - g)) if g < 7 else link(
                    nc.vector.memset(rank[:, :, g:g + 1], 0.0))
            for k in range(1, 8):
                w = 8 - k
                link(nc.vector.tensor_tensor(cmp[:, :, 0:w], vals[:, :, 0:w], vals[:, :, k:8], ALU.is_ge))
                link(nc.vector.tensor_tensor(rank[:, :, k:8], rank[:, :, k:8], cmp[:, :, 0:w], ALU.add))
                link(nc.vector.tensor_tensor(rank[:, :, 0:w], rank[:, :, 0:w], cmp[:, :, 0:w], ALU.subtract))

        def logits_sum(dve, link, m, ne):
            dve.wait_ge(m.lgl, 1)
            for h in range(2):
                lv = bank[4 + h][:, 0:8 * 2 * ne].rearrange("p (t e) -> p t e", t=8)
                op = nc.vector.tensor_tensor(lg[:, 8 * h:8 * h + 8, 0:ne], lv[:, :, 0:ne],
                                             lgl[:, 8 * h:8 * h + 8, 0:ne], ALU.add)
            op.then_inc(m.lgl, 1)
            dve.wait_ge(m.lgl, 2)

        def over_experts(v, n):
            return v.unsqueeze(2).broadcast_to([P, TILES, n])

        def route0_vector(dve, m):
            link = Chain(dve, m.rs)
            sg = sc[:, :, :].rearrange("p t (g k) -> p t g k", g=GROUPS0)
            logits_sum(dve, link, m, E0)
            link(nc.vector.memset(cw[:, :, 0:SH0], 1.0))
            link(nc.vector.tensor_scalar(cw[:, :, 0:SH0], cw[:, :, 0:SH0], tg[:, 2:3], None, ALU.mult))

            def groups():
                dve.wait_ge(m.ra, 1)
                link(nc.vector.tensor_reduce(gs[:, :, :], sg, AX_X, ALU.add))
                ranks(link, gs)

            def candidates():
                link(nc.vector.tensor_scalar(cmp[:, :, :], rank[:, :, :], float(TOPG0) - 0.5, None, ALU.is_lt))
                link(nc.vector.tensor_tensor(msc[:, :, :].rearrange("p t (g k) -> p t g k", g=GROUPS0), sg,
                                             cmp[:, :, :].unsqueeze(3).broadcast_to([P, TILES, GROUPS0, E0 // GROUPS0]),
                                             ALU.mult))
                for t in range(TILES):
                    op = nc.vector.max(top8[:, t, :], msc[:, t, :])
                link(op)

            def chosen():
                for t in range(TILES):
                    op = nc.vector.match_replace(out=rep[:, t, :], in_to_replace=top8[:, t, :], in_values=msc[:, t, :],
                                                 imm_value=-1.0)
                link(op)
                link(nc.vector.tensor_tensor(selw[:, :, :], rep[:, :, :], msc[:, :, :], ALU.not_equal))

            def weights():
                link(nc.vector.tensor_tensor(selw[:, :, :], selw[:, :, :], msc[:, :, :], ALU.mult))
                link(nc.vector.tensor_reduce(rsum[:, :], selw[:, :, :], AX_X, ALU.add))
                link(nc.vector.tensor_scalar(rsum[:, :], rsum[:, :], 1e-12, None, ALU.max))
                link(nc.vector.reciprocal(rrec[:, :], rsum[:, :]))
                link(nc.vector.tensor_scalar(rrec[:, :], rrec[:, :], tg[:, 2:3], None, ALU.mult))
                link(nc.vector.tensor_tensor(cw[:, :, SH0:NB0], selw[:, :, :], over_experts(rrec[:, :], E0), ALU.mult))

            return groups, candidates, chosen, weights

        def route0_scalar(act, m):
            act.wait_ge(m.lgl, 2)
            nc.scalar.activation(sc[:, :, :], lg[:, :, :], ACT.Sigmoid).then_inc(m.ra, 1)

        def route1_vector(dve, m):
            link = Chain(dve, m.rs)
            logits_sum(dve, link, m, E1)
            link(nc.vector.tensor_reduce(rmx[:, :], lg[:, :, 0:E1], AX_X, ALU.max))
            link(nc.vector.tensor_tensor(msc[:, :, 0:E1], lg[:, :, 0:E1], over_experts(rmx[:, :], E1), ALU.subtract))
            link(nc.vector.memset(cw[:, :, 0:SH1], 1.0))
            link(nc.vector.tensor_scalar(cw[:, :, 0:SH1], cw[:, :, 0:SH1], tg[:, 3:4], None, ALU.mult))

            def softmax():
                dve.wait_ge(m.ra, 1)
                link(nc.vector.tensor_reduce(rsum[:, :], rep[:, :, 0:E1], AX_X, ALU.add))
                link(nc.vector.reciprocal(rrec[:, :], rsum[:, :]))
                link(nc.vector.tensor_tensor(sc[:, :, 0:E1], rep[:, :, 0:E1], over_experts(rrec[:, :], E1), ALU.mult))
                link(nc.vector.tensor_tensor(gs[:, :, :], sc[:, :, 0:E1],
                                             rbias[:, :].unsqueeze(1).broadcast_to([P, TILES, E1]), ALU.add))

            def order():
                ranks(link, gs)

            def weights():
                link(nc.vector.tensor_scalar(cmp[:, :, :], rank[:, :, :], float(TOP1) - 0.5, None, ALU.is_lt))
                link(nc.vector.tensor_tensor(selw[:, :, 0:E1], cmp[:, :, :], sc[:, :, 0:E1], ALU.mult))
                link(nc.vector.tensor_scalar(selw[:, :, 0:E1], selw[:, :, 0:E1], tg[:, 3:4], None, ALU.mult))

            def spread():
                link(nc.vector.tensor_copy(cw[:, :, SH1:NB1].rearrange("p t (e k) -> p t e k", k=2),
                                           selw[:, :, 0:E1].unsqueeze(3).broadcast_to([P, TILES, E1, 2])))

            return softmax, order, weights, spread

        def route1_scalar(act, m):
            act.wait_ge(m.rs, 2)
            nc.scalar.activation(rep[:, :, 0:E1], msc[:, :, 0:E1], ACT.Exp).then_inc(m.ra, 1)

        A = s_a1

        def sync_a1(sp):
            sp.wait_ge(moe[0].acc, 4 * NB0)
            for b in range(BATCH):
                if b:
                    sp.wait_ge(A["clo"], b)
                sp.dma_start(craw[:, :, :], ctxt_in[:, :, b * SEQ:(b + 1) * SEQ]).then_inc(A["ctx_t"], 16)
                if b:
                    sp.wait_ge(A["tlo"], b)
                sp.dma_start(traw[:, :, :], ctx_in[:, b * TPB:(b + 1) * TPB, :]).then_inc(A["ctx"], 16)
                if b == 0:
                    sp.dma_start(wsim[:, :, :], wsim_in).then_inc(A["par"], 16)
                    sp.dma_start(w1row[:, :], w1row_in.broadcast_to([P, DIM])).then_inc(A["par"], 16)
                    sp.dma_start(bsim[:, :], bsim_in.broadcast_to([P, 1])).then_inc(A["par"], 16)
                    sp.dma_start(bqv[:, :], bqv_in.broadcast_to([P, DIM])).then_inc(A["par"], 16)
                    sp.dma_start(wqv[:, :, :], wqv_in).then_inc(A["wq"], 16)

        def tensor_a1(pe):
            def transposes(b):
                pe.wait_ge(A["xn"], b + 1)
                if b >= 1:
                    pe.wait_ge(A["a"], 2 * b)
                if b >= 2:
                    pe.wait_ge(A["hbc"], b - 1)
                for c in range(CH):
                    for j in range(TPB):
                        mm = pe.transpose(bank[2 + c][:, j * P:(j + 1) * P], xn[:, TPB * b + j, c * P:(c + 1) * P],
                                          ident)
                    mm.then_inc(A["tr"], 1)

            def scores(b):
                pe.wait_ge(A["alo"], b + 1)
                pe.wait_ge(A["clo"], b + 1)
                for j in range(TPB):
                    if 4 * b + j >= 2:
                        pe.wait_ge(A["p"], 4 * b + j - 1)
                    k = 0
                    for c in range(CH):
                        for ap_, cp in ((aench, ctxh), (aench, ctxl), (aencl, ctxh)):
                            mm = pe.matmul(bank[j % 2][:, :], ap_[:, c, j * P:(j + 1) * P], cp[:, c, :],
                                           start=(k == 0), stop=(k == 5))
                            k += 1
                    mm.then_inc(A["sim"], 1)

            def probs_transposed(b):
                pe.wait_ge(A["pn"], 4 * b + 4)
                for jc in range(TPB):
                    if jc >= 2:
                        pe.wait_ge(A["ptl"], 4 * b + jc - 1)
                    elif b:
                        pe.wait_ge(A["x"], 4 * b)
                    for j in range(TPB):
                        mm = pe.transpose(bank[4 + jc % 2][:, j * P:(j + 1) * P], prob1[:, j, jc * P:(jc + 1) * P],
                                          ident)
                    mm.then_inc(A["pt"], 1)

            def context_bar(b):
                pe.wait_ge(A["batt"], b + 1)
                if b + 1 < BATCH:
                    pe.wait_ge(A["a"], 2 * b + 4)
                for c in range(CH):
                    for j in range(TPB):
                        mm = pe.matmul(bank[2][:, c:c + 1], xn[:, TPB * b + j, c * P:(c + 1) * P], batt[:, j:j + 1],
                                       start=(j == 0), stop=(j == TPB - 1))
                mm.then_inc(A["hb"], 1)

            def attended(b):
                pe.wait_ge(A["tlo"], b + 1)
                if b:
                    pe.wait_ge(A["prod"], 2 * b)
                for c in range(CH):
                    k = 0
                    for jc in range(TPB):
                        if c == 0:
                            pe.wait_ge(A["ptl"], 4 * b + jc + 1)
                        for tp, pp in ((tokh, p1th), (tokh, p1tl), (tokl, p1th)):
                            mm = pe.matmul(bank[6 + c][:, :], tp[:, jc, c * P:(c + 1) * P], pp[:, jc, :],
                                           start=(k == 0), stop=(k == 11))
                            k += 1
                    mm.then_inc(A["hq"], 1)

            def output(b):
                pe.wait_ge(A["elo"], b + 1)
                pe.wait_ge(A["wlo"], b + 1)
                for j0 in (0, 2):
                    for g, (fh, fl) in enumerate(((ench[:, b % 2], encl[:, b % 2]), (hqh, hql), (prodh, prodl))):
                        if g and j0 == 0:
                            pe.wait_ge(A["hql" if g == 1 else "prl"], 2 * b + 2)
                        for j in (j0, j0 + 1):
                            if g == 0 and j0:
                                pe.wait_ge(A["x"], 4 * b + j - 1)
                            k = 0
                            for c in range(CH):
                                for fp, wp in ((fh, wqh), (fh, wql), (fl, wqh)):
                                    mm = pe.matmul(bank[4 + j % 2][:, 0:DIM], fp[:, c, j * P:(j + 1) * P],
                                                   wp[:, CH * g + c, :], start=(g == 0 and k == 0),
                                                   stop=(g == 2 and k == 5))
                                    k += 1
                            if g == 2:
                                mm.then_inc(A["o"], 1)

            transposes(0)
            scores(0)
            for b in range(BATCH):
                if b + 1 < BATCH:
                    transposes(b + 1)
                probs_transposed(b)
                if b + 1 < BATCH:
                    scores(b + 1)
                context_bar(b)
                attended(b)
                output(b)

        def scalar_a1(act):
            def encoder(b):
                if b >= 2:
                    act.wait_ge(A["o"], 4 * (b - 1))
                    act.wait_ge(A["prod"], 2 * (b - 1))
                for c in range(CH):
                    act.wait_ge(A["tr"], 2 * b + c + 1)
                    nc.scalar.activation(ench[:, b % 2, c, :], bank[2 + c][:, :], ACT.Copy).then_inc(A["ehi"], 1)
                    nc.scalar.activation(enc[:, b % 2, c, :], bank[2 + c][:, :], ACT.Copy).then_inc(A["enc"], 1)
                if b:
                    act.wait_ge(A["sim"], 4 * b)
                for c in range(CH):
                    act.wait_ge(A["a"], 2 * b + c + 1)
                    nc.scalar.activation(aench[:, c, :], aenc[:, c, :], ACT.Copy).then_inc(A["ahi"], 1)

            def context(b):
                act.wait_ge(A["ctx_t"], 16 * b + 16)
                if b:
                    act.wait_ge(A["sim"], 4 * b)
                nc.scalar.activation(ctxh[:, :, :], craw[:, :, :], ACT.Copy).then_inc(A["chi"], 1)

            def tokens(b):
                act.wait_ge(A["ctx"], 16 * b + 16)
                if b:
                    act.wait_ge(A["hq"], 2 * b)
                nc.scalar.activation(tokh[:, :, :], traw[:, :, :], ACT.Copy).then_inc(A["thi"], 1)

            def softmax(b):
                if b:
                    act.wait_ge(A["pt"], 4 * b)
                for j in range(TPB):
                    act.wait_ge(A["nm"], 4 * b + j + 1)
                    nc.scalar.activation(prob1[:, j, :], bank[j % 2][:, :], ACT.Exp, bias=nm1[:, j:j + 1],
                                         accum_out=den1[:, j:j + 1]).then_inc(A["p"], 1)
                act.wait_ge(A["ngmx"], b + 1)
                nc.scalar.activation(eb[:, :], msim[:, :], ACT.Exp, bias=ngmx1[:, :],
                                     accum_out=ebs[:, :]).then_inc(A["eb"], 1)

            def probs_high(b):
                if b:
                    act.wait_ge(A["hq"], 2 * b)
                for jc in range(TPB):
                    act.wait_ge(A["pt"], 4 * b + jc + 1)
                    nc.scalar.activation(p1th[:, jc, :], bank[4 + jc % 2][:, :], ACT.Copy).then_inc(A["pth"], 1)

            def features(b):
                act.wait_ge(A["w14"], b + 1)
                if b:
                    act.wait_ge(A["o"], 4 * b)
                nc.scalar.activation(wqh[:, 0:CH, :], w14[:, :, :], ACT.Copy).then_inc(A["whi"], 1)
                for c in range(CH):
                    act.wait_ge(A["hq"], 2 * b + c + 1)
                    nc.scalar.activation(hqh[:, c, :], bank[6 + c][:, :], ACT.Copy).then_inc(A["hqh"], 1)
                for c in range(CH):
                    act.wait_ge(A["prod"], 2 * b + c + 1)
                    nc.scalar.activation(prodh[:, c, :], prod[:, c, :], ACT.Copy).then_inc(A["prh"], 1)

            context(0)
            encoder(0)
            tokens(0)
            act.wait_ge(A["wq"], 16)
            nc.scalar.activation(wqh[:, CH:3 * CH, :], wqv[:, CH:3 * CH, :], ACT.Copy).then_inc(A["wqs"], 1)
            softmax(0)
            for b in range(BATCH):
                if b + 1 < BATCH:
                    encoder(b + 1)
                    context(b + 1)
                probs_high(b)
                if b + 1 < BATCH:
                    softmax(b + 1)
                features(b)
                if b + 1 < BATCH:
                    tokens(b + 1)

        def vector_a1(dve):
            def row_terms(b):
                if b:
                    dve.wait_ge(A["msim"], b)
                for j in range(TPB):
                    if 4 * b + j:
                        dve.wait_ge(A["r"], 4 * b + j)
                    nc.vector.tensor_tensor_reduce(out=junk[:, :], in0=xn[:, TPB * b + j, :], in1=w1row[:, :], scale=1.0,
                                                   scalar=bsim[:, 0:1], op0=ALU.mult, op1=ALU.add,
                                                   accum_out=rterm[:, j:j + 1]).then_inc(A["r"], 1)

            def encoder(b):
                if b:
                    dve.wait_ge(A["alo"], b)
                for c in range(CH):
                    dve.wait_ge(A["enc"], 2 * b + c + 1)
                    nc.vector.tensor_scalar(aenc[:, c, :], bank[2 + c][:, :], wsim[:, 1, c:c + 1], wsim[:, 0, c:c + 1],
                                            ALU.mult, ALU.add).then_inc(A["a"], 1)
                dve.wait_ge(A["ahi"], 2 * b + 2)
                nc.vector.tensor_tensor(aencl[:, :, :], aenc[:, :, :], f32(aench[:, :, :]),
                                        ALU.subtract).then_inc(A["alo"], 1)

            def maxima(b):
                for j in range(TPB):
                    dve.wait_ge(A["sim"], 4 * b + j + 1)
                    nc.vector.tensor_reduce(nm1[:, j:j + 1], bank[j % 2][:, :], AX_X, ALU.max,
                                            negate=True).then_inc(A["nm"], 1)
                dve.wait_ge(A["nm"], 4 * b + 4)
                dve.wait_ge(A["r"], 4 * b + 4)
                if b:
                    dve.wait_ge(A["eb"], b)
                nc.vector.tensor_tensor(msim[:, :], rterm[:, :], nm1[:, :], ALU.subtract).then_inc(A["msim"], 1)
                dve.wait_ge(A["msim"], b + 1)
                nc.vector.tensor_reduce(mx1[:, :], msim[:, :], AX_X, ALU.max).then_inc(A["mx"], 1)

            def normalised(b):
                for j in range(TPB):
                    dve.wait_ge(A["p"], 4 * b + j + 1)
                    nc.vector.reciprocal(rd1[:, j:j + 1], den1[:, j:j + 1]).then_inc(A["rd"], 1)
                    dve.wait_ge(A["rd"], 4 * b + j + 1)
                    nc.vector.tensor_scalar(prob1[:, j, :], prob1[:, j, :], rd1[:, j:j + 1], None,
                                            ALU.mult).then_inc(A["pn"], 1)
                dve.wait_ge(A["gmx"], b + 1)
                nc.vector.tensor_scalar(ngmx1[:, :], gmx1[:, :], -1.0, None, ALU.mult).then_inc(A["ngmx"], 1)

            def row_softmax(b):
                dve.wait_ge(A["ebt"], b + 1)
                nc.vector.reciprocal(ebr[:, :], ebt[:, :]).then_inc(A["ebr"], 1)
                dve.wait_ge(A["ebr"], b + 1)
                nc.vector.tensor_scalar(batt[:, :], eb[:, :], ebr[:, 0:1], None, ALU.mult).then_inc(A["batt"], 1)

            def probs_low(b):
                for jc in range(TPB):
                    dve.wait_ge(A["pth"], 4 * b + jc + 1)
                    nc.vector.tensor_tensor(p1tl[:, jc, :], bank[4 + jc % 2][:, :], f32(p1th[:, jc, :]),
                                            ALU.subtract).then_inc(A["ptl"], 1)

            def features(b):
                dve.wait_ge(A["hb"], b + 1)
                nc.vector.tensor_copy(hbar[:, :], bank[2][:, 0:CH]).then_inc(A["hbc"], 1)
                dve.wait_ge(A["hbc"], b + 1)
                for c in range(CH):
                    op = nc.vector.scalar_tensor_tensor(out=w14[:, c, :], in0=wqv[:, 3 * CH + c, :], scalar=hbar[:, c:c + 1],
                                                        in1=wqv[:, c, :], op0=ALU.mult, op1=ALU.add)
                op.then_inc(A["w14"], 1)
                dve.wait_ge(A["whi"], b + 1)
                nc.vector.tensor_tensor(wql[:, 0:CH, :], w14[:, :, :], f32(wqh[:, 0:CH, :]),
                                        ALU.subtract).then_inc(A["wlo"], 1)
                for c in range(CH):
                    dve.wait_ge(A["hqh"], 2 * b + c + 1)
                    nc.vector.tensor_tensor(prod[:, c, :], enc[:, b % 2, c, :], bank[6 + c][:, :],
                                            ALU.mult).then_inc(A["prod"], 1)
                    nc.vector.tensor_tensor(hql[:, c, :], bank[6 + c][:, :], f32(hqh[:, c, :]),
                                            ALU.subtract).then_inc(A["hql"], 1)
                for c in range(CH):
                    dve.wait_ge(A["prh"], 2 * b + c + 1)
                    nc.vector.tensor_tensor(prodl[:, c, :], prod[:, c, :], f32(prodh[:, c, :]),
                                            ALU.subtract).then_inc(A["prl"], 1)

            def residual(b):
                dve.wait_ge(A["xb"], TPB * (b + 1))
                for j in range(TPB):
                    t = TPB * b + j
                    dve.wait_ge(A["o"], t + 1)
                    nc.vector.scalar_tensor_tensor(out=x[:, t, :], in0=bank[4 + j % 2][:, 0:DIM], scalar=tg[:, 1:2],
                                                   in1=x[:, t, :], op0=ALU.mult, op1=ALU.add).then_inc(A["x"], 1)

            ln_stats(dve, 2, 0)
            ln_stats(dve, 2, 1)
            ln_norm(dve, 2, 0, A["xn"])
            dve.wait_ge(A["par"], 64)
            nc.vector.tensor_scalar(bqvg[:, :], bqv[:, :], tg[:, 1:2], None, ALU.mult).then_inc(A["bq"], 1)
            encoder(0)
            dve.wait_ge(A["xn"], 1)
            row_terms(0)
            ln_norm(dve, 2, 1, A["xn"])
            maxima(0)
            normalised(0)
            dve.wait_ge(A["wqs"], 1)
            nc.vector.tensor_tensor(wql[:, CH:3 * CH, :], wqv[:, CH:3 * CH, :], f32(wqh[:, CH:3 * CH, :]),
                                    ALU.subtract).then_inc(A["wq2"], 1)
            row_softmax(0)
            for b in range(BATCH):
                if b + 1 < BATCH:
                    encoder(b + 1)
                    dve.wait_ge(A["xn"], b + 2)
                    row_terms(b + 1)
                probs_low(b)
                if b + 2 < BATCH:
                    ln_stats(dve, 2, b + 2)
                if b + 1 < BATCH:
                    maxima(b + 1)
                    normalised(b + 1)
                features(b)
                if b + 1 < BATCH:
                    row_softmax(b + 1)
                if b + 2 < BATCH:
                    ln_norm(dve, 2, b + 2, A["xn"])
                residual(b)

        def pool_a1(pool):
            def low_parts(b):
                pool.wait_ge(A["chi"], b + 1)
                nc.gpsimd.tensor_tensor(ctxl[:, :, :], craw[:, :, :], f32(ctxh[:, :, :]), ALU.subtract).then_inc(A["clo"], 1)
                pool.wait_ge(A["enc"], 2 * b + 2)
                nc.gpsimd.tensor_tensor(encl[:, b % 2], enc[:, b % 2], f32(ench[:, b % 2]),
                                        ALU.subtract).then_inc(A["elo"], 1)

            def token_low(b):
                pool.wait_ge(A["thi"], b + 1)
                nc.gpsimd.tensor_tensor(tokl[:, :, :], traw[:, :, :], f32(tokh[:, :, :]), ALU.subtract).then_inc(A["tlo"], 1)

            def add_bias(b):
                pool.wait_ge(A["xn"], b + 1)
                for t in range(TPB * b, TPB * b + TPB):
                    nc.gpsimd.tensor_tensor(x[:, t, :], x[:, t, :], bqvg[:, :], ALU.add).then_inc(A["xb"], 1)

            def row_sums(b):
                pool.wait_ge(A["mx"], b + 1)
                nc.gpsimd.partition_all_reduce(gmx1[:, :], mx1[:, :], P, RMAX).then_inc(A["gmx"], 1)
                pool.wait_ge(A["eb"], b + 1)
                nc.gpsimd.partition_all_reduce(ebt[:, :], ebs[:, :], P, RADD).then_inc(A["ebt"], 1)

            ln_rsqrt(pool, 2, 0)
            ln_rsqrt(pool, 2, 1)
            low_parts(0)
            pool.wait_ge(A["bq"], 1)
            add_bias(0)
            row_sums(0)
            token_low(0)
            for b in range(BATCH):
                if b + 1 < BATCH:
                    low_parts(b + 1)
                    add_bias(b + 1)
                if b + 2 < BATCH:
                    ln_rsqrt(pool, 2, b + 2)
                if b + 1 < BATCH:
                    row_sums(b + 1)
                    token_low(b + 1)

        @block.sync
        def _(sp):
            def load_keys(s):
                if s >= 2:
                    sp.wait_ge(s_klo, s - 1)
                sp.dma_start(kraw[:, s % 2], kt_in[:, :, s * KPC:(s + 1) * KPC]).then_inc(s_kraw[s % 2], 16)

            def load_values(g):
                if g >= 2:
                    sp.wait_ge(s_vd, 2 * g - 2)
                a, b = VGROUPS[g]
                sp.dma_start(vraw[:, g % 2, 0:b - a, :], v_in[:, a:b, :]).then_inc(s_vraw[g % 2], 16)

            def load_x(b):
                sp.dma_start(x[:, b * TPB:(b + 1) * TPB, :], x_in[:, b * TPB:(b + 1) * TPB, :]).then_inc(s_x[b], 16)

            def stack_keys(s):
                sp.wait_ge(s_klo, s + 1)
                for r, part in enumerate((0, 1, 1, 0)):
                    for g in range(4):
                        sp.dma_start(kst[32 * r:32 * r + 32, 2 * g:2 * g + 2, s * KPC:(s + 1) * KPC].bitcast(F32),
                                     khl[32 * g:32 * g + 32, s % 2, part].bitcast(F32)).then_inc(s_kst[s], 16)

            load_x(0)
            load_keys(0)
            sp.dma_start(consts[:, :], consts_in).then_inc(s_const, 16)
            sp.dma_start(gates[:, :], gates_in.broadcast_to([P, 4])).then_inc(s_gates, 16)
            load_values(0)
            stack_keys(0)
            load_x(1)
            load_keys(1)
            load_values(1)
            load_x(2)
            load_x(3)
            load_values(2)
            load_values(3)
            load_keys(2)
            for s in range(1, KPIECES):
                stack_keys(s)
                if s == 1:
                    load_keys(3)
            for L, (nb, w_in, rw_in) in enumerate(((NB0, w0_in, rw0_in), (NB1, w1_in, rw1_in))):
                m = moe[L]
                if L == 0:
                    sp.wait_ge(s_xa, 2 * TILES)
                    sp.wait_ge(s_pv, UNITS)
                    sp.dma_start(rraw[:, :, :], rw_in).then_inc(m.rload, 16)
                else:
                    sp.wait_ge(A["x"], TILES)
                    sp.dma_start(rraw[:, :, 0:E1], rw_in).then_inc(m.rload, 16)
                    sp.dma_start(rbias[:, :], rbias1_in.broadcast_to([P, E1])).then_inc(m.rload, 16)
                moe_sync(sp, L, m, nb, w_in)
                if L == 0:
                    sync_a1(sp)
            for b in range(BATCH):
                sp.wait_ge(moe[1].acc, 4 * (NB1 - 1) + b + 1)
                sp.dma_start(out[:, b * TPB:(b + 1) * TPB, :], x[:, b * TPB:(b + 1) * TPB, :]).then_inc(s_out, 16)
            sp.wait_ge(s_out, 16 * BATCH)

        @block.tensor
        def _(pe):
            attention_tensor(pe)
            moe_prep_tensor(pe, 0, moe[0])
            moe_tensor(pe, 0, moe[0], NB0)
            tensor_a1(pe)
            moe_prep_tensor(pe, 1, moe[1])
            moe_tensor(pe, 1, moe[1], NB1)

        @block.scalar
        def _(act):
            attention_scalar(act)
            moe_prep_scalar(act, 0, moe[0])
            route0_scalar(act, moe[0])
            moe_scalar(act, 0, moe[0], NB0)
            scalar_a1(act)
            moe_prep_scalar(act, 1, moe[1])
            route1_scalar(act, moe[1])
            moe_scalar(act, 1, moe[1], NB1)

        @block.vector
        def _(dve):
            attention_vector(dve)
            dve.wait_ge(s_xa, 2 * TILES)
            moe_prep_vector(dve, 0, moe[0])
            moe_vector(dve, 0, moe[0], NB0, route0_vector(dve, moe[0]))
            dve.wait_ge(moe[0].acc, 4 * NB0)
            vector_a1(dve)
            dve.wait_ge(A["x"], TILES)
            moe_prep_vector(dve, 1, moe[1])
            moe_vector(dve, 1, moe[1], NB1, route1_vector(dve, moe[1]))

        @block.gpsimd
        def _(pool):
            attention_pool(pool)
            for L, m, nb in ((0, moe[0], NB0), (1, moe[1], NB1)):
                if L == 1:
                    pool_a1(pool)
                for b in range(BATCH):
                    ln_rsqrt(pool, 1 + 2 * L, b)
                moe_pool(pool, L, m, nb)


def _weights(gate, up, down):
    import numpy as np

    def cols(w):
        return w.T.reshape(CH, P, FF).transpose(1, 0, 2).reshape(P, CH * FF)
    return [np.concatenate([cols(gate[s:s + FF]), cols(up[s:s + FF]), down[:, s:s + FF].T], axis=1)
            for s in range(0, gate.shape[0], FF)]


def kernel(**inputs):
    import numpy as np
    import concourse.bacc as bacc
    from concourse import mybir as mb
    from concourse.bass_utils import run_bass_kernel_spmd as run

    a = {k: np.asarray(v) for k, v in inputs.items()}
    f = np.float32

    def by_tile(v):
        return v.reshape(-1, P, DIM).transpose(1, 0, 2)

    def by_chunk(w):
        return w.reshape(-1, P, w.shape[1]).transpose(1, 0, 2)

    tokens = a["ctx_1024"].reshape(TOKENS, DIM)
    padded = np.pad(tokens, ((BAND, BAND), (0, 0)))
    kt = padded.T.reshape(4, 2, 32, KCOLS).transpose(0, 2, 1, 3).reshape(P, 2, KCOLS)
    rows, keys = np.arange(P)[:, None], np.arange(WIN)[None, :]
    band = np.abs(keys - BAND - rows) <= BAND
    masks = [band & ~((j == 0) & (keys < BAND)) & ~((j == TPB - 1) & (keys >= P + BAND)) for j in range(TPB)]
    head = np.stack([(np.arange(P) % 32) < 16, (np.arange(P) % 32) >= 16], 1)
    consts = np.concatenate([np.eye(P), head] + [np.where(m, 0.0, MASKED) for m in masks], 1).astype(f)
    w0 = np.stack(sum([_weights(a["L0_ffn_expert_gate"][e], a["L0_ffn_expert_up"][e], a["L0_ffn_expert_down"][e])
                       for e in range(E0)],
                      _weights(a["L0_ffn_shared_gate_w"], a["L0_ffn_shared_up_w"], a["L0_ffn_shared_down_w"])))
    w1 = np.stack(sum([_weights(a["L1_ffn_w1"][e], a["L1_ffn_w3"][e], a["L1_ffn_w2"][e]) for e in range(E1)],
                      _weights(a["L1_ffn_sw1"], a["L1_ffn_sw3"], a["L1_ffn_sw2"])))
    wsim = a["L1_xattn_w_sim"].reshape(3, CH, P).transpose(2, 0, 1)[:, 1:3]
    arrays = {
        "x": by_tile(a["x"]), "kt": kt, "v": by_tile(padded), "ctx": by_tile(tokens), "ctxt": by_chunk(tokens.T),
        "consts": consts, "gates": np.concatenate([a["g_xattn"], a["g_ffn"]])[None],
        "rw0": by_chunk(a["L0_ffn_gate_w"].T), "w0": w0, "wsim": wsim, "w1row": a["L1_xattn_w_sim"][None, 0:DIM],
        "bsim": a["L1_xattn_b_sim"][None], "wqv": by_chunk(a["L1_xattn_W_qv"]), "bqv": a["L1_xattn_b_qv"][None],
        "rw1": by_chunk(a["L1_ffn_gate_w"].T), "rbias1": a["L1_ffn_gate_bias"][None], "w1": w1,
    }
    arrays = {f"in_{k}": np.ascontiguousarray(v) for k, v in arrays.items()}
    nc = bacc.Bacc("TRN2", target_bir_lowering=False, num_devices=1)
    args = [nc.dram_tensor(k, v.shape, mb.dt.from_np(v.dtype), kind="ExternalInput").ap() for k, v in arrays.items()]
    args.append(nc.dram_tensor("out", (P, TILES, DIM), mb.dt.float32, kind="ExternalOutput").ap())
    gated_xattn_moe_kernel(nc, *args)
    r = run(nc, [arrays], core_ids=[0])
    return np.asarray(r.results[0]["out"]).transpose(1, 0, 2).reshape(BATCH, SEQ, DIM)
```

```python
from contextlib import ExitStack

import concourse.bass as bass
from concourse import mybir

P = 128
BATCH, SEQ, DIM = 4, 512, 256
TOKENS = BATCH * SEQ
TILES = TOKENS // P
TPB = SEQ // P
CH = DIM // P
HEADS, HD = 16, 16
PAIRS = HEADS // 2
BAND = 64
WIN = P + 2 * BAND
KCOLS = TOKENS + 2 * BAND
KPIECES = ((0, P + WIN), (P + WIN, P + WIN + 896), (P + WIN + 896, KCOLS))
VGROUPS = ((0, 5), (5, 9), (9, 13), (13, 17))
VTILES = TILES + 1
VW = 3 * HD + 1
MASKED = -1e9
BIG = 3e38
EPS = 1e-5
FF = 128
WCOLS = 2 * CH * FF + DIM
E0, TOP0, GROUPS0, TOPG0 = 32, 8, 8, 4
E1, TOP1 = 8, 2
SH0, SH1 = 1, 4
NB0 = SH0 + E0
NB1 = SH1 + 2 * E1

ALU = mybir.AluOpType
ACT = mybir.ActivationFunctionType
AX_X = mybir.AxisListType.X
F32 = mybir.dt.float32
F32R = mybir.dt.float32r
BF16 = mybir.dt.bfloat16
F16 = mybir.dt.float16
RMAX = bass.bass_isa.ReduceOp.max
RADD = bass.bass_isa.ReduceOp.add


def f32(ap):
    return ap.bitcast(F32)


def late(t, n):
    return not isinstance(t, int) or t >= n


def gated_xattn_moe_kernel(nc, x_in, kt_in, v_in, ctx_in, ctxt_in, consts_in, gates_in, rw0_in, w0_in,
                           wsim_in, w1row_in, bsim_in, wqv_in, bqv_in, rw1_in, rbias1_in, w1_in, out):
    ctx = ExitStack()
    with ctx:
        def sb(name, shape, dt, scope=ctx):
            return scope.enter_context(nc.sbuf_tensor(name, shape, dt))

        def sem(name):
            return ctx.enter_context(nc.semaphore(name))

        bank = [ctx.enter_context(nc.psum_tensor(f"bank{i}", [P, 512], F32)) for i in range(8)]

        x = sb("x", [P, TILES, DIM], F32)
        consts = sb("consts", [P, P + 2 + TPB * WIN], F32)
        ident = consts[:, 0:P]
        head_mask = consts[:, P:P + 2]
        band_f32 = consts[:, P + 2:P + 2 + TPB * WIN]
        gates = sb("gates", [P, 4], F32)
        tg = sb("tg", [P, 4], F32)
        stats = sb("stats", [P, TILES, 6], F32)
        meanvar = sb("meanvar", [P, TILES, 2], F32)
        varp = sb("varp", [P, TILES], F32)
        minus_half = sb("minus_half", [P, TPB], F32)
        rstd = sb("rstd", [P, TILES], F32)

        a0 = ExitStack()
        kst = sb("kst", [P, PAIRS, KCOLS], F32R, a0)
        kraw = sb("kraw", [P, 2, 896], F32, a0)
        khl0 = sb("khl0", [P, 2, 2, P + WIN], F32R, a0)
        khl1 = sb("khl1", [P, 2, 2, 896], F32R, a0)
        v3 = sb("v3", [P, VTILES, HEADS, VW], BF16, a0)
        vraw = sb("vraw", [P, 2, 5, DIM], F32, a0)
        band = sb("band", [P, TILES, WIN], BF16, a0)
        identb = sb("identb", [P, P], BF16, a0)
        qf = sb("qf", [P, 2, DIM], F32, a0)
        qn = sb("qn", [P, 2, PAIRS, 4, 32], F32R, a0)
        qst = sb("qst", [P, PAIRS, P], F32R, a0)
        qm = sb("qm", [P, 2, 2, PAIRS, P], F32R, a0)
        nmax = sb("nmax", [P, 4, 2], F32, a0)
        prob = sb("prob", [P, 4, 2, WIN], F32, a0)
        pth = sb("pth", [P, 4, 2, WIN], F16, a0)
        ptl = sb("ptl", [P, 4, 2, WIN], F16, a0)
        rden = sb("rden", [P, 2, PAIRS], F32, a0)
        rdeng = sb("rdeng", [P, 2, PAIRS], F32, a0)
        osum = sb("osum", [P, 2, PAIRS, HD], F32, a0)
        a0.close()

        xn = sb("xn", [P, TILES, DIM], F32)

        rraw = sb("rraw", [P, CH, E0], F32)
        rwhl = sb("rwhl", [P, CH, 2 * E0], F32R)
        rbias = sb("rbias", [P, E1], F32)
        rt = ExitStack()
        xh = sb("xh", [P, CH, TOKENS], F32R, rt)
        xl = sb("xl", [P, CH, TOKENS], F32R, rt)
        wraw = sb("wraw", [P, 2, WCOLS], F32, rt)
        wh = sb("wh", [P, 2, WCOLS], F32R, rt)
        wl = sb("wl", [P, 2, WCOLS], F32R, rt)
        sil = sb("sil", [P, 2, 512], F32, rt)
        hid = sb("hid", [P, 2, 512], F32, rt)
        hidh = sb("hidh", [P, 2, 512], F32R, rt)
        hidl = sb("hidl", [P, 2, 512], F32R, rt)
        cw = sb("cw", [P, TILES, NB0], F32, rt)
        lgt = sb("lgt", [E0, 2, SEQ], F32, rt)
        lg = sb("lg", [P, TILES, E0], F32, rt)
        sc = sb("sc", [P, TILES, E0], F32, rt)
        msc = sb("msc", [P, TILES, E0], F32, rt)
        rep = sb("rep", [P, TILES, E0], F32, rt)
        selw = sb("selw", [P, TILES, E0], F32, rt)
        gs = sb("gs", [P, TILES, 8], F32, rt)
        rep8 = sb("rep8", [P, TILES, 8], F32, rt)
        cmp = sb("cmp", [P, TILES, 8], F32, rt)
        top8 = sb("top8", [P, TILES, 8], F32, rt)
        rsum = sb("rsum", [P, TILES], F32, rt)
        rrec = sb("rrec", [P, TILES], F32, rt)
        rmx = sb("rmx", [P, TILES], F32, rt)
        rt.close()

        a1 = ExitStack()
        craw = sb("craw", [P, CH, SEQ], F32, a1)
        ctxh = sb("ctxh", [P, CH, SEQ], F32R, a1)
        ctxl = sb("ctxl", [P, CH, SEQ], F32R, a1)
        traw = sb("traw", [P, TPB, DIM], F32, a1)
        tokh = sb("tokh", [P, TPB, DIM], F32R, a1)
        tokl = sb("tokl", [P, TPB, DIM], F32R, a1)
        enc = sb("enc", [P, 3, CH, SEQ], F32, a1)
        ench = sb("ench", [P, 3, CH, SEQ], F32R, a1)
        encl = sb("encl", [P, 3, CH, SEQ], F32R, a1)
        aenc = sb("aenc", [P, CH, SEQ], F32, a1)
        aench = sb("aench", [P, CH, SEQ], F32R, a1)
        aencl = sb("aencl", [P, CH, SEQ], F32R, a1)
        prob1 = sb("prob1", [P, 2, TPB, SEQ], F32, a1)
        p1th = sb("p1th", [P, TPB, SEQ], F32R, a1)
        p1tl = sb("p1tl", [P, TPB, SEQ], F32R, a1)
        hqh = sb("hqh", [P, CH, SEQ], F32R, a1)
        hql = sb("hql", [P, CH, SEQ], F32R, a1)
        prod = sb("prod", [P, CH, SEQ], F32, a1)
        prodh = sb("prodh", [P, CH, SEQ], F32R, a1)
        prodl = sb("prodl", [P, CH, SEQ], F32R, a1)
        wqv = sb("wqv", [P, 4 * CH, DIM], F32, a1)
        wqh = sb("wqh", [P, 3 * CH, DIM], F32R, a1)
        wql = sb("wql", [P, 3 * CH, DIM], F32R, a1)
        w14 = sb("w14", [P, CH, DIM], F32, a1)
        wsim = sb("wsim", [P, 2, CH], F32, a1)
        w1row = sb("w1row", [P, DIM], F32, a1)
        bqv = sb("bqv", [P, DIM], F32, a1)
        bqvg = sb("bqvg", [P, DIM], F32, a1)
        bsim = sb("bsim", [P, 1], F32, a1)
        junk = sb("junk", [P, DIM], F32, a1)
        rterm = sb("rterm", [P, TPB], F32, a1)
        nm1 = sb("nm1", [P, TPB], F32, a1)
        den1 = sb("den1", [P, TPB], F32, a1)
        rd1 = sb("rd1", [P, TPB], F32, a1)
        msim = sb("msim", [P, TPB], F32, a1)
        mx1 = sb("mx1", [P, 1], F32, a1)
        gmx1 = sb("gmx1", [P, 1], F32, a1)
        ngmx1 = sb("ngmx1", [P, 1], F32, a1)
        eb = sb("eb", [P, TPB], F32, a1)
        ebs = sb("ebs", [P, 1], F32, a1)
        ebt = sb("ebt", [P, 1], F32, a1)
        ebr = sb("ebr", [P, 1], F32, a1)
        batt = sb("batt", [P, TPB], F32, a1)
        hbar = sb("hbar", [P, CH], F32, a1)
        a1.close()

        s_const = sem("const_loaded")
        s_bandf = sem("band_loaded")
        s_gates = sem("gates_loaded")
        s_x = [sem(f"x_loaded{b}") for b in range(BATCH)]
        s_kraw = sem("kraw_loaded")
        s_vraw = [sem(f"vraw_loaded{i}") for i in range(2)]
        s_tg = sem("tanh_ready")
        s_band = sem("band_ready")
        s_identb = sem("identb_ready")
        s_ln = [sem(f"ln_stats{i}") for i in range(4)]
        s_lnp = [sem(f"ln_rsqrt{i}") for i in range(4)]
        s_fill = sem("pool_filled")
        s_khi = sem("k_hi")
        s_klo = sem("k_lo")
        s_kst0 = [sem(f"k_stacked0_{g}_") for g in range(4)]
        s_kst = {i: sem(f"k_stacked{i}") for i in (1, 2)}
        s_va = sem("v_parts_act")
        s_vd = sem("v_parts_dve")
        s_qn = sem("q_hi")
        s_ql = sem("q_lo")
        s_tq = sem("q_transposed")
        s_qst = sem("q_stacked")
        s_qm = sem("q_masked")
        s_s = sem("scores_ready")
        s_nm = sem("max_ready")
        s_p = sem("probs_ready")
        s_pt = sem("probs_transposed")
        s_pth = sem("pt_hi")
        s_ptl = sem("pt_lo")
        s_pv = sem("pv_done")
        s_rr = sem("rden_gated")
        s_o = sem("o_summed")
        s_os = sem("o_scaled")
        s_xa = sem("x_attended")

        class Moe:

            def __init__(self, n):
                def s(name):
                    return sem(f"{name}{n}")
                self.rload = s("router_loaded")
                self.rhi = s("router_hi")
                self.rlo = s("router_lo")
                self.xn = s("xn_ready")
                self.tr = s("xn_transposed")
                self.xh = s("xh_ready")
                self.xl = s("xl_ready")
                self.lt = s("logits_made")
                self.ltc = s("logits_copied")
                self.lg = s("logits_transposed")
                self.lgl = s("logits_ready")
                self.rs = s("route_step")
                self.ra = s("route_act")
                self.cw = s("cw_ready")
                self.wload = [s(f"w_loaded_{i}_") for i in range(2)]
                self.whi = s("w_hi")
                self.wlo = s("w_lo")
                self.gate = s("gate_ready")
                self.up = s("up_ready")
                self.sil = s("silu_ready")
                self.h = s("h_ready")
                self.hh = s("h_hi")
                self.hl = s("h_lo")
                self.y = s("y_ready")
                self.acc = s("y_added")

        moe = [Moe(0), Moe(1)]
        s_a1 = {n: sem("a1_" + n) for n in (
            "par", "bq", "wq", "wqs", "ctx_t", "ctx", "chi", "clo", "thi", "tlo", "xn", "tr", "enc", "elo",
            "a", "ahi", "alo", "r", "sim", "nm", "p", "rd", "pn", "pt", "pth", "ptl", "msim", "mx", "gmx", "ngmx", "eb", "ebt",
            "ebr", "batt", "hb", "hbc", "w14", "whi", "wlo", "hq", "hqh", "hql", "prod", "prh", "prl", "xb", "o", "x")}
        s_out = sem("out_stored")

        block = ctx.enter_context(nc.Block())

        UNITS = TILES * PAIRS
        TURN_BANKS = (0, 1, 4, 5)
        S_TURN = (0, 1, 3, 5, 6, 7, 8, 9)
        Q_TURN = (2, 4)

        def s_bank(k, par):
            return bank[TURN_BANKS[(10 * par + S_TURN[k]) % 4]]

        def q_bank(h, par):
            return bank[TURN_BANKS[(10 * par + Q_TURN[h]) % 4]]

        def bank_free(pe, t, turn):
            tt, before = (t, turn - 4) if turn >= 4 else (t - 1, turn + 6)
            if isinstance(tt, int) and (tt < 0 or (tt + 1 >= TILES and before in Q_TURN)):
                return
            if before in Q_TURN:
                pe.wait_ge(s_qst, 2 * (tt + 1) + Q_TURN.index(before) + 1)
            else:
                pe.wait_ge(s_p, 8 * tt + S_TURN.index(before) + 1)

        def q_transpose(pe, t, h, par, to):
            pe.wait_ge(s_ql, t + 1)
            for j in range(4):
                src = f32(qn[:, par, 4 * h + j].rearrange("p a b -> p (a b)"))
                mm = pe.transpose(to[:, j * P:(j + 1) * P], src, ident)
            mm.then_inc(s_tq, 1)

        def attention_tensor(pe):
            pe.wait_ge(s_const, 16)
            for h in range(2):
                q_transpose(pe, 0, h, 0, bank[TURN_BANKS[2 + h]])

            def step(t, k, par, last):
                u = 8 * t + k
                if not last:
                    if k == 0 or k == 4:
                        pe.wait_ge(s_qm, 4 * t + k // 2 + 2)
                    if isinstance(t, int) and t == 0 and k == 0:
                        pe.wait_ge(s_identb, 1)
                        pe.wait_ge(s_band, 1)
                    if isinstance(t, int) and t == 0 and k % 2 == 0:
                        pe.wait_ge(s_kst0[k // 2], 64)
                    bank_free(pe, t, S_TURN[k])
                    sp = s_bank(k, par)
                    if isinstance(t, int):
                        msk = band[:, t:t + 1, :].broadcast_to([P, 2, WIN])
                    else:
                        msk = band[:, bass.ds(t, 1), :].broadcast_to([P, 2, WIN])
                    pe.matmul(sp[:, :], identb[:, :], msk, start=True, stop=False, skip_group_check=True)
                    for hh in range(2):
                        ks = kst[:, k, 128 * t:128 * t + WIN] if isinstance(t, int) else kst[:, k, bass.ds(128 * t, WIN)]
                        mm = pe.matmul(sp[:, hh * WIN:(hh + 1) * WIN], qm[:, par, hh, k, :], ks,
                                       start=False, stop=True, skip_group_check=True)
                    mm.then_inc(s_s, 1)
                    if (k == 1 or k == 2) and not (isinstance(t, int) and t + 1 >= TILES):
                        bank_free(pe, t, Q_TURN[k - 1])
                        q_transpose(pe, t + 1, k - 1, 1 - par, q_bank(k - 1, par))
                if late(u, 3) and not (isinstance(u, int) and u - 3 >= UNITS):
                    pe.wait_ge(s_p, u - 2)
                    if late(u, 5):
                        pe.wait_ge(s_ptl, u - 4)
                    for hh in range(2):
                        for kb in range(2):
                            mm = pe.transpose(bank[2 + (k + 1) % 2][:, hh * WIN + kb * P:hh * WIN + kb * P + P],
                                              prob[:, (k + 1) % 4, hh, kb * P:(kb + 1) * P], ident)
                    mm.then_inc(s_pt, 1)
                if late(u, 5):
                    kk = (k - 5) % PAIRS
                    tt = t if k >= 5 else t - 1
                    pe.wait_ge(s_ptl, u - 4)
                    if kk == 0 or kk == 4:
                        if late(tt, 1):
                            pe.wait_ge(s_o, 2 * (2 * (tt - 1) + kk // 4 + 1))
                        if isinstance(t, int) and t == 0:
                            pe.wait_ge(s_fill, 2)
                            pe.wait_ge(s_vd, 2)
                    for hh in range(2):
                        head = 2 * kk + hh
                        o = bank[6 + kk // 4][:, (head % 8) * VW:(head % 8 + 1) * VW]
                        n = 0
                        for kb in range(2):
                            if isinstance(tt, int):
                                vv = v3[:, tt + kb, head, :]
                            else:
                                vv = v3[:, bass.ds(tt + kb, 1), head, :]
                            for part in (pth, ptl):
                                mm = pe.matmul(o, part[:, (k + 3) % 4, hh, kb * P:(kb + 1) * P], vv,
                                               start=(n == 0), stop=(n == 3))
                                n += 1
                    mm.then_inc(s_pv, 1)

            for t in (0, 1):
                for k in range(PAIRS):
                    step(t, k, t, False)
            for piece in (1, 2):
                pe.wait_ge(s_kst[piece], 256)
            pe.wait_ge(s_vd, 2 * len(VGROUPS))
            pe.wait_ge(s_band, BATCH)
            with pe.Fori(0, (TILES - 4) // 4) as i:
                for j in range(4):
                    for k in range(PAIRS):
                        step(4 * i + 2 + j, k, j % 2, False)
            for t in (TILES - 2, TILES - 1):
                for k in range(PAIRS):
                    step(t, k, t % 2, False)
            for k in range(5):
                step(TILES, k, 0, True)

        def q_stack(act, t, h, src):
            act.wait_ge(s_tq, 2 * t + h + 1)
            if late(t, 1):
                act.wait_ge(s_qm, 4 * (t - 1) + 2 * h + 2)
            nc.scalar.activation(qst[:, 4 * h:4 * h + 4, :], src[:, :].rearrange("p (a b) -> p a b", a=4),
                                 ACT.Copy).then_inc(s_qst, 1)

        def k_parts(s):
            a, b = KPIECES[s]
            return kraw[:, :, 0:b - a], (khl1 if s else khl0)

        def k_hi(s):
            raw, parts = k_parts(s)
            nc.scalar.wait_ge(s_kraw, 16 * (s + 1))
            if s == 2:
                nc.scalar.wait_ge(s_kst[1], 256)
            nc.scalar.activation(parts[:, 0], raw, ACT.Copy).then_inc(s_khi, 1)

        def v_part(g, j):
            a, b = VGROUPS[g]
            return v3[:, a:b, :, j * HD:(j + 1) * HD]

        def v_raw(g):
            a, b = VGROUPS[g]
            return vraw[:, g % 2, 0:b - a, :].rearrange("p t (h d) -> p t h d", h=HEADS)

        def v_act(g, j):
            if j == 0:
                nc.scalar.wait_ge(s_vraw[g % 2], 16 * (g // 2 + 1))
            else:
                nc.scalar.wait_ge(s_vd, 2 * g + 1)
            nc.scalar.activation(v_part(g, j), v_raw(g), ACT.Copy).then_inc(s_va, 1)

        def v_dve(g, j):
            nc.vector.wait_ge(s_va, 2 * g + j + 1)
            if j == 0:
                nc.vector.tensor_tensor(v_raw(g), v_raw(g), v_part(g, 0), ALU.subtract).then_inc(s_vd, 1)
            else:
                nc.vector.tensor_tensor(v_part(g, 2), v_raw(g), v_part(g, 1), ALU.subtract).then_inc(s_vd, 1)

        EARLY = {0: ("v", 0, 1), 2: ("v", 1, 0), 4: ("v", 1, 1), 5: ("v", 2, 0), 7: ("v", 2, 1), 8: ("k", 2, 0),
                 10: ("v", 3, 0), 12: ("v", 3, 1)}

        def attention_scalar(act):
            k_hi(0)
            act.wait_ge(s_gates, 16)
            nc.scalar.activation(tg[:, :], gates[:, :], ACT.Tanh).then_inc(s_tg, 1)
            v_act(0, 0)
            q_stack(act, 0, 0, bank[TURN_BANKS[2]])
            q_stack(act, 0, 1, bank[TURN_BANKS[3]])
            k_hi(1)

            def step(t, k, par, last):
                u = 8 * t + k
                if late(u, 3) and not (isinstance(u, int) and u - 3 >= UNITS):
                    act.wait_ge(s_pt, u - 2)
                    if late(u, 7):
                        act.wait_ge(s_pv, u - 6)
                    nc.scalar.activation(pth[:, (k + 1) % 4], bank[2 + (k + 1) % 2][:, :].rearrange("p (a b) -> p a b", a=2),
                                         ACT.Copy).then_inc(s_pth, 1)
                if last:
                    return
                if (k == 2 or k == 3) and not (isinstance(t, int) and t + 1 >= TILES):
                    q_stack(act, t + 1, k - 2, q_bank(k - 2, par))
                act.wait_ge(s_nm, u + 1)
                if late(u, 4):
                    act.wait_ge(s_pt, u - 3)
                for hh in range(2):
                    e = nc.scalar.activation(prob[:, k % 4, hh, :], s_bank(k, par)[:, hh * WIN:(hh + 1) * WIN], ACT.Exp,
                                             bias=nmax[:, k % 4, hh:hh + 1])
                e.then_inc(s_p, 1)
                if isinstance(t, int) and u in EARLY:
                    what, g, j = EARLY[u]
                    if what == "v":
                        v_act(g, j)
                    else:
                        k_hi(g)

            for t in (0, 1):
                for k in range(PAIRS):
                    step(t, k, t, False)
            with act.Fori(0, (TILES - 4) // 4) as i:
                for j in range(4):
                    for k in range(PAIRS):
                        step(4 * i + 2 + j, k, j % 2, False)
            for t in (TILES - 2, TILES - 1):
                for k in range(PAIRS):
                    step(t, k, t % 2, False)
            for k in range(3):
                step(TILES, k, 0, True)

        def attention_vector(dve):
            def q_norm(t, par):
                if late(t, 2):
                    dve.wait_ge(s_tq, 2 * (t - 1))
                if isinstance(t, int):
                    xt, mean, rs = x[:, t:t + 1, :], meanvar[:, t, 0:1], rstd[:, t:t + 1]
                else:
                    xt, mean, rs = x[:, bass.ds(t, 1), :], meanvar[:, bass.ds(t, 1), 0], rstd[:, bass.ds(t, 1)]
                nc.vector.tensor_scalar(qf[:, par:par + 1], xt, mean, rs, ALU.subtract, ALU.mult).then_inc(s_qn, 1)
                xt = xt.rearrange("p t (a b) -> p (t a) b", a=PAIRS).unsqueeze(2).broadcast_to([P, PAIRS, 2, 32])
                nc.vector.tensor_scalar(qn[:, par, :, 0:2], xt, mean, rs, ALU.subtract, ALU.mult).then_inc(s_qn, 1)

            def k_lo(s):
                raw, parts = k_parts(s)
                dve.wait_ge(s_khi, s + 1)
                nc.vector.tensor_tensor(parts[:, 1], raw, f32(parts[:, 0]), ALU.subtract).then_inc(s_klo, 1)

            def o_sum(t, h):
                n = 2 * t + h
                dve.wait_ge(s_pv, 8 * t + 4 * h + 4)
                if late(t, 1):
                    dve.wait_ge(s_xa, n - 1)
                ov = bank[6 + h][:, 0:8 * VW].rearrange("p (a b) -> p a b", a=8)
                nc.vector.reciprocal(rden[:, h, :], ov[:, :, 3 * HD]).then_inc(s_o, 1)
                nc.vector.tensor_reduce(osum[:, h], ov[:, :, 0:3 * HD].rearrange("p a (c d) -> p a d c", c=3),
                                        AX_X, ALU.add).then_inc(s_o, 1)

            ln_stats(dve, 0, 0)
            k_lo(0)
            dve.wait_ge(s_lnp[0], 2)
            q_norm(0, 0)
            dve.wait_ge(s_bandf, 16)
            nc.vector.tensor_copy(band[:, 0:TPB, :], band_f32.rearrange("p (t w) -> p t w", t=TPB)).then_inc(s_band, 1)
            v_dve(0, 0)
            q_norm(1, 1)
            k_lo(1)

            def step(t, k, par, last):
                u = 8 * t + k
                if not last:
                    dve.wait_ge(s_s, u + 1)
                    nc.vector.tensor_reduce(nmax[:, k % 4, :], s_bank(k, par)[:, :].rearrange("p (a b) -> p a b", a=2),
                                            AX_X, ALU.max, negate=True).then_inc(s_nm, 1)
                    if k == 6 and not (isinstance(t, int) and t + 2 >= TILES):
                        q_norm(t + 2, par)
                    if isinstance(t, int) and u in (3, 10, 12):
                        ln_stats(dve, 0, {3: 1, 10: 2, 12: 3}[u])
                if late(u, 4) and not (isinstance(u, int) and u - 4 >= UNITS):
                    dve.wait_ge(s_pth, u - 3)
                    nc.vector.tensor_tensor(ptl[:, k % 4], bank[2 + k % 2][:, :].rearrange("p (a b) -> p a b", a=2),
                                            pth[:, k % 4], ALU.subtract).then_inc(s_ptl, 1)
                if (k == 1 or k == 5) and late(t, 1):
                    o_sum(t - 1, k // 4)
                if isinstance(t, int) and u - 1 in EARLY:
                    what, g, j = EARLY[u - 1]
                    if what == "v":
                        v_dve(g, j)
                    else:
                        k_lo(g)

            for t in (0, 1):
                for k in range(PAIRS):
                    step(t, k, t, False)
            dve.wait_ge(s_lnp[0], 2 * BATCH)
            with dve.Fori(0, (TILES - 4) // 4) as i:
                for j in range(4):
                    for k in range(PAIRS):
                        step(4 * i + 2 + j, k, j % 2, False)
            for t in (TILES - 2, TILES - 1):
                for k in range(PAIRS):
                    step(t, k, t % 2, False)
            dve.wait_ge(s_xa, 2 * (TILES - TPB))
            for k in range(6):
                step(TILES, k, 0, True)
                if 2 <= k <= 4:
                    ln_stats(dve, 1, k - 2)

        def attention_pool(pool):
            nc.gpsimd.memset(minus_half[:, :], -0.5).then_inc(s_fill, 1)
            nc.gpsimd.memset(v3[:, :, :, 3 * HD:VW], 1.0).then_inc(s_fill, 1)

            def q_lo(t, par):
                pool.wait_ge(s_qn, 2 * t + 2)
                full = qf[:, par].rearrange("p (a b) -> p a b", a=PAIRS).unsqueeze(2).broadcast_to([P, PAIRS, 2, 32])
                nc.gpsimd.tensor_tensor(qn[:, par, :, 2:4], full, f32(qn[:, par, :, 0:2]), ALU.subtract).then_inc(s_ql, 1)

            def q_mask(t, par, h):
                pool.wait_ge(s_qst, 2 * t + h + 1)
                if late(t, 2):
                    pool.wait_ge(s_s, 8 * (t - 1))
                pairs = slice(4 * h, 4 * h + 4)
                for hh in range(2):
                    m = head_mask[:, hh:hh + 1].unsqueeze(2).broadcast_to([P, 4, P])
                    nc.gpsimd.tensor_tensor(qm[:, par, hh, pairs], f32(qst[:, pairs, :]), m, ALU.mult).then_inc(s_qm, 1)

            def x_update(t, h):
                n = 2 * t + h
                pool.wait_ge(s_o, 2 * n + 2)
                nc.gpsimd.tensor_tensor(rdeng[:, h, :], rden[:, h, :], tg[:, 0:1].broadcast_to([P, PAIRS]),
                                        ALU.mult).then_inc(s_rr, 1)
                pool.wait_ge(s_rr, n + 1)
                nc.gpsimd.tensor_tensor(osum[:, h], osum[:, h],
                                        rdeng[:, h, :].unsqueeze(2).broadcast_to([P, PAIRS, HD]),
                                        ALU.mult).then_inc(s_os, 1)
                pool.wait_ge(s_os, n + 1)
                if isinstance(t, int):
                    xt = x[:, t, h * P:(h + 1) * P]
                else:
                    xt = x[:, bass.ds(t, 1), h * P:(h + 1) * P]
                nc.gpsimd.tensor_tensor(xt, xt, osum[:, h].rearrange("p a b -> p (a b)"), ALU.add).then_inc(s_xa, 1)

            def tile(t, par):
                if late(t, 1):
                    x_update(t - 1, 0)
                if not (isinstance(t, int) and t + 1 >= TILES):
                    q_mask(t + 1, 1 - par, 0)
                    q_mask(t + 1, 1 - par, 1)
                if isinstance(t, int) and t == 1:
                    ln_rsqrt(pool, 0, 1)
                    ln_rsqrt(pool, 0, 2)
                if late(t, 1):
                    x_update(t - 1, 1)
                if isinstance(t, int) and t == 1:
                    ln_rsqrt(pool, 0, 3)
                if not (isinstance(t, int) and t + 2 >= TILES):
                    q_lo(t + 2, par)

            pool.wait_ge(s_fill, 1)
            ln_rsqrt(pool, 0, 0)
            pool.wait_ge(s_const, 16)
            nc.gpsimd.tensor_copy(identb[:, :], ident).then_inc(s_identb, 1)
            q_lo(0, 0)
            q_mask(0, 0, 0)
            q_mask(0, 0, 1)
            q_lo(1, 1)
            pool.wait_ge(s_bandf, 16)
            for b in range(1, BATCH):
                nc.gpsimd.tensor_copy(band[:, TPB * b:TPB * b + TPB, :],
                                      band_f32.rearrange("p (t w) -> p t w", t=TPB)).then_inc(s_band, 1)
            pool.wait_ge(s_tg, 1)
            tile(0, 0)
            tile(1, 1)
            with pool.Fori(0, (TILES - 4) // 4) as i:
                for j in range(4):
                    tile(4 * i + 2 + j, j % 2)
            for t in (TILES - 2, TILES - 1):
                tile(t, t % 2)
            x_update(TILES - 1, 0)
            ln_rsqrt(pool, 1, 0)
            ln_rsqrt(pool, 1, 1)
            x_update(TILES - 1, 1)
            ln_rsqrt(pool, 1, 2)

        def ln_stats(dve, n, b):
            if n == 0:
                dve.wait_ge(s_x[b], 16)
            for t in range(TPB * b, TPB * b + TPB):
                op = nc.vector.bn_stats(stats[:, t, :], x[:, t, :])
            op.then_inc(s_ln[n], 1)
            dve.wait_ge(s_ln[n], 2 * b + 1)
            for t in range(TPB * b, TPB * b + TPB):
                op = nc.vector.bn_aggr(meanvar[:, t, :], stats[:, t, :])
            op.then_inc(s_ln[n], 1)

        def ln_rsqrt(pool, n, b):
            ts = slice(TPB * b, TPB * b + TPB)
            pool.wait_ge(s_ln[n], 2 * b + 2)
            nc.gpsimd.tensor_scalar(varp[:, ts], meanvar[:, ts, 1], EPS, None, ALU.add).then_inc(s_lnp[n], 1)
            pool.wait_ge(s_lnp[n], 2 * b + 1)
            nc.gpsimd.tensor_tensor(rstd[:, ts], varp[:, ts], minus_half[:, :], ALU.pow).then_inc(s_lnp[n], 1)

        def ln_norm(dve, n, b, ready):
            dve.wait_ge(s_lnp[n], 2 * b + 2)
            for t in range(TPB * b, TPB * b + TPB):
                op = nc.vector.tensor_scalar(xn[:, t, :], x[:, t, :], meanvar[:, t, 0:1], rstd[:, t:t + 1],
                                             ALU.subtract, ALU.mult)
            op.then_inc(ready, 1)

        X_BANKS = ((0, 2), (1, 3), (6, 7), (6, 7))

        def x_transposes(pe, m, b):
            pe.wait_ge(m.xn, b + 1)
            if b == 3:
                pe.wait_ge(m.xl, 2 * b)
            for c in range(CH):
                for j in range(TPB):
                    mm = pe.transpose(bank[X_BANKS[b][c]][:, j * P:(j + 1) * P],
                                      xn[:, TPB * b + j, c * P:(c + 1) * P], ident)
                mm.then_inc(m.tr, 1)

        def x_high(act, m, b):
            for c in range(CH):
                act.wait_ge(m.tr, 2 * b + c + 1)
                nc.scalar.activation(xh[:, c, b * SEQ:(b + 1) * SEQ], bank[X_BANKS[b][c]][:, :],
                                     ACT.Copy).then_inc(m.xh, 1)

        def x_low(dve, m, b):
            for c in range(CH):
                dve.wait_ge(m.xh, 2 * b + c + 1)
                cols = slice(b * SEQ, (b + 1) * SEQ)
                nc.vector.tensor_tensor(xl[:, c, cols], bank[X_BANKS[b][c]][:, :], f32(xh[:, c, cols]),
                                        ALU.subtract).then_inc(m.xl, 1)

        def moe_tensor(pe, L, m, nb):
            ne = (E0, E1)[L]

            def logits(b):
                pe.wait_ge(m.xl, 2 * (b + 1))
                if b == 0:
                    pe.wait_ge(m.rlo, 1)
                else:
                    pe.wait_ge(m.ltc, b)
                n = 0
                for c in range(CH):
                    for wp in range(2):
                        for xp in (xh, xl):
                            mm = pe.matmul(bank[4][0:ne, :], rwhl[:, c, wp * ne:(wp + 1) * ne],
                                           xp[:, c, b * SEQ:(b + 1) * SEQ], start=(n == 0), stop=(n == 7))
                            n += 1
                mm.then_inc(m.lt, 1)

            def logits_by_token(b):
                pe.wait_ge(m.ltc, b + 1)
                for j in range(TPB):
                    t = TPB * b + j
                    mm = pe.transpose(bank[5][:, t * ne:(t + 1) * ne], lgt[0:ne, b % 2, j * P:(j + 1) * P],
                                      ident[0:ne, 0:ne])
                mm.then_inc(m.lg, 1)

            def gate_up(v, b, par):
                vp = b % 2
                if b == 0:
                    e1 = v // 4 + 1 if isinstance(v, int) else None
                    pe.wait_ge(m.wlo, e1 if e1 is not None else v_e[0] + 1)
                if late(v, 2):
                    pe.wait_ge(m.sil, v - 1)
                for half, ready in ((0, m.gate), (1, m.up)):
                    if half == 1 and late(v, 2):
                        pe.wait_ge(m.h, v - 1)
                    o = bank[2 * half + vp]
                    n = 0
                    for c in range(CH):
                        w = slice((CH * half + c) * FF, (CH * half + c + 1) * FF)
                        for wp, xp in ((wh, xh), (wh, xl), (wl, xh)):
                            mm = pe.matmul(o[:, :], wp[:, par, w], xp[:, c, b * SEQ:(b + 1) * SEQ],
                                           start=(n == 0), stop=(n == 5))
                            n += 1
                    mm.then_inc(ready, 1)

            def down(v, b, par):
                vp = b % 2
                if isinstance(v, int) and v == 1:
                    pe.wait_ge(m.lgl, 1)
                pe.wait_ge(m.hl, v)
                if late(v, 3):
                    pe.wait_ge(m.acc, v - 2)
                for j in range(TPB):
                    o = bank[4 + 2 * vp + j // 2][:, (j % 2) * DIM:(j % 2 + 1) * DIM]
                    n = 0
                    for hp, wp in ((hidh, wh), (hidh, wl), (hidl, wh)):
                        mm = pe.matmul(o, hp[:, vp, j * P:(j + 1) * P], wp[:, par, 2 * CH * FF:WCOLS],
                                       start=(n == 0), stop=(n == 2))
                        n += 1
                mm.then_inc(m.y, 1)

            v_e = [None]

            def body(e, par):
                v_e[0] = e
                for b in range(4):
                    gate_up(4 * e + b, b, par)
                    if late(4 * e + b, 1):
                        down(4 * e + b, (b - 1) % 4, par if b else 1 - par)

            if L == 0:
                x_transposes(pe, m, 0)
                x_transposes(pe, m, 1)
            if L == 1:
                x_transposes(pe, m, 2)
            logits(0)
            if L == 0:
                x_transposes(pe, m, 2)
            gate_up(0, 0, 0)
            logits_by_token(0)
            logits(1)
            gate_up(1, 1, 0)
            x_transposes(pe, m, 3)
            logits_by_token(1)
            logits(2)
            gate_up(2, 2, 0)
            logits_by_token(2)
            logits(3)
            logits_by_token(3)
            down(1, 0, 0)
            down(2, 1, 0)
            gate_up(3, 3, 0)
            down(3, 2, 0)
            body(1, 1)
            with pe.Fori(1, (nb - 1) // 2) as i:
                body(2 * i, 0)
                body(2 * i + 1, 1)
            for e in range(2 * ((nb - 1) // 2), nb):
                body(e, e % 2)
            down(4 * nb, 3, (nb - 1) % 2)

        def moe_scalar(act, L, m, nb, route):
            ne = (E0, E1)[L]

            def weights_hi(e, par, loaded):
                act.wait_ge(m.wload[par], loaded)
                if late(e, 2):
                    act.wait_ge(m.y, 4 * (e - 1))
                nc.scalar.activation(wh[:, par], wraw[:, par], ACT.Copy).then_inc(m.whi, 1)

            def logits_copy(b):
                act.wait_ge(m.lt, b + 1)
                if b >= 2:
                    act.wait_ge(m.lg, b - 1)
                nc.scalar.activation(lgt[0:ne, b % 2, :], bank[4][0:ne, :], ACT.Copy).then_inc(m.ltc, 1)

            def silu(v, b):
                vp = b % 2
                act.wait_ge(m.gate, v + 1)
                if late(v, 2):
                    act.wait_ge(m.h, v - 1)
                nc.scalar.activation(sil[:, vp], bank[vp][:, :], ACT.Silu).then_inc(m.sil, 1)

            def hidden_hi(v, b):
                vp = b % 2
                act.wait_ge(m.h, v + 1)
                if late(v, 2):
                    act.wait_ge(m.y, v - 1)
                nc.scalar.activation(hidh[:, vp], hid[:, vp], ACT.Copy).then_inc(m.hh, 1)

            def step(v, b):
                silu(v, b)
                hidden_hi(v, b)

            def body(e, par, loaded):
                for b in range(4):
                    step(4 * e + b, b)
                    if b == 2 and not (isinstance(e, int) and (e + 1 >= nb or e == 0)):
                        weights_hi(e + 1, 1 - par, loaded)

            if L == 0:
                x_high(act, m, 0)
            act.wait_ge(m.rload, 16 + 16 * L)
            nc.scalar.activation(rwhl[:, :, 0:ne], rraw[:, :, 0:ne], ACT.Copy).then_inc(m.rhi, 1)
            weights_hi(0, 0, 16)
            if L == 0:
                x_high(act, m, 1)
            logits_copy(0)
            x_high(act, m, 2)
            weights_hi(1, 1, 16)
            step(0, 0)
            logits_copy(1)
            step(1, 1)
            x_high(act, m, 3)
            logits_copy(2)
            silu(2, 2)
            logits_copy(3)
            hidden_hi(2, 2)
            route(act, m)
            step(3, 3)
            body(1, 1, 32)
            with act.Fori(1, (nb - 1) // 2) as i:
                body(2 * i, 0, 16 * i + 16)
                body(2 * i + 1, 1, 16 * i + 32)
            for e in range(2 * ((nb - 1) // 2), nb):
                body(e, e % 2, 16 * ((e + 1) // 2 + 1))

        def moe_vector(dve, L, m, nb, first, routing):
            n = 1 + 2 * L
            ne = (E0, E1)[L]

            def add(v, e, b):
                vp = b % 2
                dve.wait_ge(m.y, v + 1)
                if late(v, 4):
                    dve.wait_ge(m.acc, v - 3)
                for j in range(TPB):
                    t = TPB * b + j
                    w = cw[:, t, e:e + 1] if isinstance(e, int) else cw[:, t, bass.ds(e, 1)]
                    op = nc.vector.scalar_tensor_tensor(
                        out=x[:, t, :], in0=bank[4 + 2 * vp + j // 2][:, (j % 2) * DIM:(j % 2 + 1) * DIM],
                        scalar=w, in1=x[:, t, :], op0=ALU.mult, op1=ALU.add)
                op.then_inc(m.acc, 1)

            def hidden(v, b):
                vp = b % 2
                dve.wait_ge(m.up, v + 1)
                dve.wait_ge(m.sil, v + 1)
                if late(v, 2):
                    dve.wait_ge(m.hl, v - 1)
                nc.vector.tensor_tensor(hid[:, vp], sil[:, vp], bank[2 + vp][:, :], ALU.mult).then_inc(m.h, 1)

            def hidden_lo(v, b):
                vp = b % 2
                dve.wait_ge(m.hh, v + 1)
                nc.vector.tensor_tensor(hidl[:, vp], hid[:, vp], f32(hidh[:, vp]), ALU.subtract).then_inc(m.hl, 1)

            def step(v, e, b):
                hidden(v, b)
                if late(v, 8):
                    hidden_lo(v, b)
                if late(v, 1):
                    add(v - 1, e if b else e - 1, (b - 1) % 4)

            if L == 0:
                ln_norm(dve, n, 0, m.xn)
                ln_norm(dve, n, 1, m.xn)
                x_low(dve, m, 0)
            dve.wait_ge(m.rhi, 1)
            nc.vector.tensor_tensor(rwhl[:, :, ne:2 * ne], rraw[:, :, 0:ne], f32(rwhl[:, :, 0:ne]),
                                    ALU.subtract).then_inc(m.rlo, 1)
            if L == 0:
                ln_norm(dve, n, 2, m.xn)
                x_low(dve, m, 1)
                dve.wait_ge(s_xa, 2 * TILES)
            ln_stats(dve, n, 3)
            x_low(dve, m, 2)
            ln_norm(dve, n, 3, m.xn)
            hidden(0, 0)
            hidden(1, 1)
            x_low(dve, m, 3)
            hidden(2, 2)
            first()
            add(0, 0, 0)
            add(1, 0, 1)
            parts = ({2: routing[0:2], 3: routing[2:4], 4: routing[4:]},
                     {2: (), 3: routing[0:1], 4: routing[1:2], 5: routing[2:3], 6: routing[3:4], 7: routing[4:]})[L]
            for v in range(2, 8):
                if v > 2:
                    step(v, v // 4, v % 4)
                for part in parts.get(v, ()):
                    part()
            dve.wait_ge(m.hl, 8)
            with dve.Fori(1, (nb - 1) // 2) as i:
                for e in range(2):
                    for b in range(4):
                        step(8 * i + 4 * e + b, 2 * i + e, b)
            for e in range(2 * ((nb - 1) // 2), nb):
                for b in range(4):
                    step(4 * e + b, e, b)
                    if L == 0 and e == nb - 1 and b:
                        dve.wait_ge(m.acc, 4 * e + b)
                        ln_stats(dve, 2, b - 1)
                        if b >= 2:
                            ln_norm(dve, 2, b - 2, A["xn"])
            add(4 * nb - 1, nb - 1, 3)

        def moe_pool(pool, L, m, nb):
            def low(e, par):
                pool.wait_ge(m.whi, e + 1)
                nc.gpsimd.tensor_tensor(wl[:, par], wraw[:, par], f32(wh[:, par]), ALU.subtract).then_inc(m.wlo, 1)

            low(0, 0)
            ln_rsqrt(pool, 1 + 2 * L, 3)
            low(1, 1)
            for v in range(8):
                if v == 7:
                    low(2, 0)
                pool.wait_ge(m.hh, v + 1)
                nc.gpsimd.tensor_tensor(hidl[:, v % 2], hid[:, v % 2], f32(hidh[:, v % 2]), ALU.subtract).then_inc(m.hl, 1)
            low(3, 1)
            with pool.Fori(2, nb // 2) as i:
                for par in range(2):
                    low(2 * i + par, par)
            if nb % 2:
                low(nb - 1, 0)

        def moe_sync(sp, L, m, nb, w_in):
            wv = w_in.rearrange("e p c -> p e c")

            def load(e, par):
                if late(e, 2):
                    sp.wait_ge(m.wlo, e - 1)
                src = wv[:, e, :] if isinstance(e, int) else wv[:, bass.ds(e, 1), :]
                sp.dma_start(wraw[:, par], src).then_inc(m.wload[par], 16)

            load(0, 0)
            load(1, 1)
            with sp.Fori(1, nb // 2) as i:
                load(2 * i, 0)
                load(2 * i + 1, 1)
            if nb % 2:
                load(nb - 1, 0)

        class Chain:

            def __init__(self, eng, s):
                self.eng, self.s, self.n = eng, s, 0

            def __call__(self, op):
                op.then_inc(self.s, 1)
                self.n += 1
                self.eng.wait_ge(self.s, self.n)

        def mark_largest(link, n):
            def sort():
                for t in range(TILES):
                    op = nc.vector.max(top8[:, t, :], gs[:, t, :])
                link(op)
                link(nc.vector.memset(top8[:, :, n:8], BIG))

            def mark():
                for t in range(TILES):
                    op = nc.vector.match_replace(out=rep8[:, t, :], in_to_replace=top8[:, t, :], in_values=gs[:, t, :],
                                                 imm_value=-BIG)
                link(op)
                link(nc.vector.tensor_tensor(cmp[:, :, :], rep8[:, :, :], gs[:, :, :], ALU.not_equal))

            return sort, mark

        def take_logits(dve, m, ne):
            dve.wait_ge(m.lg, BATCH)
            nc.vector.tensor_copy(lg[:, :, 0:ne],
                                  bank[5][:, 0:TILES * ne].rearrange("p (t e) -> p t e", t=TILES)).then_inc(m.lgl, 1)
            dve.wait_ge(m.lgl, 1)

        def over_experts(v, n):
            return v.unsqueeze(2).broadcast_to([P, TILES, n])

        def route0_vector(dve, m):
            link = Chain(dve, m.rs)
            sg = sc[:, :, :].rearrange("p t (g k) -> p t g k", g=GROUPS0)

            def first():
                take_logits(dve, m, E0)
                link(nc.vector.memset(cw[:, :, 0:SH0], 1.0))
                link(nc.vector.tensor_scalar(cw[:, :, 0:SH0], cw[:, :, 0:SH0], tg[:, 2:3], None, ALU.mult))

            def groups():
                dve.wait_ge(m.ra, 1)
                link(nc.vector.tensor_reduce(gs[:, :, :], sg, AX_X, ALU.add))

            def candidates():
                link(nc.vector.tensor_tensor(msc[:, :, :].rearrange("p t (g k) -> p t g k", g=GROUPS0), sg,
                                             cmp[:, :, :].unsqueeze(3).broadcast_to([P, TILES, GROUPS0, E0 // GROUPS0]),
                                             ALU.mult))
                for t in range(TILES):
                    op = nc.vector.max(top8[:, t, :], msc[:, t, :])
                link(op)

            def chosen():
                for t in range(TILES):
                    op = nc.vector.match_replace(out=rep[:, t, :], in_to_replace=top8[:, t, :], in_values=msc[:, t, :],
                                                 imm_value=-1.0)
                link(op)
                link(nc.vector.tensor_tensor(selw[:, :, :], rep[:, :, :], msc[:, :, :], ALU.not_equal))

            def weights():
                link(nc.vector.tensor_tensor(selw[:, :, :], selw[:, :, :], msc[:, :, :], ALU.mult))
                link(nc.vector.tensor_reduce(rsum[:, :], selw[:, :, :], AX_X, ALU.add))
                link(nc.vector.tensor_scalar(rsum[:, :], rsum[:, :], 1e-12, None, ALU.max))
                link(nc.vector.reciprocal(rrec[:, :], rsum[:, :]))
                link(nc.vector.tensor_scalar(rrec[:, :], rrec[:, :], tg[:, 2:3], None, ALU.mult))
                link(nc.vector.tensor_tensor(cw[:, :, SH0:NB0], selw[:, :, :], over_experts(rrec[:, :], E0), ALU.mult))

            return first, (groups, *mark_largest(link, TOPG0), candidates, chosen, weights)

        def route0_scalar(act, m):
            act.wait_ge(m.lgl, 1)
            nc.scalar.activation(sc[:, :, :], lg[:, :, :], ACT.Sigmoid).then_inc(m.ra, 1)

        def route1_vector(dve, m):
            link = Chain(dve, m.rs)

            def first():
                take_logits(dve, m, E1)
                link(nc.vector.tensor_reduce(rmx[:, :], lg[:, :, 0:E1], AX_X, ALU.max))
                link(nc.vector.tensor_tensor(msc[:, :, 0:E1], lg[:, :, 0:E1], over_experts(rmx[:, :], E1), ALU.subtract))
                link(nc.vector.memset(cw[:, :, 0:SH1], 1.0))
                link(nc.vector.tensor_scalar(cw[:, :, 0:SH1], cw[:, :, 0:SH1], tg[:, 3:4], None, ALU.mult))

            def softmax():
                dve.wait_ge(m.ra, 1)
                link(nc.vector.tensor_reduce(rsum[:, :], rep[:, :, 0:E1], AX_X, ALU.add))
                link(nc.vector.reciprocal(rrec[:, :], rsum[:, :]))
                link(nc.vector.tensor_tensor(sc[:, :, 0:E1], rep[:, :, 0:E1], over_experts(rrec[:, :], E1), ALU.mult))
                link(nc.vector.tensor_tensor(gs[:, :, :], sc[:, :, 0:E1],
                                             rbias[:, :].unsqueeze(1).broadcast_to([P, TILES, E1]), ALU.add))

            def weights():
                link(nc.vector.tensor_tensor(selw[:, :, 0:E1], cmp[:, :, :], sc[:, :, 0:E1], ALU.mult))
                link(nc.vector.tensor_scalar(selw[:, :, 0:E1], selw[:, :, 0:E1], tg[:, 3:4], None, ALU.mult))

            def spread():
                link(nc.vector.tensor_copy(cw[:, :, SH1:NB1].rearrange("p t (e k) -> p t e k", k=2),
                                           selw[:, :, 0:E1].unsqueeze(3).broadcast_to([P, TILES, E1, 2])))

            return first, (softmax, *mark_largest(link, TOP1), weights, spread)

        def route1_scalar(act, m):
            act.wait_ge(m.rs, 2)
            nc.scalar.activation(rep[:, :, 0:E1], msc[:, :, 0:E1], ACT.Exp).then_inc(m.ra, 1)

        A = s_a1

        def sync_a1(sp):
            sp.wait_ge(moe[0].up, 4 * NB0)
            for b in range(BATCH):
                if b:
                    sp.wait_ge(A["clo"], b)
                sp.dma_start(craw[:, :, :], ctxt_in[:, :, b * SEQ:(b + 1) * SEQ]).then_inc(A["ctx_t"], 16)
                if b:
                    sp.wait_ge(A["tlo"], b)
                sp.dma_start(traw[:, :, :], ctx_in[:, b * TPB:(b + 1) * TPB, :]).then_inc(A["ctx"], 16)
                if b == 0:
                    sp.dma_start(rraw[:, :, 0:E1], rw1_in).then_inc(moe[1].rload, 16)
                    sp.dma_start(rbias[:, :], rbias1_in.broadcast_to([P, E1])).then_inc(moe[1].rload, 16)

        def parameters_a1(sp):
            sp.dma_start(wsim[:, :, :], wsim_in).then_inc(A["par"], 16)
            sp.dma_start(w1row[:, :], w1row_in.broadcast_to([P, DIM])).then_inc(A["par"], 16)
            sp.dma_start(bsim[:, :], bsim_in.broadcast_to([P, 1])).then_inc(A["par"], 16)
            sp.dma_start(bqv[:, :], bqv_in.broadcast_to([P, DIM])).then_inc(A["par"], 16)
            sp.dma_start(wqv[:, :, :], wqv_in).then_inc(A["wq"], 16)

        def tensor_a1(pe):
            def transposes(b):
                pe.wait_ge(A["xn"], b + 1)
                if b >= 1:
                    pe.wait_ge(A["a"], 2 * b)
                if b >= 2:
                    pe.wait_ge(A["hbc"], b - 1)
                for c in range(CH):
                    for j in range(TPB):
                        mm = pe.transpose(bank[2 + c][:, j * P:(j + 1) * P], xn[:, TPB * b + j, c * P:(c + 1) * P],
                                          ident)
                    mm.then_inc(A["tr"], 1)

            def scores(b, tiles):
                pe.wait_ge(A["alo"], b + 1)
                pe.wait_ge(A["clo"], b + 1)
                for j in tiles:
                    if 4 * b + j >= 2:
                        pe.wait_ge(A["p"], 4 * b + j - 1)
                    k = 0
                    for c in range(CH):
                        for ap_, cp in ((aench, ctxh), (aench, ctxl), (aencl, ctxh)):
                            mm = pe.matmul(bank[j % 2][:, :], ap_[:, c, j * P:(j + 1) * P], cp[:, c, :],
                                           start=(k == 0), stop=(k == 5))
                            k += 1
                    mm.then_inc(A["sim"], 1)

            def probs_transposed(b, chunks):
                pe.wait_ge(A["pn"], 4 * b + 4)
                for jc in chunks:
                    if jc >= 2:
                        pe.wait_ge(A["ptl"], 4 * b + jc - 1)
                    elif b:
                        pe.wait_ge(A["x"], 4 * b)
                    for j in range(TPB):
                        mm = pe.transpose(bank[4 + jc % 2][:, j * P:(j + 1) * P], prob1[:, b % 2, j, jc * P:(jc + 1) * P],
                                          ident)
                    mm.then_inc(A["pt"], 1)

            def context_bar(b):
                pe.wait_ge(A["batt"], b + 1)
                if b + 1 < BATCH:
                    pe.wait_ge(A["a"], 2 * b + 4)
                for c in range(CH):
                    for j in range(TPB):
                        mm = pe.matmul(bank[2][:, c:c + 1], xn[:, TPB * b + j, c * P:(c + 1) * P], batt[:, j:j + 1],
                                       start=(j == 0), stop=(j == TPB - 1))
                mm.then_inc(A["hb"], 1)

            def attended(b):
                pe.wait_ge(A["tlo"], b + 1)
                if b:
                    pe.wait_ge(A["prod"], 2 * b)
                for c in range(CH):
                    k = 0
                    for jc in range(TPB):
                        if c == 0:
                            pe.wait_ge(A["ptl"], 4 * b + jc + 1)
                        for tp, pp in ((tokh, p1th), (tokh, p1tl), (tokl, p1th)):
                            mm = pe.matmul(bank[6 + c][:, :], tp[:, jc, c * P:(c + 1) * P], pp[:, jc, :],
                                           start=(k == 0), stop=(k == 11))
                            k += 1
                    mm.then_inc(A["hq"], 1)

            def output(b):
                pe.wait_ge(A["elo"], b + 1)
                pe.wait_ge(A["wlo"], b + 1)
                for j0 in (0, 2):
                    for g, (fh, fl) in enumerate(((ench[:, b % 3], encl[:, b % 3]), (hqh, hql), (prodh, prodl))):
                        if g and j0 == 0:
                            pe.wait_ge(A["hql" if g == 1 else "prl"], 2 * b + 2)
                        for j in (j0, j0 + 1):
                            k = 0
                            for c in range(CH):
                                for fp, wp in ((fh, wqh), (fh, wql), (fl, wqh)):
                                    mm = pe.matmul(bank[4 + j % 2][:, (j // 2) * DIM:(j // 2 + 1) * DIM], fp[:, c, j * P:(j + 1) * P],
                                                   wp[:, CH * g + c, :], start=(g == 0 and k == 0),
                                                   stop=(g == 2 and k == 5))
                                    k += 1
                            if g == 2:
                                mm.then_inc(A["o"], 1)

            transposes(0)
            transposes(1)
            scores(0, range(TPB))
            for b in range(BATCH):
                probs_transposed(b, (0, 1))
                if b + 1 < BATCH:
                    scores(b + 1, (0, 1))
                context_bar(b)
                probs_transposed(b, (2, 3))
                if b + 1 < BATCH:
                    scores(b + 1, (2, 3))
                if b + 2 < BATCH:
                    transposes(b + 2)
                attended(b)
                if b == BATCH - 1:
                    x_transposes(pe, moe[1], 0)
                    x_transposes(pe, moe[1], 1)
                output(b)

        def scalar_a1(act):
            def encoder(b):
                if b >= 3:
                    act.wait_ge(A["o"], 4 * (b - 2))
                    act.wait_ge(A["prod"], 2 * (b - 2))
                for c in range(CH):
                    act.wait_ge(A["tr"], 2 * b + c + 1)
                    nc.scalar.activation(ench[:, b % 3, c, :], bank[2 + c][:, :], ACT.Copy)
                    nc.scalar.activation(enc[:, b % 3, c, :], bank[2 + c][:, :], ACT.Copy).then_inc(A["enc"], 1)

            def scaled_high(b):
                if b:
                    act.wait_ge(A["sim"], 4 * b)
                for c in range(CH):
                    act.wait_ge(A["a"], 2 * b + c + 1)
                    nc.scalar.activation(aench[:, c, :], aenc[:, c, :], ACT.Copy).then_inc(A["ahi"], 1)

            def context(b):
                act.wait_ge(A["ctx_t"], 16 * b + 16)
                if b:
                    act.wait_ge(A["sim"], 4 * b)
                nc.scalar.activation(ctxh[:, :, :], craw[:, :, :], ACT.Copy).then_inc(A["chi"], 1)

            def tokens(b):
                act.wait_ge(A["ctx"], 16 * b + 16)
                if b:
                    act.wait_ge(A["hq"], 2 * b)
                nc.scalar.activation(tokh[:, :, :], traw[:, :, :], ACT.Copy).then_inc(A["thi"], 1)

            def softmax(b, tiles):
                if b >= 2 and 0 in tiles:
                    act.wait_ge(A["pt"], 4 * (b - 1))
                for j in tiles:
                    act.wait_ge(A["nm"], 4 * b + j + 1)
                    nc.scalar.activation(prob1[:, b % 2, j, :], bank[j % 2][:, :], ACT.Exp, bias=nm1[:, j:j + 1],
                                         accum_out=den1[:, j:j + 1]).then_inc(A["p"], 1)

            def row_exp(b):
                act.wait_ge(A["ngmx"], b + 1)
                nc.scalar.activation(eb[:, :], msim[:, :], ACT.Exp, bias=ngmx1[:, :],
                                     accum_out=ebs[:, :]).then_inc(A["eb"], 1)

            def probs_high(b, chunks):
                if b and 0 in chunks:
                    act.wait_ge(A["hq"], 2 * b)
                for jc in chunks:
                    act.wait_ge(A["pt"], 4 * b + jc + 1)
                    nc.scalar.activation(p1th[:, jc, :], bank[4 + jc % 2][:, :], ACT.Copy).then_inc(A["pth"], 1)

            def weights_high(b):
                act.wait_ge(A["w14"], b + 1)
                if b:
                    act.wait_ge(A["o"], 4 * b)
                nc.scalar.activation(wqh[:, 0:CH, :], w14[:, :, :], ACT.Copy).then_inc(A["whi"], 1)

            def attended_high(b):
                for c in range(CH):
                    act.wait_ge(A["hq"], 2 * b + c + 1)
                    nc.scalar.activation(hqh[:, c, :], bank[6 + c][:, :], ACT.Copy).then_inc(A["hqh"], 1)

            def product_high(b):
                for c in range(CH):
                    act.wait_ge(A["prod"], 2 * b + c + 1)
                    nc.scalar.activation(prodh[:, c, :], prod[:, c, :], ACT.Copy).then_inc(A["prh"], 1)

            context(0)
            encoder(0)
            scaled_high(0)
            tokens(0)
            act.wait_ge(A["wq"], 16)
            nc.scalar.activation(wqh[:, CH:3 * CH, :], wqv[:, CH:3 * CH, :], ACT.Copy).then_inc(A["wqs"], 1)
            encoder(1)
            softmax(0, range(TPB))
            scaled_high(1)
            context(1)
            row_exp(0)
            for b in range(BATCH):
                probs_high(b, (0, 1))
                if b + 1 < BATCH:
                    softmax(b + 1, (0, 1))
                weights_high(b)
                probs_high(b, (2, 3))
                if b + 1 < BATCH:
                    softmax(b + 1, (2, 3))
                if b + 2 < BATCH:
                    context(b + 2)
                attended_high(b)
                if b + 1 < BATCH:
                    row_exp(b + 1)
                product_high(b)
                if b == BATCH - 1:
                    x_high(act, moe[1], 0)
                    x_high(act, moe[1], 1)
                if b + 1 < BATCH:
                    tokens(b + 1)
                if b + 2 < BATCH:
                    encoder(b + 2)
                    scaled_high(b + 2)

        def vector_a1(dve):
            def row_terms(b):
                if b:
                    dve.wait_ge(A["msim"], b)
                for j in range(TPB):
                    if 4 * b + j:
                        dve.wait_ge(A["r"], 4 * b + j)
                    nc.vector.tensor_tensor_reduce(out=junk[:, :], in0=xn[:, TPB * b + j, :], in1=w1row[:, :], scale=1.0,
                                                   scalar=bsim[:, 0:1], op0=ALU.mult, op1=ALU.add,
                                                   accum_out=rterm[:, j:j + 1]).then_inc(A["r"], 1)

            def encoder(b):
                if b:
                    dve.wait_ge(A["alo"], b)
                for c in range(CH):
                    dve.wait_ge(A["enc"], 2 * b + c + 1)
                    nc.vector.tensor_scalar(aenc[:, c, :], bank[2 + c][:, :], wsim[:, 1, c:c + 1], wsim[:, 0, c:c + 1],
                                            ALU.mult, ALU.add).then_inc(A["a"], 1)

            def scaled_low(b):
                dve.wait_ge(A["ahi"], 2 * b + 2)
                nc.vector.tensor_tensor(aencl[:, :, :], aenc[:, :, :], f32(aench[:, :, :]),
                                        ALU.subtract).then_inc(A["alo"], 1)

            def maxima(b, tiles):
                for j in tiles:
                    dve.wait_ge(A["sim"], 4 * b + j + 1)
                    nc.vector.tensor_reduce(nm1[:, j:j + 1], bank[j % 2][:, :], AX_X, ALU.max,
                                            negate=True).then_inc(A["nm"], 1)

            def row_maxima(b):
                dve.wait_ge(A["nm"], 4 * b + 4)
                dve.wait_ge(A["r"], 4 * b + 4)
                if b:
                    dve.wait_ge(A["eb"], b)
                nc.vector.tensor_tensor(msim[:, :], rterm[:, :], nm1[:, :], ALU.subtract).then_inc(A["msim"], 1)
                dve.wait_ge(A["msim"], b + 1)
                nc.vector.tensor_reduce(mx1[:, :], msim[:, :], AX_X, ALU.max).then_inc(A["mx"], 1)

            def normalised(b):
                for j in range(TPB):
                    dve.wait_ge(A["p"], 4 * b + j + 1)
                    nc.vector.reciprocal(rd1[:, j:j + 1], den1[:, j:j + 1]).then_inc(A["rd"], 1)
                    dve.wait_ge(A["rd"], 4 * b + j + 1)
                    nc.vector.tensor_scalar(prob1[:, b % 2, j, :], prob1[:, b % 2, j, :], rd1[:, j:j + 1], None,
                                            ALU.mult).then_inc(A["pn"], 1)
                dve.wait_ge(A["gmx"], b + 1)
                nc.vector.tensor_scalar(ngmx1[:, :], gmx1[:, :], -1.0, None, ALU.mult).then_inc(A["ngmx"], 1)

            def row_softmax(b):
                dve.wait_ge(A["ebt"], b + 1)
                nc.vector.reciprocal(ebr[:, :], ebt[:, :]).then_inc(A["ebr"], 1)
                dve.wait_ge(A["ebr"], b + 1)
                nc.vector.tensor_scalar(batt[:, :], eb[:, :], ebr[:, 0:1], None, ALU.mult).then_inc(A["batt"], 1)

            def probs_low(b, chunks):
                for jc in chunks:
                    dve.wait_ge(A["pth"], 4 * b + jc + 1)
                    nc.vector.tensor_tensor(p1tl[:, jc, :], bank[4 + jc % 2][:, :], f32(p1th[:, jc, :]),
                                            ALU.subtract).then_inc(A["ptl"], 1)

            def weights_by_bar(b):
                dve.wait_ge(A["hb"], b + 1)
                nc.vector.tensor_copy(hbar[:, :], bank[2][:, 0:CH]).then_inc(A["hbc"], 1)
                dve.wait_ge(A["hbc"], b + 1)
                for c in range(CH):
                    op = nc.vector.scalar_tensor_tensor(out=w14[:, c, :], in0=wqv[:, 3 * CH + c, :], scalar=hbar[:, c:c + 1],
                                                        in1=wqv[:, c, :], op0=ALU.mult, op1=ALU.add)
                op.then_inc(A["w14"], 1)

            def weights_low(b):
                dve.wait_ge(A["whi"], b + 1)
                nc.vector.tensor_tensor(wql[:, 0:CH, :], w14[:, :, :], f32(wqh[:, 0:CH, :]),
                                        ALU.subtract).then_inc(A["wlo"], 1)

            def features(b):
                for c in range(CH):
                    dve.wait_ge(A["hqh"], 2 * b + c + 1)
                    nc.vector.tensor_tensor(prod[:, c, :], enc[:, b % 3, c, :], bank[6 + c][:, :],
                                            ALU.mult).then_inc(A["prod"], 1)
                    nc.vector.tensor_tensor(hql[:, c, :], bank[6 + c][:, :], f32(hqh[:, c, :]),
                                            ALU.subtract).then_inc(A["hql"], 1)
                for c in range(CH):
                    dve.wait_ge(A["prh"], 2 * b + c + 1)
                    nc.vector.tensor_tensor(prodl[:, c, :], prod[:, c, :], f32(prodh[:, c, :]),
                                            ALU.subtract).then_inc(A["prl"], 1)

            def residual(b):
                dve.wait_ge(A["xb"], TPB * (b + 1))
                for j in (0, 2, 1, 3):
                    t = TPB * b + j
                    if j < 2:
                        dve.wait_ge(A["o"], t + 3)
                    nc.vector.scalar_tensor_tensor(out=x[:, t, :], in0=bank[4 + j % 2][:, (j // 2) * DIM:(j // 2 + 1) * DIM], scalar=tg[:, 1:2],
                                                   in1=x[:, t, :], op0=ALU.mult, op1=ALU.add).then_inc(A["x"], 1)

            dve.wait_ge(A["par"], 64)
            nc.vector.tensor_scalar(bqvg[:, :], bqv[:, :], tg[:, 1:2], None, ALU.mult).then_inc(A["bq"], 1)
            encoder(0)
            scaled_low(0)
            dve.wait_ge(A["xn"], 1)
            row_terms(0)
            encoder(1)
            maxima(0, range(TPB))
            row_maxima(0)
            normalised(0)
            scaled_low(1)
            dve.wait_ge(A["wqs"], 1)
            nc.vector.tensor_tensor(wql[:, CH:3 * CH, :], wqv[:, CH:3 * CH, :], f32(wqh[:, CH:3 * CH, :]),
                                    ALU.subtract)
            row_softmax(0)
            ln_norm(dve, 2, 2, A["xn"])
            row_terms(1)
            for b in range(BATCH):
                probs_low(b, (0, 1))
                if b + 1 < BATCH:
                    maxima(b + 1, (0, 1))
                weights_by_bar(b)
                probs_low(b, (2, 3))
                weights_low(b)
                if b == BATCH - 1:
                    ln_stats(dve, 3, 2)
                if b + 1 < BATCH:
                    maxima(b + 1, (2, 3))
                    row_maxima(b + 1)
                    normalised(b + 1)
                if b + 3 < BATCH:
                    ln_stats(dve, 2, b + 3)
                features(b)
                if b + 1 < BATCH:
                    row_softmax(b + 1)
                if b + 3 < BATCH:
                    ln_norm(dve, 2, b + 3, A["xn"])
                if b + 2 < BATCH:
                    encoder(b + 2)
                    scaled_low(b + 2)
                if b == BATCH - 1:
                    dve.wait_ge(A["elo"], BATCH)
                    x_low(dve, moe[1], 0)
                    ln_norm(dve, 3, 2, moe[1].xn)
                    x_low(dve, moe[1], 1)
                if b == BATCH - 2:
                    ln_stats(dve, 3, 0)
                    ln_stats(dve, 3, 1)
                    ln_norm(dve, 3, 0, moe[1].xn)
                    ln_norm(dve, 3, 1, moe[1].xn)
                residual(b)
                if b + 2 < BATCH:
                    dve.wait_ge(A["xn"], b + 3)
                    row_terms(b + 2)

        def pool_a1(pool):
            def context_low(b):
                pool.wait_ge(A["chi"], b + 1)
                nc.gpsimd.tensor_tensor(ctxl[:, :, :], craw[:, :, :], f32(ctxh[:, :, :]), ALU.subtract).then_inc(A["clo"], 1)

            def encoder_low(b):
                pool.wait_ge(A["enc"], 2 * b + 2)
                nc.gpsimd.tensor_tensor(encl[:, b % 3], enc[:, b % 3], f32(ench[:, b % 3]),
                                        ALU.subtract).then_inc(A["elo"], 1)

            def token_low(b):
                pool.wait_ge(A["thi"], b + 1)
                nc.gpsimd.tensor_tensor(tokl[:, :, :], traw[:, :, :], f32(tokh[:, :, :]), ALU.subtract).then_inc(A["tlo"], 1)

            def add_bias(b):
                pool.wait_ge(A["xn"], b + 1)
                for t in range(TPB * b, TPB * b + TPB):
                    nc.gpsimd.tensor_tensor(x[:, t, :], x[:, t, :], bqvg[:, :], ALU.add).then_inc(A["xb"], 1)

            def row_max(b):
                pool.wait_ge(A["mx"], b + 1)
                nc.gpsimd.partition_all_reduce(gmx1[:, :], mx1[:, :], P, RMAX).then_inc(A["gmx"], 1)

            def row_sum(b):
                pool.wait_ge(A["eb"], b + 1)
                nc.gpsimd.partition_all_reduce(ebt[:, :], ebs[:, :], P, RADD).then_inc(A["ebt"], 1)

            ln_rsqrt(pool, 2, 0)
            ln_rsqrt(pool, 2, 1)
            ln_rsqrt(pool, 2, 2)
            context_low(0)
            encoder_low(0)
            pool.wait_ge(A["bq"], 1)
            add_bias(0)
            row_max(0)
            token_low(0)
            row_sum(0)
            context_low(1)
            encoder_low(1)
            add_bias(1)
            for b in range(BATCH):
                if b + 1 < BATCH:
                    row_max(b + 1)
                if b + 3 < BATCH:
                    ln_rsqrt(pool, 2, b + 3)
                if b + 2 < BATCH:
                    context_low(b + 2)
                if b + 1 < BATCH:
                    row_sum(b + 1)
                if b + 2 < BATCH:
                    add_bias(b + 2)
                if b + 1 < BATCH:
                    token_low(b + 1)
                if b + 2 < BATCH:
                    encoder_low(b + 2)
                else:
                    ln_rsqrt(pool, 3, 2 * b - BATCH)
                    if b < BATCH - 1:
                        ln_rsqrt(pool, 3, 2 * b - BATCH + 1)

        @block.sync
        def _(sp):
            def load_keys(s):
                if s >= 1:
                    sp.wait_ge(s_klo, s)
                a, b = KPIECES[s]
                sp.dma_start(kraw[:, :, 0:b - a], kt_in[:, :, a:b]).then_inc(s_kraw, 16)

            def load_values(g):
                if g >= 2:
                    sp.wait_ge(s_vd, 2 * g - 2)
                a, b = VGROUPS[g]
                sp.dma_start(vraw[:, g % 2, 0:b - a, :], v_in[:, a:b, :]).then_inc(s_vraw[g % 2], 16)

            def load_x(b):
                sp.dma_start(x[:, b * TPB:(b + 1) * TPB, :], x_in[:, b * TPB:(b + 1) * TPB, :]).then_inc(s_x[b], 16)

            def stack_keys(s):
                sp.wait_ge(s_klo, s + 1)
                a, b = KPIECES[s]
                parts = khl1 if s else khl0
                for g in range(4):
                    for r, part in enumerate((0, 1, 1, 0)):
                        sp.dma_start(kst[32 * r:32 * r + 32, 2 * g:2 * g + 2, a:b].bitcast(F32),
                                     parts[32 * g:32 * g + 32, part].bitcast(F32)).then_inc(s_kst[s] if s else s_kst0[g], 16)

            load_x(0)
            load_keys(0)
            sp.dma_start(consts[:, 0:P + 2], consts_in[:, 0:P + 2]).then_inc(s_const, 16)
            sp.dma_start(band_f32, consts_in[:, P + 2:]).then_inc(s_bandf, 16)
            load_values(0)
            sp.dma_start(gates[:, :], gates_in.broadcast_to([P, 4])).then_inc(s_gates, 16)
            load_keys(1)
            stack_keys(0)
            load_values(1)
            load_x(1)
            load_values(2)
            load_keys(2)
            stack_keys(1)
            load_x(2)
            load_x(3)
            load_values(3)
            stack_keys(2)
            for L, (nb, w_in) in enumerate(((NB0, w0_in), (NB1, w1_in))):
                m = moe[L]
                if L == 0:
                    sp.wait_ge(s_xa, 2 * TILES)
                    sp.wait_ge(s_pv, UNITS)
                    sp.dma_start(rraw[:, :, :], rw0_in).then_inc(m.rload, 16)
                else:
                    sp.wait_ge(A["o"], TILES)
                moe_sync(sp, L, m, nb, w_in)
                if L == 0:
                    parameters_a1(sp)
                    sync_a1(sp)
            for b in range(BATCH):
                sp.wait_ge(moe[1].acc, 4 * (NB1 - 1) + b + 1)
                sp.dma_start(out[:, b * TPB:(b + 1) * TPB, :], x[:, b * TPB:(b + 1) * TPB, :]).then_inc(s_out, 16)
            sp.wait_ge(s_out, 16 * BATCH)

        @block.tensor
        def _(pe):
            attention_tensor(pe)
            moe_tensor(pe, 0, moe[0], NB0)
            tensor_a1(pe)
            moe_tensor(pe, 1, moe[1], NB1)

        @block.scalar
        def _(act):
            attention_scalar(act)
            moe_scalar(act, 0, moe[0], NB0, route0_scalar)
            scalar_a1(act)
            moe_scalar(act, 1, moe[1], NB1, route1_scalar)

        @block.vector
        def _(dve):
            attention_vector(dve)
            moe_vector(dve, 0, moe[0], NB0, *route0_vector(dve, moe[0]))
            dve.wait_ge(moe[0].acc, 4 * NB0)
            vector_a1(dve)
            dve.wait_ge(A["x"], TILES)
            moe_vector(dve, 1, moe[1], NB1, *route1_vector(dve, moe[1]))

        @block.gpsimd
        def _(pool):
            attention_pool(pool)
            for L, m, nb in ((0, moe[0], NB0), (1, moe[1], NB1)):
                if L == 1:
                    pool_a1(pool)
                moe_pool(pool, L, m, nb)


def _weights(gate, up, down):
    import numpy as np

    def cols(w):
        return w.T.reshape(CH, P, FF).transpose(1, 0, 2).reshape(P, CH * FF)
    return [np.concatenate([cols(gate[s:s + FF]), cols(up[s:s + FF]), down[:, s:s + FF].T], axis=1)
            for s in range(0, gate.shape[0], FF)]


def kernel(**inputs):
    import numpy as np
    import concourse.bacc as bacc
    from concourse import mybir as mb
    from concourse.bass_utils import run_bass_kernel_spmd as run

    a = {k: np.asarray(v) for k, v in inputs.items()}
    f = np.float32

    def by_tile(v):
        return v.reshape(-1, P, DIM).transpose(1, 0, 2)

    def by_chunk(w):
        return w.reshape(-1, P, w.shape[1]).transpose(1, 0, 2)

    tokens = a["ctx_1024"].reshape(TOKENS, DIM)
    padded = np.pad(tokens, ((BAND, BAND), (0, 0)))
    kt = padded.T.reshape(4, 2, 32, KCOLS).transpose(0, 2, 1, 3).reshape(P, 2, KCOLS)
    rows, keys = np.arange(P)[:, None], np.arange(WIN)[None, :]
    band = np.abs(keys - BAND - rows) <= BAND
    masks = [band & ~((j == 0) & (keys < BAND)) & ~((j == TPB - 1) & (keys >= P + BAND)) for j in range(TPB)]
    head = np.stack([(np.arange(P) % 32) < 16, (np.arange(P) % 32) >= 16], 1)
    consts = np.concatenate([np.eye(P), head] + [np.where(m, 0.0, MASKED) for m in masks], 1).astype(f)
    w0 = np.stack(sum([_weights(a["L0_ffn_expert_gate"][e], a["L0_ffn_expert_up"][e], a["L0_ffn_expert_down"][e])
                       for e in range(E0)],
                      _weights(a["L0_ffn_shared_gate_w"], a["L0_ffn_shared_up_w"], a["L0_ffn_shared_down_w"])))
    w1 = np.stack(sum([_weights(a["L1_ffn_w1"][e], a["L1_ffn_w3"][e], a["L1_ffn_w2"][e]) for e in range(E1)],
                      _weights(a["L1_ffn_sw1"], a["L1_ffn_sw3"], a["L1_ffn_sw2"])))
    wsim = a["L1_xattn_w_sim"].reshape(3, CH, P).transpose(2, 0, 1)[:, 1:3]
    arrays = {
        "x": by_tile(a["x"]), "kt": kt, "v": by_tile(padded), "ctx": by_tile(tokens), "ctxt": by_chunk(tokens.T),
        "consts": consts, "gates": np.concatenate([a["g_xattn"], a["g_ffn"]])[None],
        "rw0": by_chunk(a["L0_ffn_gate_w"].T), "w0": w0, "wsim": wsim, "w1row": a["L1_xattn_w_sim"][None, 0:DIM],
        "bsim": a["L1_xattn_b_sim"][None], "wqv": by_chunk(a["L1_xattn_W_qv"]), "bqv": a["L1_xattn_b_qv"][None],
        "rw1": by_chunk(a["L1_ffn_gate_w"].T), "rbias1": a["L1_ffn_gate_bias"][None], "w1": w1,
    }
    arrays = {f"in_{k}": np.ascontiguousarray(v) for k, v in arrays.items()}
    nc = bacc.Bacc("TRN2", target_bir_lowering=False, num_devices=1)
    args = [nc.dram_tensor(k, v.shape, mb.dt.from_np(v.dtype), kind="ExternalInput").ap() for k, v in arrays.items()]
    args.append(nc.dram_tensor("out", (P, TILES, DIM), mb.dt.float32, kind="ExternalOutput").ap())
    gated_xattn_moe_kernel(nc, *args)
    r = run(nc, [arrays], core_ids=[0])
    return np.asarray(r.results[0]["out"]).transpose(1, 0, 2).reshape(BATCH, SEQ, DIM)
```
